# Optimizing a Trainium2 kernel written in Bass

```python
import numpy as np
import jax
import jax.numpy as jnp

def _softmax(x, axis=-1):
    return jax.nn.softmax(x, axis=axis)

def _gelu(x):
    return jax.nn.gelu(x, approximate=True)

def _silu(x):
    return jax.nn.silu(x)

def _sigmoid(x):
    return jax.nn.sigmoid(x)

def _layernorm(x, axis=-1, eps=1e-05):
    m = jnp.mean(x, axis=axis, keepdims=True)
    v = jnp.var(x, axis=axis, keepdims=True)
    return (x - m) / jnp.sqrt(v + eps)

def _scatter_add(tgt, idx, src, axis=0):
    return tgt.at[idx].add(src)

def _segment_sum(src, seg, n):
    return jax.ops.segment_sum(src, seg, n)
kernel_name = 'mk_perceiver_d2_seqx_r2_13f1aa'

def setup_inputs(seed: int=0):
    np.random.seed(seed)
    _w = jnp.asarray

    def _rec_inputs():
        import jax
        import jax.numpy as jnp
        _rk = jax.random.key(seed)
        x = 7.22e-05 + 1 * jax.random.normal(jax.random.fold_in(_rk, 1), (16, 64, 512), jnp.float32)
        _lenS = 64 - jax.random.randint(jax.random.fold_in(_rk, 7), (16,), 0, max(1, 64 // 4) + 1, jnp.int32)
        _lenS2 = 1601 - jax.random.randint(jax.random.fold_in(_rk, 8), (16,), 0, max(1, 1601 // 4) + 1, jnp.int32)
        _ctx_1024P = jax.random.normal(jax.random.fold_in(_rk, 11), (16, 16, 512), jnp.float32)
        _ctx_1024c = jax.random.dirichlet(jax.random.fold_in(_rk, 511), 0.3 * jnp.ones((16,), jnp.float32), (16, 1601))
        _ctx_1024t = jnp.einsum('bsk,bkd->bsd', _ctx_1024c, _ctx_1024P)
        _ctx_1024t = _ctx_1024t * jax.lax.rsqrt(jnp.mean(jnp.square(_ctx_1024t)) + 1e-12) * 0.953939
        ctx_1024 = -0.000514642 + 1.00011 * (_ctx_1024t + 0.3 * jax.random.normal(jax.random.fold_in(_rk, 611), (16, 1601, 512), jnp.float32))
        _validS = jnp.arange(64)[None, :] < _lenS[:, None]
        _validS2 = jnp.arange(1601)[None, :] < _lenS2[:, None]
        _causal = jnp.tril(jnp.ones((64, 64), dtype=bool))
        mask_Bx1xSxS2_bk1 = jnp.broadcast_to(_validS2[:, None, None, :], (16, 1, 64, 1601))
        return (x, ctx_1024, mask_Bx1xSxS2_bk1)
    x, ctx_1024, mask_Bx1xSxS2_bk1 = _rec_inputs()

    def _L0_xattn_setup():
        import jax, jax.numpy as jnp
        import numpy as np
        B, L_ENC, L_DEC, D = (16, 256, 128, 512)
        key = jax.random.key(seed)
        k1, k2, k3, k4, k5, k6 = jax.random.split(key, 6)
        encoder_hc = jax.random.normal(k1, (B, L_ENC, D), dtype=jnp.float32)
        decoder_hq = jax.random.normal(k2, (B, L_DEC, D), dtype=jnp.float32)
        w_sim = jax.random.normal(k3, (3 * D,), dtype=jnp.float32) * 0.02
        b_sim = jax.random.normal(k4, (1,), dtype=jnp.float32) * 0.02
        W_qv = jax.random.normal(k5, (4 * D, D), dtype=jnp.float32) * 0.02
        b_qv = jax.random.normal(k6, (D,), dtype=jnp.float32) * 0.02
        return {'encoder_hc': encoder_hc, 'decoder_hq': decoder_hq, 'w_sim': w_sim, 'b_sim': b_sim, 'W_qv': W_qv, 'b_qv': b_qv}
    _L0_xattn_all = _L0_xattn_setup()
    _L0_xattn_in = {k: v for k, v in _L0_xattn_all.items() if k in ('w_sim', 'b_sim', 'W_qv', 'b_qv')}
    del _L0_xattn_all

    def _L0_attn_setup():
        import jax, jax.numpy as jnp
        import numpy as np
        HIDDEN, KEY_DIM, VALUE_DIM = (512, 512, 512)
        BATCH, SEQ = (8, 1024)
        key = jax.random.key(seed)
        ks = jax.random.split(key, 9)
        s = lambda fan_in: 1.0 / np.sqrt(fan_in)
        return {'y_all': jax.random.normal(ks[0], (BATCH, SEQ, HIDDEN), dtype=jnp.float32), 'Wq': jax.random.uniform(ks[1], (HIDDEN, KEY_DIM), jnp.float32, -s(HIDDEN), s(HIDDEN)), 'bq': jax.random.uniform(ks[2], (KEY_DIM,), jnp.float32, -s(HIDDEN), s(HIDDEN)), 'Wk': jax.random.uniform(ks[3], (HIDDEN, KEY_DIM), jnp.float32, -s(HIDDEN), s(HIDDEN)), 'bk': jax.random.uniform(ks[4], (KEY_DIM,), jnp.float32, -s(HIDDEN), s(HIDDEN)), 'Wv': jax.random.uniform(ks[5], (HIDDEN, VALUE_DIM), jnp.float32, -s(HIDDEN), s(HIDDEN)), 'bv': jax.random.uniform(ks[6], (VALUE_DIM,), jnp.float32, -s(HIDDEN), s(HIDDEN)), 'Wo': jax.random.uniform(ks[7], (VALUE_DIM, HIDDEN), jnp.float32, -s(VALUE_DIM), s(VALUE_DIM)), 'bo': jax.random.uniform(ks[8], (HIDDEN,), jnp.float32, -s(VALUE_DIM), s(VALUE_DIM))}
    _L0_attn_all = _L0_attn_setup()
    _L0_attn_in = {k: v for k, v in _L0_attn_all.items() if k in ('Wq', 'bq', 'Wk', 'bk', 'Wv', 'bv', 'Wo', 'bo')}
    del _L0_attn_all

    def _L0_ffn_setup():
        import jax, jax.numpy as jnp
        import numpy as np
        BEST_K = 2

        def _expert(xf, w1, w3, w2):
            return jax.nn.silu(xf @ w1) * (xf @ w3) @ w2
        key = jax.random.key(seed)
        ks = jax.random.split(key, 9)
        E, S_sh, D, H = (8, 2, 512, 256)
        B, S = (2, 1024)
        w = lambda k, shape: jax.random.normal(k, shape, dtype=jnp.float32) * 0.02
        return {'x': jax.random.normal(ks[0], (B, S, D), dtype=jnp.float32), 'router_w': w(ks[1], (D, E)), 'router_b': jnp.zeros((E,), dtype=jnp.float32), 'routed_w1': w(ks[2], (E, D, H)), 'routed_w3': w(ks[3], (E, D, H)), 'routed_w2': w(ks[4], (E, H, D)), 'shared_w1': w(ks[5], (S_sh, D, H)), 'shared_w3': w(ks[6], (S_sh, D, H)), 'shared_w2': w(ks[7], (S_sh, H, D))}
    _L0_ffn_all = _L0_ffn_setup()
    _L0_ffn_in = {k: v for k, v in _L0_ffn_all.items() if k in ('router_w', 'router_b', 'routed_w1', 'routed_w3', 'routed_w2', 'shared_w1', 'shared_w3', 'shared_w2')}
    del _L0_ffn_all

    def _L1_xattn_setup():
        import jax, jax.numpy as jnp
        import numpy as np
        B, S, D, H = (4, 1024, 512, 16)
        HD = D // H
        key = jax.random.key(seed)
        ks = jax.random.split(key, 12)
        scale = 1.0 / np.sqrt(D)
        inp = {'queries': jax.random.normal(ks[0], (B, S, D), jnp.float32), 'keys': jax.random.normal(ks[1], (B, S, D), jnp.float32), 'values': jax.random.normal(ks[2], (B, S, D), jnp.float32), 'mask': jax.random.randint(ks[3], (B, 1, S, S), 0, 2).astype(bool), 'Wq': jax.random.normal(ks[4], (D, D), jnp.float32) * scale, 'bq': jnp.zeros((D,), jnp.float32), 'Wk': jax.random.normal(ks[5], (D, D), jnp.float32) * scale, 'bk': jnp.zeros((D,), jnp.float32), 'Wv': jax.random.normal(ks[6], (D, D), jnp.float32) * scale, 'bv': jnp.zeros((D,), jnp.float32), 'Wo': jax.random.normal(ks[7], (D, D), jnp.float32) * scale, 'bo': jnp.zeros((D,), jnp.float32)}
        return inp
    _L1_xattn_all = _L1_xattn_setup()
    _L1_xattn_in = {k: v for k, v in _L1_xattn_all.items() if k in ('Wq', 'bq', 'Wk', 'bk', 'Wv', 'bv', 'Wo', 'bo')}
    del _L1_xattn_all

    def _L1_attn_setup():
        import jax, jax.numpy as jnp
        import numpy as np
        B, N, DM, H, FF = (8, 1024, 512, 16, 2048)
        D = DM // H // 2
        LAMBDA_INIT = 0.8 - 0.6 * float(np.exp(-0.3 * 1.0))

        def _layernorm(x, g, b, eps=1e-05):
            mu = jnp.mean(x, axis=-1, keepdims=True)
            var = jnp.mean(jnp.square(x - mu), axis=-1, keepdims=True)
            return (x - mu) * jax.lax.rsqrt(var + eps) * g + b

        def _rmsnorm(x, eps=1e-05):
            return x * jax.lax.rsqrt(jnp.mean(x * x, axis=-1, keepdims=True) + eps)

        def _diff_attn(x, Wq, Wk, Wv, lq1, lq2, lk1, lk2, Wo, bo):
            b, n, d = x.shape
            scale = D ** (-0.5)
            q = (x @ Wq.T).reshape(b, n, H, D, 2).transpose(0, 1, 4, 2, 3).reshape(b, n, 2 * H, D) * scale
            k = (x @ Wk.T).reshape(b, n, H, D, 2).transpose(0, 1, 4, 2, 3).reshape(b, n, 2 * H, D)
            v = (x @ Wv.T).reshape(b, n, H, 2 * D).transpose(0, 2, 1, 3)
            att = jnp.einsum('bnqd,bnkd->bnqk', q, k)
            att = jnp.nan_to_num(att)
            att = jax.nn.softmax(att.astype(jnp.float32), axis=-1)
            lam = jnp.exp(jnp.sum(lq1 * lk1)) - jnp.exp(jnp.sum(lq2 * lk2)) + LAMBDA_INIT
            att6 = att.reshape(b, n, 2, H, 2, H)
            att2 = att6[:, :, 0, :, 0, :] - lam * att6[:, :, 1, :, 1, :]
            out = jnp.einsum('bnah,bhnd->bnad', att2, v)
            out = _rmsnorm(out) * (1.0 - LAMBDA_INIT)
            out = out.reshape(b, n, d)
            return out @ Wo.T + bo
        key = jax.random.key(seed)
        ks = jax.random.split(key, 12)
        p = lambda k, sh, s=0.02: jax.random.normal(k, sh, jnp.float32) * s
        return {'x': jax.random.normal(ks[0], (B, N, DM), jnp.float32), 'Wq': p(ks[1], (DM, DM)), 'Wk': p(ks[2], (DM, DM)), 'Wv': p(ks[3], (DM, DM)), 'lq1': p(ks[4], (D,), 0.1), 'lq2': p(ks[5], (D,), 0.1), 'lk1': p(ks[6], (D,), 0.1), 'lk2': p(ks[7], (D,), 0.1), 'Wo': p(ks[8], (DM, DM)), 'bo': jnp.zeros((DM,), jnp.float32), 'ln1_g': jnp.ones((DM,), jnp.float32), 'ln1_b': jnp.zeros((DM,), jnp.float32), 'ln2_g': jnp.ones((DM,), jnp.float32), 'ln2_b': jnp.zeros((DM,), jnp.float32), 'W1': p(ks[9], (FF, DM)), 'b1': jnp.zeros((FF,), jnp.float32), 'W2': p(ks[10], (DM, FF)), 'b2': jnp.zeros((DM,), jnp.float32)}
    _L1_attn_all = _L1_attn_setup()
    _L1_attn_in = {k: v for k, v in _L1_attn_all.items() if k in ('Wq', 'Wk', 'Wv', 'lq1', 'lq2', 'lk1', 'lk2', 'Wo', 'bo', 'ln1_g', 'ln1_b', 'ln2_g', 'ln2_b', 'W1', 'b1', 'W2', 'b2')}
    del _L1_attn_all

    def _L1_ffn_setup():
        import jax, jax.numpy as jnp
        import numpy as np
        B, S, D_MODEL, D_HIDDEN = (4, 1024, 512, 2048)

        def act_quant(x):
            scale = 127.0 / jnp.clip(jnp.max(jnp.abs(x), axis=-1, keepdims=True), 1e-05)
            return jnp.clip(jnp.round(x * scale), -128, 127) / scale

        def weight_quant(w):
            scale = 1.0 / jnp.clip(jnp.mean(jnp.abs(w)), 1e-05)
            return jnp.clip(jnp.round(w * scale), -1, 1) / scale

        def bit_linear(x, w):
            xq = x + jax.lax.stop_gradient(act_quant(x) - x)
            wq = w + jax.lax.stop_gradient(weight_quant(w) - w)
            return jnp.einsum('bsd,hd->bsh', xq, wq)

        def depthwise_conv1d(x_bcl, w, b):
            y = jax.lax.conv_general_dilated(x_bcl, w, window_strides=(1,), padding=[(1, 1)], dimension_numbers=('NCH', 'OIH', 'NCH'), feature_group_count=x_bcl.shape[1])
            return y + b[None, :, None]
        key = jax.random.key(seed)
        ks = jax.random.split(key, 5)
        lim1 = 1.0 / np.sqrt(D_MODEL)
        lim2 = 1.0 / np.sqrt(D_HIDDEN)
        limc = 1.0 / np.sqrt(3.0)
        return {'x': jax.random.normal(ks[0], (B, S, D_MODEL), dtype=jnp.float32), 'w1': jax.random.uniform(ks[1], (D_HIDDEN, D_MODEL), jnp.float32, -lim1, lim1), 'conv_w': jax.random.uniform(ks[2], (D_HIDDEN, 1, 3), jnp.float32, -limc, limc), 'conv_b': jax.random.uniform(ks[3], (D_HIDDEN,), jnp.float32, -limc, limc), 'w2': jax.random.uniform(ks[4], (D_MODEL, D_HIDDEN), jnp.float32, -lim2, lim2)}
    _L1_ffn_all = _L1_ffn_setup()
    _L1_ffn_in = {k: v for k, v in _L1_ffn_all.items() if k in ('w1', 'conv_w', 'conv_b', 'w2')}
    del _L1_ffn_all
    return {'x': x, 'ctx_1024': ctx_1024, 'mask_Bx1xSxS2_bk1': mask_Bx1xSxS2_bk1, 'L0_xattn_w_sim': _L0_xattn_in['w_sim'], 'L0_xattn_b_sim': _L0_xattn_in['b_sim'], 'L0_xattn_W_qv': _L0_xattn_in['W_qv'], 'L0_xattn_b_qv': _L0_xattn_in['b_qv'], 'L0_attn_Wq': _L0_attn_in['Wq'], 'L0_attn_bq': _L0_attn_in['bq'], 'L0_attn_Wk': _L0_attn_in['Wk'], 'L0_attn_bk': _L0_attn_in['bk'], 'L0_attn_Wv': _L0_attn_in['Wv'], 'L0_attn_bv': _L0_attn_in['bv'], 'L0_attn_Wo': _L0_attn_in['Wo'], 'L0_attn_bo': _L0_attn_in['bo'], 'L0_ffn_router_w': _L0_ffn_in['router_w'], 'L0_ffn_router_b': _L0_ffn_in['router_b'], 'L0_ffn_routed_w1': _L0_ffn_in['routed_w1'], 'L0_ffn_routed_w3': _L0_ffn_in['routed_w3'], 'L0_ffn_routed_w2': _L0_ffn_in['routed_w2'], 'L0_ffn_shared_w1': _L0_ffn_in['shared_w1'], 'L0_ffn_shared_w3': _L0_ffn_in['shared_w3'], 'L0_ffn_shared_w2': _L0_ffn_in['shared_w2'], 'L1_xattn_Wq': _L1_xattn_in['Wq'], 'L1_xattn_bq': _L1_xattn_in['bq'], 'L1_xattn_Wk': _L1_xattn_in['Wk'], 'L1_xattn_bk': _L1_xattn_in['bk'], 'L1_xattn_Wv': _L1_xattn_in['Wv'], 'L1_xattn_bv': _L1_xattn_in['bv'], 'L1_xattn_Wo': _L1_xattn_in['Wo'], 'L1_xattn_bo': _L1_xattn_in['bo'], 'L1_attn_Wq': _L1_attn_in['Wq'], 'L1_attn_Wk': _L1_attn_in['Wk'], 'L1_attn_Wv': _L1_attn_in['Wv'], 'L1_attn_lq1': _L1_attn_in['lq1'], 'L1_attn_lq2': _L1_attn_in['lq2'], 'L1_attn_lk1': _L1_attn_in['lk1'], 'L1_attn_lk2': _L1_attn_in['lk2'], 'L1_attn_Wo': _L1_attn_in['Wo'], 'L1_attn_bo': _L1_attn_in['bo'], 'L1_attn_ln1_g': _L1_attn_in['ln1_g'], 'L1_attn_ln1_b': _L1_attn_in['ln1_b'], 'L1_attn_ln2_g': _L1_attn_in['ln2_g'], 'L1_attn_ln2_b': _L1_attn_in['ln2_b'], 'L1_attn_W1': _L1_attn_in['W1'], 'L1_attn_b1': _L1_attn_in['b1'], 'L1_attn_W2': _L1_attn_in['W2'], 'L1_attn_b2': _L1_attn_in['b2'], 'L1_ffn_w1': _L1_ffn_in['w1'], 'L1_ffn_conv_w': _L1_ffn_in['conv_w'], 'L1_ffn_conv_b': _L1_ffn_in['conv_b'], 'L1_ffn_w2': _L1_ffn_in['w2']}

def reference(x, ctx_1024, mask_Bx1xSxS2_bk1, L0_xattn_w_sim, L0_xattn_b_sim, L0_xattn_W_qv, L0_xattn_b_qv, L0_attn_Wq, L0_attn_bq, L0_attn_Wk, L0_attn_bk, L0_attn_Wv, L0_attn_bv, L0_attn_Wo, L0_attn_bo, L0_ffn_router_w, L0_ffn_router_b, L0_ffn_routed_w1, L0_ffn_routed_w3, L0_ffn_routed_w2, L0_ffn_shared_w1, L0_ffn_shared_w3, L0_ffn_shared_w2, L1_xattn_Wq, L1_xattn_bq, L1_xattn_Wk, L1_xattn_bk, L1_xattn_Wv, L1_xattn_bv, L1_xattn_Wo, L1_xattn_bo, L1_attn_Wq, L1_attn_Wk, L1_attn_Wv, L1_attn_lq1, L1_attn_lq2, L1_attn_lk1, L1_attn_lk2, L1_attn_Wo, L1_attn_bo, L1_attn_ln1_g, L1_attn_ln1_b, L1_attn_ln2_g, L1_attn_ln2_b, L1_attn_W1, L1_attn_b1, L1_attn_W2, L1_attn_b2, L1_ffn_w1, L1_ffn_conv_w, L1_ffn_conv_b, L1_ffn_w2):
    import jax
    import jax.numpy as jnp

    def _L0_xattn_ref(encoder_hc, decoder_hq, w_sim, b_sim, W_qv, b_qv):
        import jax, jax.numpy as jnp
        import numpy as np
        B, L_ENC, L_DEC, D = (16, 256, 128, 512)
        d = encoder_hc.shape[-1]
        w1, w2, w3 = (w_sim[:d], w_sim[d:2 * d], w_sim[2 * d:])
        Sim = (encoder_hc @ w1)[:, :, None] + (decoder_hq @ w2)[:, None, :] + jnp.einsum('bid,bjd->bij', encoder_hc * w3, decoder_hq) + b_sim[0]
        A = jax.nn.softmax(Sim, axis=2)
        hq_hat = jnp.einsum('bij,bjd->bid', A, decoder_hq)
        Batt = jax.nn.softmax(jnp.max(Sim, axis=2), axis=1)
        hc_bar = jnp.einsum('bi,bid->bd', Batt, encoder_hc)[:, None, :]
        hc_hat = jnp.broadcast_to(hc_bar, encoder_hc.shape)
        feats = jnp.concatenate([encoder_hc, hq_hat, encoder_hc * hq_hat, encoder_hc * hc_hat], axis=-1)
        hcq = feats @ W_qv + b_qv
        return hcq

    def _L0_attn_ref(y_all, Wq, bq, Wk, bk, Wv, bv, Wo, bo):
        import jax, jax.numpy as jnp
        import numpy as np
        HIDDEN, KEY_DIM, VALUE_DIM = (512, 512, 512)
        BATCH, SEQ = (8, 1024)
        B, T, H = y_all.shape
        dk = Wq.shape[1]
        q = (y_all @ Wq + bq) / jnp.sqrt(jnp.asarray(dk, y_all.dtype))
        k = y_all @ Wk + bk
        v = y_all @ Wv + bv
        scores = jnp.einsum('bid,bjd->bij', q, k)
        causal = jnp.tril(jnp.ones((T, T), dtype=bool))
        scores = jnp.where(causal, scores, -jnp.inf)
        weights = jax.nn.softmax(scores, axis=-1)
        ctx = jnp.einsum('bij,bjd->bid', weights, v)
        return ctx @ Wo + bo

    def _L0_ffn_ref(x, router_w, router_b, routed_w1, routed_w3, routed_w2, shared_w1, shared_w3, shared_w2):
        import jax, jax.numpy as jnp
        import numpy as np
        BEST_K = 2

        def _expert(xf, w1, w3, w2):
            return jax.nn.silu(xf @ w1) * (xf @ w3) @ w2
        B, S, D = x.shape
        T = B * S
        xf = x.reshape(T, D)
        logits = xf @ router_w + router_b
        topk_vals, topk_idx = jax.lax.top_k(logits, BEST_K)
        sparse = jnp.full_like(logits, -jnp.inf)
        sparse = sparse.at[jnp.arange(T)[:, None], topk_idx].set(topk_vals)
        gates = jax.nn.softmax(sparse, axis=-1)
        routed = jax.vmap(_expert, in_axes=(None, 0, 0, 0))(xf, routed_w1, routed_w3, routed_w2)
        routed_out = jnp.einsum('etd,te->td', routed, gates)
        shared_out = jax.vmap(_expert, in_axes=(None, 0, 0, 0))(xf, shared_w1, shared_w3, shared_w2).sum(axis=0)
        return (routed_out + shared_out).reshape(B, S, D)

    def _L1_xattn_ref(queries, keys, values, mask, Wq, bq, Wk, bk, Wv, bv, Wo, bo):
        import jax, jax.numpy as jnp
        import numpy as np
        B, S, D, H = (4, 1024, 512, 16)
        HD = D // H
        b, sq, d = queries.shape

        def split_heads(x):
            return x.reshape(b, x.shape[1], H, HD).transpose(0, 2, 1, 3)
        q = split_heads(queries @ Wq + bq)
        k = split_heads(keys @ Wk + bk)
        v = split_heads(values @ Wv + bv)
        scores = jnp.einsum('bhqd,bhkd->bhqk', q, k) / jnp.sqrt(jnp.float32(HD))
        scores = jnp.where(mask, jnp.float32(-1000000000000000.0), scores)
        attn = jax.nn.softmax(scores, axis=-1)
        ctx = jnp.einsum('bhqk,bhkd->bhqd', attn, v)
        ctx = ctx.transpose(0, 2, 1, 3).reshape(b, sq, d)
        return ctx @ Wo + bo

    def _L1_attn_ref(x, Wq, Wk, Wv, lq1, lq2, lk1, lk2, Wo, bo, ln1_g, ln1_b, ln2_g, ln2_b, W1, b1, W2, b2):
        import jax, jax.numpy as jnp
        import numpy as np
        B, N, DM, H, FF = (8, 1024, 512, 16, 2048)
        D = DM // H // 2
        LAMBDA_INIT = 0.8 - 0.6 * float(np.exp(-0.3 * 1.0))

        def _layernorm(x, g, b, eps=1e-05):
            mu = jnp.mean(x, axis=-1, keepdims=True)
            var = jnp.mean(jnp.square(x - mu), axis=-1, keepdims=True)
            return (x - mu) * jax.lax.rsqrt(var + eps) * g + b

        def _rmsnorm(x, eps=1e-05):
            return x * jax.lax.rsqrt(jnp.mean(x * x, axis=-1, keepdims=True) + eps)

        def _diff_attn(x, Wq, Wk, Wv, lq1, lq2, lk1, lk2, Wo, bo):
            b, n, d = x.shape
            scale = D ** (-0.5)
            q = (x @ Wq.T).reshape(b, n, H, D, 2).transpose(0, 1, 4, 2, 3).reshape(b, n, 2 * H, D) * scale
            k = (x @ Wk.T).reshape(b, n, H, D, 2).transpose(0, 1, 4, 2, 3).reshape(b, n, 2 * H, D)
            v = (x @ Wv.T).reshape(b, n, H, 2 * D).transpose(0, 2, 1, 3)
            att = jnp.einsum('bnqd,bnkd->bnqk', q, k)
            att = jnp.nan_to_num(att)
            att = jax.nn.softmax(att.astype(jnp.float32), axis=-1)
            lam = jnp.exp(jnp.sum(lq1 * lk1)) - jnp.exp(jnp.sum(lq2 * lk2)) + LAMBDA_INIT
            att6 = att.reshape(b, n, 2, H, 2, H)
            att2 = att6[:, :, 0, :, 0, :] - lam * att6[:, :, 1, :, 1, :]
            out = jnp.einsum('bnah,bhnd->bnad', att2, v)
            out = _rmsnorm(out) * (1.0 - LAMBDA_INIT)
            out = out.reshape(b, n, d)
            return out @ Wo.T + bo
        skip = x
        h = _layernorm(x, ln1_g, ln1_b)
        src2 = _diff_attn(h, Wq, Wk, Wv, lq1, lq2, lk1, lk2, Wo, bo)
        conn = skip + src2
        skip2 = conn
        h2 = _layernorm(conn, ln2_g, ln2_b)
        src3 = jax.nn.relu(h2 @ W1.T + b1) @ W2.T + b2
        return skip2 + src3

    def _L1_ffn_ref(x, w1, conv_w, conv_b, w2):
        import jax, jax.numpy as jnp
        import numpy as np
        B, S, D_MODEL, D_HIDDEN = (4, 1024, 512, 2048)

        def act_quant(x):
            scale = 127.0 / jnp.clip(jnp.max(jnp.abs(x), axis=-1, keepdims=True), 1e-05)
            return jnp.clip(jnp.round(x * scale), -128, 127) / scale

        def weight_quant(w):
            scale = 1.0 / jnp.clip(jnp.mean(jnp.abs(w)), 1e-05)
            return jnp.clip(jnp.round(w * scale), -1, 1) / scale

        def bit_linear(x, w):
            xq = x + jax.lax.stop_gradient(act_quant(x) - x)
            wq = w + jax.lax.stop_gradient(weight_quant(w) - w)
            return jnp.einsum('bsd,hd->bsh', xq, wq)

        def depthwise_conv1d(x_bcl, w, b):
            y = jax.lax.conv_general_dilated(x_bcl, w, window_strides=(1,), padding=[(1, 1)], dimension_numbers=('NCH', 'OIH', 'NCH'), feature_group_count=x_bcl.shape[1])
            return y + b[None, :, None]
        h = bit_linear(x, w1)
        h = depthwise_conv1d(h.transpose(0, 2, 1), conv_w, conv_b)
        h = h.transpose(0, 2, 1)
        h = jax.nn.silu(h)
        return bit_linear(h, w2)
    x = x + _L0_xattn_ref(_layernorm(x, axis=-1), ctx_1024, L0_xattn_w_sim, L0_xattn_b_sim, L0_xattn_W_qv, L0_xattn_b_qv)
    x = x + _L0_attn_ref(_layernorm(x, axis=-1), L0_attn_Wq, L0_attn_bq, L0_attn_Wk, L0_attn_bk, L0_attn_Wv, L0_attn_bv, L0_attn_Wo, L0_attn_bo)
    x = x + _L0_ffn_ref(_layernorm(x, axis=-1), L0_ffn_router_w, L0_ffn_router_b, L0_ffn_routed_w1, L0_ffn_routed_w3, L0_ffn_routed_w2, L0_ffn_shared_w1, L0_ffn_shared_w3, L0_ffn_shared_w2)
    x = x + _L1_xattn_ref(_layernorm(x, axis=-1), ctx_1024, ctx_1024, mask_Bx1xSxS2_bk1, L1_xattn_Wq, L1_xattn_bq, L1_xattn_Wk, L1_xattn_bk, L1_xattn_Wv, L1_xattn_bv, L1_xattn_Wo, L1_xattn_bo)
    x = x + _L1_attn_ref(_layernorm(x, axis=-1), L1_attn_Wq, L1_attn_Wk, L1_attn_Wv, L1_attn_lq1, L1_attn_lq2, L1_attn_lk1, L1_attn_lk2, L1_attn_Wo, L1_attn_bo, L1_attn_ln1_g, L1_attn_ln1_b, L1_attn_ln2_g, L1_attn_ln2_b, L1_attn_W1, L1_attn_b1, L1_attn_W2, L1_attn_b2)
    x = x + _L1_ffn_ref(_layernorm(x, axis=-1), L1_ffn_w1, L1_ffn_conv_w, L1_ffn_conv_b, L1_ffn_w2)
    return x

_drawn_inputs = setup_inputs


def setup_inputs(seed=0):
    import zlib

    import numpy as np

    out = dict(_drawn_inputs(seed))
    spreads = {'L0_ffn_router_b': (0.0, 0.8),
     'L1_xattn_bq': (0.0, 0.455),
     'L1_xattn_bk': (0.0, 2.0),
     'L1_xattn_bv': (0.0, 0.1),
     'L1_xattn_bo': (0.0, 0.1),
     'L1_attn_bo': (0.0, 0.1),
     'L1_attn_ln1_g': (1.0, 0.562),
     'L1_attn_ln1_b': (0.0, 0.616),
     'L1_attn_ln2_g': (1.0, 0.6),
     'L1_attn_ln2_b': (0.0, 0.679),
     'L1_attn_b1': (0.0, 0.278),
     'L1_attn_b2': (0.0, 0.1)}
    factors = {'L0_xattn_b_qv': 3.364,
     'L0_attn_Wq': 2.845,
     'L0_attn_bq': 8.0,
     'L0_attn_Wk': 2.975,
     'L0_attn_bk': 200.0,
     'L0_attn_bv': 4.659,
     'L0_attn_bo': 2.799,
     'L0_ffn_router_w': 3.359,
     'L0_ffn_routed_w1': 2.924,
     'L0_ffn_routed_w3': 2.869,
     'L0_ffn_routed_w2': 2.869,
     'L1_attn_lq1': 8.0,
     'L1_attn_lq2': 200.0,
     'L1_attn_lk1': 8.0,
     'L1_attn_lk2': 8.0}
    for name, (base, spread) in spreads.items():
        noise = np.random.default_rng([zlib.crc32(name.encode()), seed]).standard_normal(out[name].shape)
        drawn = base * np.exp(spread * noise) if base else spread * noise
        out[name] = jnp.asarray(drawn.astype(out[name].dtype))
    for name, factor in factors.items():
        out[name] = (out[name] * factor).astype(out[name].dtype)
    return out
```

```python
from contextlib import ExitStack

import concourse.bass as bass
from concourse import mybir

ALU = mybir.AluOpType
ACT = mybir.ActivationFunctionType
AX = mybir.AxisListType
F32 = mybir.dt.float32
F32R = mybir.dt.float32r
BF16 = mybir.dt.bfloat16
U8 = mybir.dt.uint8
U32 = mybir.dt.uint32

P = 128
D = 512
KC = D // P
BATCH, SEQ, KEYS = 16, 64, 1601
TOKENS = BATCH * SEQ
TILES = TOKENS // P
HALF = 512
HALVES = TOKENS // HALF
EPS = 1e-5
ROUND = 1.5 * 2.0**23


class Space:

    def __init__(self, nc, ctx, stage):
        self.nc, self.ctx, self.stage = nc, ctx, stage

    def sb(self, name, shape, dt=F32):
        return self.ctx.enter_context(self.nc.sbuf_tensor(f"{self.stage}_{name}", shape, dt))

    def ps(self, name, shape, dt=F32):
        return self.ctx.enter_context(self.nc.psum_tensor(f"{self.stage}_{name}", shape, dt))

    def sem(self, name):
        return self.ctx.enter_context(self.nc.semaphore(f"{self.stage}_{name}"))


def wait_after(engine, semaphore, count):
    if not isinstance(count, int) or count > 0:
        engine.wait_ge(semaphore, count)


def product(pe, out, w_hi, w_lo, x_hi, x_lo, first, last):
    pe.matmul(out, w_hi, x_hi, start=first, stop=False)
    pe.matmul(out, w_hi, x_lo, start=False, stop=False)
    return pe.matmul(out, w_lo, x_hi, start=False, stop=last)


def rows_of(ap, n):
    return ap.rearrange("(a d) -> a d", a=1).to_broadcast([n, ap.shape[0]])


def split_hi(nc, hi, x):
    return nc.scalar.activation(hi, x, ACT.Copy)


def split_lo(nc, lo, x, hi):
    return nc.vector.tensor_tensor(lo, x, hi.bitcast(F32), ALU.subtract)


def norm_stage(nc, stage, x_sb, xn, ident, gamma=None, beta=None, y=None, yT=None, hi=None, lo=None,
               prefetch=None):
    with ExitStack() as ctx:
        s = Space(nc, ctx, stage)
        stats = s.sb("stats", [P, TILES, 6])
        mv = s.sb("mv", [P, TILES, 2])
        table = s.sb("table", [P, 1])
        ve = s.sb("ve", [P, TILES])
        sd = s.sb("sd", [P, TILES])
        r0 = s.sb("r0", [P, TILES])
        r1 = s.sb("r1", [P, TILES])
        r2 = s.sb("r2", [P, TILES])
        rstd = s.sb("rstd", [P, TILES])
        g_sb = s.sb("gamma", [P, D]) if gamma is not None else None
        b_sb = s.sb("beta", [P, D]) if beta is not None else None
        turned = s.ps("turned", [P, 4, D])
        affine_loaded, var_ready, sd_ready = s.sem("affine_loaded"), s.sem("var_ready"), s.sem("sd_ready")
        chain, normed, mid = s.sem("chain"), s.sem("normed"), s.sem("mid")
        turned_ready, hi_ready, lo_ready = s.sem("turned_ready"), s.sem("hi_ready"), s.sem("lo_ready")
        src = y if y is not None else xn
        transposed = yT is not None or hi is not None

        with nc.Block() as block:

            @block.sync
            def _(sp):
                if gamma is not None:
                    sp.dma_start(g_sb[:], rows_of(gamma, P)).then_inc(affine_loaded, 16)
                    sp.dma_start(b_sb[:], rows_of(beta, P)).then_inc(affine_loaded, 16)
                if prefetch is not None:
                    prefetch(sp)

            @block.vector
            def _(dve):
                step = [0]

                def link(ins):
                    step[0] += 1
                    ins.then_inc(chain, 1)
                    dve.wait_ge(chain, step[0])

                for t in range(TILES):
                    last = nc.vector.bn_stats(stats[:, t, :], x_sb[:, t, :])
                link(last)
                for t in range(TILES):
                    last = nc.vector.bn_aggr(mv[:, t, :], stats[:, t, :])
                link(last)
                nc.vector.tensor_scalar(ve[:], mv[:, :, 1], EPS, None, ALU.add).then_inc(var_ready, 1)
                dve.wait_ge(sd_ready, 1)
                link(nc.vector.reciprocal(r0[:], sd[:]))
                link(nc.vector.tensor_tensor(r1[:], r0[:], r0[:], ALU.mult))
                link(nc.vector.tensor_tensor(r2[:], r1[:], ve[:], ALU.mult))
                link(nc.vector.tensor_scalar(r1[:], r2[:], -0.5, 1.5, ALU.mult, ALU.add))
                link(nc.vector.tensor_tensor(rstd[:], r0[:], r1[:], ALU.mult))
                if gamma is not None:
                    dve.wait_ge(affine_loaded, 32)
                for t in range(TILES):
                    ins = nc.vector.tensor_scalar(xn[:, t, :], x_sb[:, t, :], mv[:, t, 0:1], rstd[:, t:t + 1],
                                                  ALU.subtract, ALU.mult)
                    if gamma is None:
                        ins.then_inc(normed, 1)
                        continue
                    ins.then_inc(mid, 1)
                    dve.wait_ge(mid, 2 * t + 1)
                    nc.vector.tensor_tensor(y[:, t, :], xn[:, t, :], g_sb[:], ALU.mult).then_inc(mid, 1)
                    dve.wait_ge(mid, 2 * t + 2)
                    nc.vector.tensor_tensor(y[:, t, :], y[:, t, :], b_sb[:], ALU.add).then_inc(normed, 1)
                if hi is not None:
                    for t in range(TILES):
                        dve.wait_ge(hi_ready, t + 1)
                        split_lo(nc, lo[:, :, t * P:(t + 1) * P], turned[:, t % 4, :].rearrange("p (k c) -> p k c", k=KC),
                                 hi[:, :, t * P:(t + 1) * P]).then_inc(lo_ready, 1)

            @block.scalar
            def _(act):
                nc.scalar.activation(table[:], ident[:, 0:1], ACT.Sqrt)
                act.wait_ge(var_ready, 1)
                nc.scalar.activation(sd[:], ve[:], ACT.Sqrt).then_inc(sd_ready, 1)
                if transposed:
                    for t in range(TILES):
                        act.wait_ge(turned_ready, t + 1)
                        out = yT if yT is not None else hi
                        split_hi(nc, out[:, :, t * P:(t + 1) * P],
                                 turned[:, t % 4, :].rearrange("p (k c) -> p k c", k=KC)).then_inc(hi_ready, 1)

            @block.tensor
            def _(pe):
                if transposed:
                    for t in range(TILES):
                        pe.wait_ge(normed, t + 1)
                        if t >= 4:
                            pe.wait_ge(hi_ready, t - 3)
                            if hi is not None:
                                pe.wait_ge(lo_ready, t - 3)
                        for k in range(KC):
                            last = pe.transpose(turned[:, t % 4, k * P:(k + 1) * P], src[:, t, k * P:(k + 1) * P], ident[:])
                        last.then_inc(turned_ready, 1)


GROUP = 401
GROUPS = 4
GROUP_W = [GROUP] * 3 + [KEYS - 3 * GROUP]
KT = -(-KEYS // P)
TAIL = KEYS - (KT - 1) * P
BUNCH = [(0, 4), (4, 8), (8, 12), (12, 13)]


def rows(n):
    return TAIL if n == KT - 1 else P


def bidaf_scores_stage(nc, hcwT, ident, ctx_rows, ctx_cols, hq, neg_max):
    with ExitStack() as ctx:
        s = Space(nc, ctx, "bs")
        cols = s.sb("cols", [P, GROUPS, 2, KC, GROUP])
        rws = s.sb("rows", [P, 2, KT, D])
        q = s.sb("q", [P, KC, P])
        a = s.sb("a", [P, KEYS])
        aT = s.sb("aT", [P, KT, P])
        mx = s.sb("mx", [P, GROUPS])
        nm = s.sb("nm", [P, 1])
        rs = s.sb("rs", [P, GROUPS])
        rsum = s.sb("rsum", [P, 1])
        rinv = s.sb("rinv", [P, 1])
        S = s.ps("S", [P, GROUPS, 512])
        turned = s.ps("turned", [P, 2, 512])
        hqp = s.ps("hqp", [P, 512])
        cols_loaded = [s.sem(f"cols_loaded{g}") for g in range(GROUPS)]
        rows_loaded = [s.sem(f"rows_loaded{g}") for g in range(GROUPS)]
        q_staged, scored, max_ready, exp_done = s.sem("q_staged"), s.sem("scored"), s.sem("max_ready"), s.sem("exp_done")
        a_turned, aT_act, aT_dve = s.sem("a_turned"), s.sem("aT_act"), s.sem("aT_dve")
        summed, hq_stored, chain = s.sem("summed"), s.sem("hq_stored"), s.sem("chain")
        CHAIN = 4

        with nc.Block() as block:

            @block.sync
            def _(sp):
                def load_cols(pair, g):
                    w = GROUP_W[g]
                    for b in range(2):
                        src = ctx_cols[2 * pair + b].rearrange("(k p) j -> p k j", p=P)[:, :, g * GROUP:g * GROUP + w]
                        sp.dma_start(cols[:, g, b, :, 0:w], src).then_inc(cols_loaded[g], 16)

                def load_rows(pair, g):
                    n0, n1 = BUNCH[g]
                    for b in range(2):
                        if g == GROUPS - 1:
                            sp.dma_start(rws[0:TAIL, b, n0, :], ctx_rows[2 * pair + b][n0 * P:KEYS, :]).then_inc(rows_loaded[g], 16)
                        else:
                            src = ctx_rows[2 * pair + b][n0 * P:n1 * P, :].rearrange("(n p) d -> p n d", p=P)
                            sp.dma_start(rws[:, b, n0:n1, :], src).then_inc(rows_loaded[g], 16)

                for g in range(GROUPS):
                    load_cols(0, g)
                for g in range(GROUPS):
                    load_rows(0, g)
                with sp.Fori(0, TILES - 1) as t:
                    for g in range(GROUPS):
                        sp.wait_ge(scored, GROUPS * t + g + 1)
                        load_cols(t + 1, g)
                    for g in range(GROUPS):
                        sp.wait_ge(summed, GROUPS * t + g + 1)
                        load_rows(t + 1, g)

            @block.tensor
            def _(pe):
                def pair(t):
                    pe.wait_ge(q_staged, t + 1)
                    wait_after(pe, exp_done, GROUPS * t)
                    for g in range(GROUPS):
                        w = GROUP_W[g]
                        pe.wait_ge(cols_loaded[g], 32 * t + 32)
                        for k in range(KC):
                            for b in range(2):
                                last = pe.matmul(S[64 * b:64 * b + 64, g, 0:w], q[:, k, 64 * b:64 * b + 64],
                                                 cols[:, g, b, k, 0:w], start=(k == 0), stop=(k == KC - 1))
                        last.then_inc(scored, 1)
                    pe.wait_ge(exp_done, GROUPS * t + GROUPS)
                    for g, (n0, n1) in enumerate(BUNCH):
                        wait_after(pe, aT_dve if g % 2 else aT_act, 2 * t + g // 2)
                        for n in range(n0, n1):
                            r = rows(n)
                            last = pe.transpose(turned[0:r, g % 2, (n - n0) * P:(n - n0 + 1) * P], a[:, n * P:n * P + r], ident[:])
                        last.then_inc(a_turned, 1)
                    wait_after(pe, hq_stored, t)
                    for g, (n0, n1) in enumerate(BUNCH):
                        pe.wait_ge(aT_dve if g % 2 else aT_act, 2 * t + g // 2 + 1)
                        pe.wait_ge(rows_loaded[g], 32 * t + 32)
                        for n in range(n0, n1):
                            r = rows(n)
                            for b in range(2):
                                last = pe.matmul(hqp[64 * b:64 * b + 64, :], aT[0:r, n, 64 * b:64 * b + 64],
                                                 rws[0:r, b, n, :], start=(n == 0), stop=(n == KT - 1))
                        last.then_inc(summed, 1)

                pair(0)
                with pe.Fori(1, TILES) as t:
                    pair(t)

            def copy_turned(copy, g):
                n0, n1 = BUNCH[g]
                r = rows(n1 - 1)
                return copy(aT[0:r, n0:n1, :], turned[0:r, g % 2, 0:(n1 - n0) * P].rearrange("p (n c) -> p n c", c=P))

            @block.vector
            def _(dve):
                def pair(t):
                    wait_after(dve, scored, GROUPS * t)
                    nc.vector.tensor_copy(q[:], hcwT[:, :, bass.ds(t * P, P)]).then_inc(q_staged, 1)
                    for g in range(GROUPS):
                        dve.wait_ge(scored, GROUPS * t + g + 1)
                        last = nc.vector.reduce_max(mx[:, g:g + 1], S[:, g, 0:GROUP_W[g]], AX.X)
                    last.then_inc(chain, 1)
                    dve.wait_ge(chain, CHAIN * t + 1)
                    nc.vector.tensor_reduce(nm[:], mx[:], AX.X, ALU.max, negate=True).then_inc(max_ready, 1)
                    dve.wait_ge(max_ready, t + 1)
                    nc.vector.tensor_copy(neg_max[:, bass.ds(t, 1)], nm[:]).then_inc(chain, 1)
                    dve.wait_ge(exp_done, GROUPS * t + GROUPS)
                    nc.vector.reduce_sum(rsum[:], rs[:], AX.X).then_inc(chain, 1)
                    dve.wait_ge(chain, CHAIN * t + 3)
                    nc.vector.reciprocal(rinv[:], rsum[:]).then_inc(chain, 1)
                    for g in (1, 3):
                        dve.wait_ge(a_turned, GROUPS * t + g + 1)
                        copy_turned(nc.vector.tensor_copy, g).then_inc(aT_dve, 1)
                    dve.wait_ge(chain, CHAIN * t + 4)
                    dve.wait_ge(summed, GROUPS * t + GROUPS)
                    nc.vector.tensor_scalar(hq[:, bass.ds(t * D, D)], hqp[:], rinv[:], None, ALU.mult).then_inc(hq_stored, 1)

                pair(0)
                with dve.Fori(1, TILES) as t:
                    pair(t)

            @block.scalar
            def _(act):
                def pair(t):
                    act.wait_ge(max_ready, t + 1)
                    wait_after(act, a_turned, GROUPS * t)
                    for g in range(GROUPS):
                        w = GROUP_W[g]
                        nc.scalar.activation(a[:, g * GROUP:g * GROUP + w], S[:, g, 0:w], ACT.Exp, bias=nm[:, 0:1],
                                             accum_out=rs[:, g:g + 1]).then_inc(exp_done, 1)
                    for g in (0, 2):
                        act.wait_ge(a_turned, GROUPS * t + g + 1)
                        copy_turned(lambda o, i: nc.scalar.activation(o, i, ACT.Copy), g).then_inc(aT_act, 1)

                pair(0)
                with act.Fori(1, TILES) as t:
                    pair(t)


def bidaf_merge_stage(nc, x_sb, hc, hq, neg_max, ident, w1, b_sim, W, bias):
    FC = 4 * KC
    with ExitStack() as ctx:
        s = Space(nc, ctx, "bm")
        w_raw = s.sb("w_raw", [P, KC, D])
        w_hi, w_lo = s.sb("w_hi", [P, FC, D], F32R), s.sb("w_lo", [P, FC, D], F32R)
        f_hi, f_lo = s.sb("f_hi", [P, 2, FC, P], F32R), s.sb("f_lo", [P, 2, FC, P], F32R)
        hh, hb = s.sb("hh", [P, 2, D]), s.sb("hb", [P, 2, D])
        w1_sb, bias_sb, bsim_sb = s.sb("w1", [P, D]), s.sb("bias", [P, D]), s.sb("bsim", [P, 1])
        scratch = s.sb("scratch", [P, D])
        sc, m, batt = s.sb("sc", [P, TILES]), s.sb("m", [P, TILES]), s.sb("batt", [P, TILES])
        blocks = s.sb("blocks", [P, P])
        mix = s.sb("mix", [P, 2, P])
        mT, eT = s.sb("mT", [TILES, P]), s.sb("eT", [TILES, P])
        mm, es, er = s.sb("mm", [TILES, 2]), s.sb("es", [TILES, 2]), s.sb("er", [TILES, 2])
        turned = s.ps("turned", [P, 4, 512])
        out = s.ps("out", [P, 2, 512])
        bar = s.ps("bar", [P, 512])
        small = s.ps("small", [P, 512])
        w_loaded, small_loaded = s.sem("w_loaded"), s.sem("small_loaded")
        w_hi_ready, w_lo_ready = s.sem("w_hi_ready"), s.sem("w_lo_ready")
        chain, blocks_ready, biased = s.sem("chain"), s.sem("blocks_ready"), s.sem("biased")
        m_ready, m_turned, max_sub, exp_done, e_ready, batt_turned = (s.sem(n) for n in
            ("m_ready", "m_turned", "max_sub", "exp_done", "e_ready", "batt_turned"))
        mix_ready, bar_ready, feats_ready, f_turned, f_hi_ready, f_lo_ready, out_ready, added = (s.sem(n) for n in
            ("mix_ready", "bar_ready", "feats_ready", "f_turned", "f_hi_ready", "f_lo_ready", "out_ready", "added"))

        with nc.Block() as block:

            @block.sync
            def _(sp):
                sp.dma_start(w1_sb[:], rows_of(w1, P)).then_inc(small_loaded, 16)
                sp.dma_start(bsim_sb[:], rows_of(b_sim, P)).then_inc(small_loaded, 16)
                sp.dma_start(bias_sb[:], rows_of(bias, P)).then_inc(small_loaded, 16)
                for c in range(4):
                    if c:
                        sp.wait_ge(w_hi_ready, c)
                        sp.wait_ge(w_lo_ready, c)
                    sp.dma_start(w_raw[:], W[c * D:(c + 1) * D, :].rearrange("(k p) n -> p k n", p=P)).then_inc(w_loaded, 16)

            @block.gpsimd
            def _(pool):
                nc.gpsimd.memset(blocks[:], 0.0).then_inc(blocks_ready, 1)
                pool.wait_ge(blocks_ready, 1)
                nc.gpsimd.memset(blocks[0:64, 0:64], 1.0).then_inc(blocks_ready, 1)
                nc.gpsimd.memset(blocks[64:128, 64:128], 1.0).then_inc(blocks_ready, 1)
                pool.wait_ge(blocks_ready, 3)
                pool.wait_ge(small_loaded, 48)
                for t in range(TILES):
                    nc.gpsimd.tensor_tensor(x_sb[:, t, :], x_sb[:, t, :], bias_sb[:], ALU.add).then_inc(biased, 1)

            @block.vector
            def _(dve):
                step = [0]

                def link(ins):
                    step[0] += 1
                    ins.then_inc(chain, 1)
                    dve.wait_ge(chain, step[0])

                dve.wait_ge(small_loaded, 48)
                for t in range(TILES):
                    link(nc.vector.tensor_tensor(scratch[:], hc[:, t, :], w1_sb[:], ALU.mult))
                    link(nc.vector.reduce_sum(sc[:, t:t + 1], scratch[:], AX.X))
                link(nc.vector.tensor_tensor(m[:], sc[:], neg_max[:], ALU.subtract))
                nc.vector.tensor_scalar(m[:], m[:], bsim_sb[:, 0:1], None, ALU.add).then_inc(m_ready, 1)
                dve.wait_ge(m_turned, 1)
                link(nc.vector.tensor_copy(mT[:], small[0:TILES, 0:P]))
                link(nc.vector.tensor_reduce(mm[:], mT[:].rearrange("t (b i) -> t b i", b=2), AX.X, ALU.max))
                for b in range(2):
                    last = nc.vector.tensor_scalar(mT[:, 64 * b:64 * b + 64], mT[:, 64 * b:64 * b + 64], mm[:, b:b + 1], None, ALU.subtract)
                    last.then_inc(max_sub, 1)
                dve.wait_ge(exp_done, 1)
                link(nc.vector.reduce_sum(es[:], eT[:].rearrange("t (b i) -> t b i", b=2), AX.X))
                link(nc.vector.reciprocal(er[:], es[:]))
                for b in range(2):
                    nc.vector.tensor_scalar(eT[:, 64 * b:64 * b + 64], eT[:, 64 * b:64 * b + 64], er[:, b:b + 1], None, ALU.mult)\
                        .then_inc(e_ready, 1)
                dve.wait_ge(batt_turned, 1)
                link(nc.vector.tensor_copy(batt[:], small[:, 256:256 + TILES]))
                dve.wait_ge(blocks_ready, 3)

                def lows(t):
                    for c in range(4):
                        dve.wait_ge(f_hi_ready, 4 * t + c + 1)
                        nc.vector.tensor_tensor(f_lo[:, t % 2, 4 * c:4 * c + 4, :], turned[:, c, :].rearrange("p (k c) -> p k c", c=P),
                                                f_hi[:, t % 2, 4 * c:4 * c + 4, :].bitcast(F32), ALU.subtract).then_inc(f_lo_ready, 1)

                def feats(t):
                    if t >= 2:
                        dve.wait_ge(bar_ready, t - 1)
                        dve.wait_ge(f_turned, 4 * t - 4)
                    nc.vector.tensor_scalar(mix[:, t % 2, :], blocks[:], batt[:, t:t + 1], None, ALU.mult).then_inc(mix_ready, 1)
                    nc.vector.tensor_tensor(hh[:, t % 2, :], hc[:, t, :], hq[:, t * D:(t + 1) * D], ALU.mult).then_inc(feats_ready, 1)
                    dve.wait_ge(bar_ready, t + 1)
                    nc.vector.tensor_tensor(hb[:, t % 2, :], hc[:, t, :], bar[:], ALU.mult).then_inc(feats_ready, 1)

                def add(t):
                    dve.wait_ge(out_ready, t + 1)
                    dve.wait_ge(biased, t + 1)
                    nc.vector.tensor_tensor(x_sb[:, t, :], out[:, t % 2, :], x_sb[:, t, :], ALU.add).then_inc(added, 1)

                for c in range(4):
                    dve.wait_ge(w_hi_ready, c + 1)
                    split_lo(nc, w_lo[:, 4 * c:4 * c + 4, :], w_raw[:], w_hi[:, 4 * c:4 * c + 4, :]).then_inc(w_lo_ready, 1)
                feats(0)
                lows(0)
                for t in range(TILES):
                    if t + 1 < TILES:
                        feats(t + 1)
                        lows(t + 1)
                    add(t)

            @block.scalar
            def _(act):
                act.wait_ge(max_sub, 2)
                nc.scalar.activation(eT[:], mT[:], ACT.Exp).then_inc(exp_done, 1)
                for c in range(4):
                    act.wait_ge(w_loaded, 16 * c + 16)
                    split_hi(nc, w_hi[:, 4 * c:4 * c + 4, :], w_raw[:]).then_inc(w_hi_ready, 1)
                for t in range(TILES):
                    if t >= 2:
                        act.wait_ge(out_ready, t - 1)
                    for c in range(4):
                        act.wait_ge(f_turned, 4 * t + c + 1)
                        split_hi(nc, f_hi[:, t % 2, 4 * c:4 * c + 4, :], turned[:, c, :].rearrange("p (k c) -> p k c", c=P))\
                            .then_inc(f_hi_ready, 1)

            @block.tensor
            def _(pe):
                pe.wait_ge(m_ready, 1)
                pe.transpose(small[0:TILES, 0:P], m[:], ident[:]).then_inc(m_turned, 1)
                pe.wait_ge(e_ready, 2)
                pe.transpose(small[:, 256:256 + TILES], eT[:], ident[0:TILES, 0:TILES]).then_inc(batt_turned, 1)

                def mixing(t):
                    pe.wait_ge(mix_ready, t + 1)
                    if t >= 1:
                        pe.wait_ge(feats_ready, 2 * t)
                    pe.matmul(bar[:], mix[:, t % 2, :], hc[:, t, :], start=True, stop=True).then_inc(bar_ready, 1)

                def turn(t):
                    for c in range(4):
                        if c == 2:
                            pe.wait_ge(feats_ready, 2 * t + 1)
                        if c == 3:
                            pe.wait_ge(feats_ready, 2 * t + 2)
                        if t:
                            pe.wait_ge(f_hi_ready, 4 * (t - 1) + c + 1)
                            pe.wait_ge(f_lo_ready, 4 * (t - 1) + c + 1)
                        src = (hc[:, t, :], hq[:, t * D:(t + 1) * D], hh[:, t % 2, :], hb[:, t % 2, :])[c]
                        for k in range(KC):
                            last = pe.transpose(turned[:, c, k * P:(k + 1) * P], src[:, k * P:(k + 1) * P], ident[:])
                        last.then_inc(f_turned, 1)

                mixing(0)
                turn(0)
                for t in range(TILES):
                    if t + 1 < TILES:
                        mixing(t + 1)
                        turn(t + 1)
                    if t >= 2:
                        pe.wait_ge(added, t - 1)
                    for f in range(FC):
                        if f % 4 == 0:
                            if t == 0:
                                pe.wait_ge(w_lo_ready, f // 4 + 1)
                            pe.wait_ge(f_lo_ready, 4 * t + f // 4 + 1)
                        last = product(pe, out[:, t % 2, :], f_hi[:, t % 2, f, :], f_lo[:, t % 2, f, :],
                                       w_hi[:, f, :], w_lo[:, f, :], f == 0, f == FC - 1)
                    last.then_inc(out_ready, 1)


def bidaf_layer(nc, x_sb, ident, ctx_rows, ctx_cols, w_sim, b_sim, W, bias):
    with ExitStack() as ctx:
        s = Space(nc, ctx, "bidaf")
        hc = s.sb("hc", [P, TILES, D])
        hq = s.sb("hq", [P, TILES * D])
        neg_max = s.sb("neg_max", [P, TILES])
        with ExitStack() as inner:
            i = Space(nc, inner, "bidafq")
            hcwT = i.sb("hcwT", [P, KC, TOKENS])
            with ExitStack() as inner2:
                hcw = Space(nc, inner2, "bidafw").sb("hcw", [P, TILES, D])
                norm_stage(nc, "n0", x_sb, hc, ident, gamma=w_sim[2 * D:3 * D], beta=w_sim[D:2 * D], y=hcw, yT=hcwT)
            bidaf_scores_stage(nc, hcwT, ident, ctx_rows, ctx_cols, hq, neg_max)
        bidaf_merge_stage(nc, x_sb, hc, hq, neg_max, ident, w_sim[0:D], b_sim, W, bias)


FEATURES, TOKENWISE, RESIDUAL = range(3)


def project_stage(nc, stage, a_hi, a_lo, jobs):
    N = len(jobs)
    UNITS = 8
    with ExitStack() as ctx:
        s = Space(nc, ctx, stage)
        raw = s.sb("raw", [P, 2, KC, D])
        w_hi, w_lo = s.sb("w_hi", [P, 2, KC, D], F32R), s.sb("w_lo", [P, 2, KC, D], F32R)
        bias_col = s.sb("bias_col", [P, N, KC])
        bias_scaled = s.sb("bias_scaled", [P, N, KC])
        bias_row = s.sb("bias_row", [P, N, D])
        out_ps = s.ps("out", [P, 4, 512])
        w_loaded = [s.sem("w_loaded0"), s.sem("w_loaded1")]
        first_loaded = [s.sem(f"first_loaded{k}") for k in range(KC)]
        bias_loaded, bias_ready = s.sem("bias_loaded"), s.sem("bias_ready")
        w_hi_ready, w_lo_ready = s.sem("w_hi_ready"), s.sem("w_lo_ready")
        produced, stored_act, stored_dve = s.sem("produced"), s.sem("stored_act"), s.sem("stored_dve")
        n_bias = sum(b is not None for _, _, b, _, _ in jobs)
        biased = [j[2] is not None for j in jobs]

        def stored_before(j):
            act = UNITS * sum(jobs[i][0] == FEATURES for i in range(j))
            return act, UNITS * j - act

        with nc.Block() as block:

            @block.sync
            def _(sp):
                for k in range(KC):
                    sp.dma_start(raw[:, 0, k, :], jobs[0][1][k * P:(k + 1) * P, :]).then_inc(first_loaded[k], 16)
                for j, (kind, W, bias, scale, out) in enumerate(jobs):
                    if bias is not None:
                        if kind == FEATURES:
                            with nc.allow_non_contiguous_dma(reason="512 values, once"):
                                sp.dma_start(bias_col[:, j, :], bias.rearrange("(k p) -> p k", p=P)).then_inc(bias_loaded, 16)
                        else:
                            sp.dma_start(bias_row[:, j, :], rows_of(bias, P)).then_inc(bias_loaded, 16)
                    if j >= 2:
                        sp.wait_ge(w_hi_ready, KC + j - 2)
                        sp.wait_ge(w_lo_ready, KC + j - 2)
                    if j:
                        sp.dma_start(raw[:, j % 2, :, :], W.rearrange("(k p) n -> p k n", p=P)).then_inc(w_loaded[j % 2], 16)

            @block.scalar
            def _(act):
                def take(j):
                    act.wait_ge(w_loaded[j % 2], 16 * ((j - 1) // 2) + 16)
                    if j >= 2:
                        act.wait_ge(produced, UNITS * (j - 1))
                    split_hi(nc, w_hi[:, j % 2, :, :], raw[:, j % 2, :, :]).then_inc(w_hi_ready, 1)

                for k in range(KC):
                    act.wait_ge(first_loaded[k], 16)
                    split_hi(nc, w_hi[:, 0, k, :], raw[:, 0, k, :]).then_inc(w_hi_ready, 1)
                for j, (kind, W, bias, scale, out) in enumerate(jobs):
                    if j + 1 < N:
                        take(j + 1)
                    if kind == FEATURES:
                        if n_bias:
                            act.wait_ge(bias_ready, 1)
                        for u in range(UNITS):
                            act.wait_ge(produced, UNITS * j + u + 1)
                            m, h = u // HALVES, u % HALVES
                            nc.scalar.activation(out[:, m, h * HALF:(h + 1) * HALF], out_ps[:, u % 4, :], ACT.Identity,
                                                 bias=bias_scaled[:, j, m:m + 1] if biased[j] else 0.0,
                                                 scale=scale).then_inc(stored_act, 1)

            @block.vector
            def _(dve):
                for k in range(KC):
                    dve.wait_ge(w_hi_ready, k + 1)
                    split_lo(nc, w_lo[:, 0, k, :], raw[:, 0, k, :], w_hi[:, 0, k, :]).then_inc(w_lo_ready, 1)
                if n_bias:
                    dve.wait_ge(bias_loaded, 16 * n_bias)
                    for j, (kind, W, bias, scale, out) in enumerate(jobs):
                        if kind == FEATURES and biased[j]:
                            last = nc.vector.tensor_scalar(bias_scaled[:, j, :], bias_col[:, j, :], scale, None, ALU.mult)
                            last_is = last
                    if any(k == FEATURES and b is not None for k, _, b, _, _ in jobs):
                        last_is.then_inc(bias_ready, 1)

                def take(j):
                    dve.wait_ge(w_hi_ready, KC + j)
                    split_lo(nc, w_lo[:, j % 2, :, :], raw[:, j % 2, :, :], w_hi[:, j % 2, :, :]).then_inc(w_lo_ready, 1)

                for j, (kind, W, bias, scale, out) in enumerate(jobs):
                    if j + 1 < N:
                        take(j + 1)
                    if kind == FEATURES:
                        continue
                    for u in range(UNITS):
                        dve.wait_ge(produced, UNITS * j + u + 1)
                        if kind == TOKENWISE and not biased[j]:
                            nc.vector.tensor_scalar(out[:, u, :], out_ps[:, u % 4, :], scale, None, ALU.mult).then_inc(stored_dve, 1)
                        elif kind == TOKENWISE:
                            nc.vector.tensor_tensor(out[:, u, :], out_ps[:, u % 4, :], bias_row[:, j, :], ALU.add).then_inc(stored_dve, 1)
                        else:
                            dve.wait_ge(bias_ready, u + 1)
                            nc.vector.tensor_tensor(out[:, u, :], out_ps[:, u % 4, :], out[:, u, :], ALU.add).then_inc(stored_dve, 1)

            @block.gpsimd
            def _(pool):
                for j, (kind, W, bias, scale, out) in enumerate(jobs):
                    if kind == RESIDUAL:
                        pool.wait_ge(bias_loaded, 16 * n_bias)
                        for u in range(TILES):
                            nc.gpsimd.tensor_tensor(out[:, u, :], out[:, u, :], bias_row[:, j, :], ALU.add).then_inc(bias_ready, 1)

            @block.tensor
            def _(pe):
                for j, (kind, W, bias, scale, out) in enumerate(jobs):
                    if j:
                        pe.wait_ge(w_lo_ready, KC + j)
                    for u in range(UNITS):
                        if UNITS * j + u >= 4:
                            v = UNITS * j + u - 4
                            by_act, by_dve = stored_before(v // UNITS)
                            if jobs[v // UNITS][0] == FEATURES:
                                pe.wait_ge(stored_act, by_act + v % UNITS + 1)
                            else:
                                pe.wait_ge(stored_dve, by_dve + v % UNITS + 1)
                        for k in range(KC):
                            if j == 0 and u == 0:
                                pe.wait_ge(w_lo_ready, k + 1)
                            if kind == FEATURES:
                                m, h = u // HALVES, u % HALVES
                                ws = slice(m * P, (m + 1) * P)
                                xs = slice(h * HALF, (h + 1) * HALF)
                                last = product(pe, out_ps[:, u % 4, :], w_hi[:, j % 2, k, ws], w_lo[:, j % 2, k, ws],
                                               a_hi[:, k, xs], a_lo[:, k, xs], k == 0, k == KC - 1)
                            else:
                                xs = slice(u * P, (u + 1) * P)
                                last = product(pe, out_ps[:, u % 4, :], a_hi[:, k, xs], a_lo[:, k, xs],
                                               w_hi[:, j % 2, k, :], w_lo[:, j % 2, k, :], k == 0, k == KC - 1)
                        last.then_inc(produced, 1)


def causal_attention_stage(nc, qT, kT, v, ident, c_hi, c_lo):
    NEVER = -1e30
    with ExitStack() as ctx:
        s = Space(nc, ctx, "ca")
        causal = s.sb("causal", [P, P])
        sc = s.sb("sc", [P, 2, P])
        pr = s.sb("pr", [P, 2, P])
        pT = s.sb("pT", [P, 2, P])
        nm, rs, ri = s.sb("nm", [P, TILES]), s.sb("rs", [P, TILES]), s.sb("ri", [P, TILES])
        S = s.ps("S", [P, 2, 512])
        T = s.ps("T", [P, 2, 512])
        C = s.ps("C", [P, 2, 512])
        (mask_steps, scored, masked, max_ready, exp_done, inv_ready, scaled, turned, pT_ready, summed, hi_ready,
         lo_ready) = (s.sem(n) for n in ("mask_steps", "scored", "masked", "max_ready", "exp_done", "inv_ready", "scaled",
                                         "turned", "pT_ready", "summed", "hi_ready", "lo_ready"))
        with nc.Block() as block:

            @block.gpsimd
            def _(pool):
                nc.gpsimd.memset(causal[:], 0.0).then_inc(mask_steps, 1)
                pool.wait_ge(mask_steps, 1)
                nc.gpsimd.affine_select(out=causal[:], in_=causal[:], compare_op=ALU.is_ge, fill=NEVER, base=0,
                                        pattern=[[-1, P]], channel_multiplier=1).then_inc(mask_steps, 1)
                pool.wait_ge(mask_steps, 2)
                nc.gpsimd.memset(causal[SEQ:P, 0:SEQ], NEVER).then_inc(mask_steps, 1)

            @block.tensor
            def _(pe):
                def scores(t):
                    if t >= 2:
                        pe.wait_ge(masked, t - 1)
                    for k in range(KC):
                        last = pe.matmul(S[:, t % 2, 0:P], qT[:, k, t * P:(t + 1) * P], kT[:, k, t * P:(t + 1) * P],
                                         start=(k == 0), stop=(k == KC - 1))
                    last.then_inc(scored, 1)

                scores(0)
                for t in range(TILES):
                    if t + 1 < TILES:
                        scores(t + 1)
                    pe.wait_ge(scaled, t + 1)
                    if t >= 2:
                        pe.wait_ge(pT_ready, t - 1)
                    pe.transpose(T[:, t % 2, 0:P], pr[:, t % 2, :], ident[:]).then_inc(turned, 1)
                    pe.wait_ge(pT_ready, t + 1)
                    if t >= 2:
                        pe.wait_ge(hi_ready, t - 1)
                        pe.wait_ge(lo_ready, t - 1)
                    for m in range(KC):
                        last = pe.matmul(C[:, t % 2, m * P:(m + 1) * P], v[:, t, m * P:(m + 1) * P], pT[:, t % 2, :],
                                         start=True, stop=True)
                    last.then_inc(summed, 1)

            @block.vector
            def _(dve):
                dve.wait_ge(mask_steps, 3)

                def front(t):
                    dve.wait_ge(scored, t + 1)
                    if t >= 2:
                        dve.wait_ge(exp_done, t - 1)
                    nc.vector.tensor_tensor(sc[:, t % 2, :], S[:, t % 2, 0:P], causal[:], ALU.add).then_inc(masked, 1)
                    dve.wait_ge(masked, t + 1)
                    nc.vector.tensor_reduce(nm[:, t:t + 1], sc[:, t % 2, :], AX.X, ALU.max, negate=True).then_inc(max_ready, 1)

                def back(t):
                    dve.wait_ge(exp_done, t + 1)
                    nc.vector.reciprocal(ri[:, t:t + 1], rs[:, t:t + 1]).then_inc(inv_ready, 1)
                    dve.wait_ge(inv_ready, t + 1)
                    nc.vector.tensor_scalar(pr[:, t % 2, :], pr[:, t % 2, :], ri[:, t:t + 1], None, ALU.mult).then_inc(scaled, 1)
                    dve.wait_ge(turned, t + 1)
                    if t >= 2:
                        dve.wait_ge(summed, t - 1)
                    nc.vector.tensor_copy(pT[:, t % 2, :], T[:, t % 2, 0:P]).then_inc(pT_ready, 1)
                    dve.wait_ge(hi_ready, t + 1)
                    split_lo(nc, c_lo[:, :, t * P:(t + 1) * P], C[:, t % 2, :].rearrange("p (k c) -> p k c", c=P),
                             c_hi[:, :, t * P:(t + 1) * P]).then_inc(lo_ready, 1)

                front(0)
                for t in range(TILES):
                    if t + 1 < TILES:
                        front(t + 1)
                    back(t)

            @block.scalar
            def _(act):
                def front(t):
                    act.wait_ge(max_ready, t + 1)
                    if t >= 2:
                        act.wait_ge(turned, t - 1)
                    nc.scalar.activation(pr[:, t % 2, :], sc[:, t % 2, :], ACT.Exp, bias=nm[:, t:t + 1],
                                         accum_out=rs[:, t:t + 1]).then_inc(exp_done, 1)

                front(0)
                for t in range(TILES):
                    if t + 1 < TILES:
                        front(t + 1)
                    act.wait_ge(summed, t + 1)
                    split_hi(nc, c_hi[:, :, t * P:(t + 1) * P], C[:, t % 2, :].rearrange("p (k c) -> p k c", c=P)).then_inc(hi_ready, 1)


def causal_layer(nc, x_sb, ident, Wq, bq, Wk, bk, Wv, bv, Wo, bo):
    with ExitStack() as ctx:
        s = Space(nc, ctx, "attn0")
        a_hi, a_lo = s.sb("a_hi", [P, KC, TOKENS], F32R), s.sb("a_lo", [P, KC, TOKENS], F32R)
        with ExitStack() as inner:
            xn = Space(nc, inner, "attn0x").sb("xn", [P, TILES, D])
            norm_stage(nc, "n1", x_sb, xn, ident, hi=a_hi, lo=a_lo)
        with ExitStack() as inner:
            i = Space(nc, inner, "attn0i")
            qT, kT, v = i.sb("qT", [P, KC, TOKENS]), i.sb("kT", [P, KC, TOKENS]), i.sb("v", [P, TILES, D])
            project_stage(nc, "pj0", a_hi, a_lo, [(FEATURES, Wq, bq, D**-0.5, qT), (FEATURES, Wk, bk, 1.0, kT),
                                                 (TOKENWISE, Wv, bv, 1.0, v)])
            causal_attention_stage(nc, qT, kT, v, ident, a_hi, a_lo)
        project_stage(nc, "pj1", a_hi, a_lo, [(RESIDUAL, Wo, bo, 1.0, x_sb)])


EXPERTS, SHARED, HID = 8, 2, 256
HC = HID // P


def router_stage(nc, a_hi, a_lo, ident, router_w, router_b, gates):
    with ExitStack() as ctx:
        s = Space(nc, ctx, "rt")
        raw = s.sb("raw", [P, KC, P])
        w_hi, w_lo = s.sb("w_hi", [P, KC, P], F32R), s.sb("w_lo", [P, KC, P], F32R)
        b_sb = s.sb("b", [EXPERTS, 1])
        lT = s.sb("lT", [EXPERTS, TOKENS])
        lg = s.sb("lg", [P, TILES, EXPERTS])
        top = s.sb("top", [P, TILES, 8])
        at = s.sb("at", [P, TILES, 8], U32)
        at_f = s.sb("at_f", [P, TILES, 8])
        diff, e1, den, g0, g1 = (s.sb(n, [P, TILES]) for n in ("diff", "e1", "den", "g0", "g1"))
        number = s.sb("number", [P, EXPERTS])
        first, second = s.sb("first", [P, TILES, EXPERTS]), s.sb("second", [P, TILES, EXPERTS])
        L = s.ps("L", [P, HALVES, 512])
        T = s.ps("T", [P, 512])
        (w_loaded, cleared, w_hi_ready, w_lo_ready, l_ready, lT_ready, turned, chain, diff_ready, e1_ready, number_ready) = (
            s.sem(n) for n in ("w_loaded", "cleared", "w_hi_ready", "w_lo_ready", "l_ready", "lT_ready", "turned", "chain",
                               "diff_ready", "e1_ready", "number_ready"))
        with nc.Block() as block:

            @block.gpsimd
            def _(pool):
                nc.gpsimd.iota(number[:], [[1, EXPERTS]], base=0, channel_multiplier=0,
                               allow_small_or_imprecise_dtypes=True).then_inc(number_ready, 1)

            @block.sync
            def _(sp):
                sp.wait_ge(cleared, 1)
                sp.dma_start(raw[:, :, 0:EXPERTS], router_w.rearrange("(k p) e -> p k e", p=P)).then_inc(w_loaded, 16)
                sp.dma_start(b_sb[:], router_b.rearrange("(e a) -> e a", a=1)).then_inc(w_loaded, 16)

            @block.scalar
            def _(act):
                act.wait_ge(w_loaded, 32)
                split_hi(nc, w_hi[:], raw[:]).then_inc(w_hi_ready, 1)
                for h in range(HALVES):
                    act.wait_ge(l_ready, h + 1)
                    nc.scalar.activation(lT[:, h * HALF:(h + 1) * HALF], L[0:EXPERTS, h, :], ACT.Identity, bias=b_sb[:, 0:1])\
                        .then_inc(lT_ready, 1)
                act.wait_ge(diff_ready, 1)
                nc.scalar.activation(e1[:], diff[:], ACT.Exp).then_inc(e1_ready, 1)

            @block.tensor
            def _(pe):
                pe.wait_ge(w_lo_ready, 1)
                for h in range(HALVES):
                    for k in range(KC):
                        last = product(pe, L[:, h, :], w_hi[:, k, :], w_lo[:, k, :], a_hi[:, k, h * HALF:(h + 1) * HALF],
                                       a_lo[:, k, h * HALF:(h + 1) * HALF], k == 0, k == KC - 1)
                    last.then_inc(l_ready, 1)
                pe.wait_ge(lT_ready, 2)
                for t in range(TILES):
                    last = pe.transpose(T[:, t * EXPERTS:(t + 1) * EXPERTS], lT[:, t * P:(t + 1) * P], ident[0:EXPERTS, 0:EXPERTS])
                last.then_inc(turned, 1)

            @block.vector
            def _(dve):
                step = [0]

                def link(ins):
                    step[0] += 1
                    ins.then_inc(chain, 1)
                    dve.wait_ge(chain, step[0])

                nc.vector.memset(raw[:], 0.0).then_inc(cleared, 1)
                dve.wait_ge(w_hi_ready, 1)
                split_lo(nc, w_lo[:], raw[:], w_hi[:]).then_inc(w_lo_ready, 1)
                dve.wait_ge(turned, 1)
                link(nc.vector.tensor_copy(lg[:], T[:, 0:TILES * EXPERTS].rearrange("p (t e) -> p t e", e=EXPERTS)))
                for t in range(TILES):
                    last = nc.vector.max(top[:, t, :], lg[:, t, :])
                link(last)
                for t in range(TILES):
                    last = nc.vector.max_index(at[:, t, :], top[:, t, :], lg[:, t, :])
                link(last)
                link(nc.vector.tensor_copy(at_f[:], at[:]))
                nc.vector.tensor_tensor(diff[:], top[:, :, 1], top[:, :, 0], ALU.subtract).then_inc(diff_ready, 1)
                dve.wait_ge(e1_ready, 1)
                link(nc.vector.tensor_scalar(den[:], e1[:], 1.0, None, ALU.add))
                link(nc.vector.reciprocal(g0[:], den[:]))
                link(nc.vector.tensor_tensor(g1[:], e1[:], g0[:], ALU.mult))
                dve.wait_ge(number_ready, 1)
                for t in range(TILES):
                    nc.vector.tensor_scalar(first[:, t, :], number[:], at_f[:, t, 0:1], g0[:, t:t + 1], ALU.is_equal, ALU.mult)
                    last = nc.vector.tensor_scalar(second[:, t, :], number[:], at_f[:, t, 1:2], g1[:, t:t + 1], ALU.is_equal, ALU.mult)
                link(last)
                nc.vector.memset(gates[:, :, EXPERTS:EXPERTS + SHARED], 1.0)
                nc.vector.tensor_tensor(gates[:, :, 0:EXPERTS], first[:], second[:], ALU.add).then_inc(chain, 1)


def experts_stage(nc, x_sb, a_hi, a_lo, gates, routed, shared):
    N = EXPERTS + SHARED
    UNITS = HALVES * HC
    with ExitStack() as ctx:
        s = Space(nc, ctx, "ex")
        raw13, raw2 = s.sb("raw13", [P, 2, KC, HID]), s.sb("raw2", [P, HC, D])
        w13_hi, w13_lo = s.sb("w13_hi", [P, 2, KC, HID], F32R), s.sb("w13_lo", [P, 2, KC, HID], F32R)
        w2_hi, w2_lo = s.sb("w2_hi", [P, HC, D], F32R), s.sb("w2_lo", [P, HC, D], F32R)
        act1, h32 = s.sb("act1", [P, 2, HALF]), s.sb("h32", [P, 2, HALF])
        h_hi, h_lo = s.sb("h_hi", [P, HC, TOKENS], F32R), s.sb("h_lo", [P, HC, TOKENS], F32R)
        gate = s.sb("gate", [P, TILES])
        H = s.ps("H", [P, 2, 2, 512])
        O = s.ps("O", [P, 4, 512])
        (w13_loaded, w2_loaded, w13_hi_ready, w13_lo_ready, w2_hi_ready, w2_lo_ready, h_produced, silu_ready, h32_ready,
         h_hi_ready, h_lo_ready, o_produced, added, gate_ready) = (s.sem(n) for n in (
             "w13_loaded", "w2_loaded", "w13_hi_ready", "w13_lo_ready", "w2_hi_ready", "w2_lo_ready", "h_produced",
             "silu_ready", "h32_ready", "h_hi_ready", "h_lo_ready", "o_produced", "added", "gate_ready"))

        def hidden(buf, u):
            return buf[:, u % HC, (u // HC) * HALF:(u // HC + 1) * HALF]

        with nc.Block() as block:

            @block.sync
            def _(sp):
                def load(n, e, w1, w3, w2):
                    wait_after(sp, w13_lo_ready, n)
                    sp.dma_start(raw13[:, 0, :, :], w1[e].rearrange("(k p) h -> p k h", p=P)).then_inc(w13_loaded, 16)
                    sp.dma_start(raw13[:, 1, :, :], w3[e].rearrange("(k p) h -> p k h", p=P)).then_inc(w13_loaded, 16)
                    wait_after(sp, w2_lo_ready, n)
                    sp.dma_start(raw2[:], w2[e].rearrange("(k p) n -> p k n", p=P)).then_inc(w2_loaded, 16)

                load(0, 0, *routed)
                with sp.Fori(1, EXPERTS) as e:
                    load(e, e, *routed)
                with sp.Fori(0, SHARED) as e:
                    load(e + EXPERTS, e, *shared)

            @block.scalar
            def _(act):
                def split13(n):
                    act.wait_ge(w13_loaded, 32 * n + 32)
                    wait_after(act, h_produced, UNITS * n)
                    split_hi(nc, w13_hi[:], raw13[:]).then_inc(w13_hi_ready, 1)

                def expert(n, more):
                    act.wait_ge(w2_loaded, 16 * n + 16)
                    wait_after(act, o_produced, TILES * n)
                    split_hi(nc, w2_hi[:], raw2[:]).then_inc(w2_hi_ready, 1)

                    def high(u):
                        act.wait_ge(h32_ready, UNITS * n + u + 1)
                        split_hi(nc, hidden(h_hi, u), h32[:, u % 2, :]).then_inc(h_hi_ready, 1)

                    for u in range(UNITS):
                        act.wait_ge(h_produced, UNITS * n + u + 1)
                        nc.scalar.activation(act1[:, u % 2, :], H[:, u % 2, 0, :], ACT.Silu).then_inc(silu_ready, 1)
                        if u:
                            high(u - 1)
                    high(UNITS - 1)
                    if more:
                        split13(n + 1)

                split13(0)
                expert(0, True)
                with act.Fori(1, N - 1) as n:
                    expert(n, True)
                expert(N - 1, False)

            @block.vector
            def _(dve):
                def split13(n):
                    dve.wait_ge(w13_hi_ready, n + 1)
                    split_lo(nc, w13_lo[:], raw13[:], w13_hi[:]).then_inc(w13_lo_ready, 1)

                def expert(n, more):
                    wait_after(dve, added, TILES * n)
                    nc.vector.tensor_copy(gate[:], gates[:, :, bass.ds(n, 1)].rearrange("p t e -> p (t e)")).then_inc(gate_ready, 1)
                    dve.wait_ge(w2_hi_ready, n + 1)
                    split_lo(nc, w2_lo[:], raw2[:], w2_hi[:]).then_inc(w2_lo_ready, 1)

                    def low(u):
                        dve.wait_ge(h_hi_ready, UNITS * n + u + 1)
                        split_lo(nc, hidden(h_lo, u), h32[:, u % 2, :], hidden(h_hi, u)).then_inc(h_lo_ready, 1)

                    for u in range(UNITS):
                        dve.wait_ge(silu_ready, UNITS * n + u + 1)
                        if u >= 2:
                            dve.wait_ge(h_lo_ready, UNITS * n + u - 1)
                        nc.vector.tensor_tensor(h32[:, u % 2, :], act1[:, u % 2, :], H[:, u % 2, 1, :], ALU.mult).then_inc(h32_ready, 1)
                        if u:
                            low(u - 1)
                    low(UNITS - 1)
                    if more:
                        split13(n + 1)
                    dve.wait_ge(gate_ready, n + 1)
                    for t in range(TILES):
                        dve.wait_ge(o_produced, TILES * n + t + 1)
                        nc.vector.scalar_tensor_tensor(out=x_sb[:, t, :], in0=O[:, t % 4, :], scalar=gate[:, t:t + 1],
                                                       in1=x_sb[:, t, :], op0=ALU.mult, op1=ALU.add).then_inc(added, 1)

                split13(0)
                expert(0, True)
                with dve.Fori(1, N - 1) as n:
                    expert(n, True)
                expert(N - 1, False)

            @block.tensor
            def _(pe):
                def expert(n):
                    pe.wait_ge(w13_lo_ready, n + 1)
                    for u in range(UNITS):
                        th, m = u // HC, u % HC
                        if u >= 2:
                            pe.wait_ge(h32_ready, UNITS * n + u - 1)
                        else:
                            wait_after(pe, h32_ready, UNITS * n)
                        for j in range(2):
                            for k in range(KC):
                                last = product(pe, H[:, u % 2, j, :], w13_hi[:, j, k, m * P:(m + 1) * P], w13_lo[:, j, k, m * P:(m + 1) * P],
                                               a_hi[:, k, th * HALF:(th + 1) * HALF], a_lo[:, k, th * HALF:(th + 1) * HALF],
                                               k == 0, k == KC - 1)
                        last.then_inc(h_produced, 1)
                    pe.wait_ge(w2_lo_ready, n + 1)
                    for t in range(TILES):
                        pe.wait_ge(h_lo_ready, UNITS * n + (t // 4) * HC + HC)
                        if t >= 4:
                            pe.wait_ge(added, TILES * n + t - 3)
                        else:
                            wait_after(pe, added, TILES * n)
                        for m in range(HC):
                            last = product(pe, O[:, t % 4, :], h_hi[:, m, t * P:(t + 1) * P], h_lo[:, m, t * P:(t + 1) * P],
                                           w2_hi[:, m, :], w2_lo[:, m, :], m == 0, m == HC - 1)
                        last.then_inc(o_produced, 1)

                expert(0)
                with pe.Fori(1, N) as n:
                    expert(n)


def experts_layer(nc, x_sb, ident, router_w, router_b, routed, shared):
    with ExitStack() as ctx:
        s = Space(nc, ctx, "moe")
        a_hi, a_lo = s.sb("a_hi", [P, KC, TOKENS], F32R), s.sb("a_lo", [P, KC, TOKENS], F32R)
        gates = s.sb("gates", [P, TILES, EXPERTS + SHARED])
        with ExitStack() as inner:
            xn = Space(nc, inner, "moex").sb("xn", [P, TILES, D])
            norm_stage(nc, "n2", x_sb, xn, ident, hi=a_hi, lo=a_lo)
        router_stage(nc, a_hi, a_lo, ident, router_w, router_b, gates)
        experts_stage(nc, x_sb, a_hi, a_lo, gates, routed, shared)


HEADS, HEAD = 16, 32
HG = P // HEAD
GR = HEADS // HG
KG = 402
KP = 4 * KG
NEVER = -3e38
MASKED = -1e15


def cross_attention_stage(nc, qoT, x_sb, x_kept, ctx_cols, mask, Wk, bk, Wv, bv, ident):
    T_GROUPS = [(n, min(n + 2, KT)) for n in range(0, KT, 2)]
    ACT_T = [i for i in range(len(T_GROUPS)) if i % 2 == 0]
    DVE_T = [i for i in range(len(T_GROUPS)) if i % 2 == 1]
    TG = len(T_GROUPS)
    TURNS = ((), (0, 1), (2, 3), (5, 6))
    AMID = 4
    DVE_CHUNKS = 2
    PARTS = ((0, 2 * KG), (2 * KG, KEYS))
    with ExitStack() as ctx:
        s = Space(nc, ctx, "xa")
        wk_hi, wk_lo = s.sb("wk_hi", [P, KC, D], F32R), s.sb("wk_lo", [P, KC, D], F32R)
        wv_hi, wv_lo = s.sb("wv_hi", [P, KC, D], F32R), s.sb("wv_lo", [P, KC, D], F32R)
        bk_sb, bv_sb = s.sb("bk", [P, KC]), s.sb("bv", [P, D])
        own_raw = s.sb("raw", [P, 2, KEYS])
        lent = x_sb[:].rearrange("p t d -> p (t d)")
        M8_AT, O_AT = 2 * KEYS, 2 * KEYS + -(-KEYS // 4)
        lent_raw = lent[:, 0:M8_AT].rearrange("p (k j) -> p k j", k=2)
        m8 = lent[:, M8_AT:O_AT].bitcast(U8)[:, 0:KEYS]
        o = lent[:, O_AT:O_AT + GR * SEQ].rearrange("p (g i) -> p g i", g=GR)
        c_hi, c_lo = s.sb("c_hi", [P, KC, KP], F32R), s.sb("c_lo", [P, KC, KP], F32R)
        kT_hi, kT_lo = s.sb("kT_hi", [P, KP], F32R), s.sb("kT_lo", [P, KP], F32R)
        v = s.sb("v", [P, KT, D])
        m = s.sb("m", [P, KP])
        pr = s.sb("pr", [P, 2, KP])
        pT = s.sb("pT", [P, KT, 2 * P])
        q_hi, q_lo = s.sb("q_hi", [P, GR, 2, P], F32R), s.sb("q_lo", [P, GR, 2, P], F32R)
        mx, nm, rs, ri = s.sb("mx", [P, 2, 2]), s.sb("nm", [P, 2]), s.sb("rs", [P, 2]), s.sb("ri", [P, 2])
        S = s.ps("S", [P, 4, 512])
        J = s.ps("J", [P, 2, 512])
        T = s.ps("T", [P, 2, 512])
        w_loaded, w_hi_ready, w_lo_ready, small_loaded, cleared = (s.sem(n) for n in (
            "w_loaded", "w_hi_ready", "w_lo_ready", "small_loaded", "cleared"))
        raw_loaded = [s.sem(f"raw_loaded{k}") for k in range(KC)]
        x_stored, x_loaded = s.sem("x_stored"), s.sem("x_loaded")
        mask_loaded, c_hi_ready, c_lo_ready, m_ready, q_hi_ready, q_ready, c_lo_pool = (s.sem(n) for n in (
            "mask_loaded", "c_hi_ready", "c_lo_ready", "m_ready", "q_hi_ready", "q_ready", "c_lo_pool"))
        k_made, v_made, k_hi_ready, k_lo_ready, v_stored, scored, masked, max_ready, exp_done, inv_ready, scaled = (s.sem(n) for n in (
            "k_made", "v_made", "k_hi_ready", "k_lo_ready", "v_stored", "scored", "masked", "max_ready", "exp_done", "inv_ready", "scaled"))
        turned, t_act, t_dve, o_made, o_stored, o_kept = (s.sem(n) for n in (
            "turned", "t_act", "t_dve", "o_made", "o_stored", "o_kept"))
        KU, VU = GR * 4, KT
        SU = GR * 2 * 2
        TU = GR * TG
        w_raw = v[:, 0:2 * KC, :].rearrange("p (w k) n -> p w k n", w=2)

        def raw(k):
            return own_raw[:, k, :] if k < 2 else lent_raw[:, k - 2, :]

        def wait_low(engine, b, part, k):
            if k < DVE_CHUNKS:
                engine.wait_ge(c_lo_ready, DVE_CHUNKS * (2 * b + part) + k + 1)
            else:
                engine.wait_ge(c_lo_pool, (KC - DVE_CHUNKS) * (2 * b + part) + k - DVE_CHUNKS + 1)

        def before(b, g):
            if g:
                return b, g - 1
            return None if isinstance(b, int) and b == 0 else (b - 1, GR - 1)

        with nc.Block() as block:

            @block.sync
            def _(sp):
                sp.dma_start(x_kept, x_sb[:]).then_inc(x_stored, 16)
                with nc.allow_non_contiguous_dma(reason="512 values, once"):
                    sp.dma_start(bk_sb[:], bk.rearrange("(k p) -> p k", p=P)).then_inc(small_loaded, 16)
                sp.dma_start(bv_sb[:], rows_of(bv, P)).then_inc(small_loaded, 16)
                sp.dma_start(w_raw[:, 0], Wk.rearrange("(k p) n -> p k n", p=P)).then_inc(w_loaded, 16)
                sp.dma_start(w_raw[:, 1], Wv.rearrange("(k p) n -> p k n", p=P)).then_inc(w_loaded, 16)

                def load(b):
                    for k in range(KC):
                        if before(b, 0):
                            wait_low(sp, b - 1, 1, k)
                        sp.dma_start(raw(k), ctx_cols[b, k * P:(k + 1) * P, :]).then_inc(raw_loaded[k], 16)
                        if k == 1:
                            sp.wait_ge(x_stored, 16)
                            wait_after(sp, m_ready, b)
                            for i in range(2):
                                sp.dma_start(m8[SEQ * i:SEQ * i + SEQ, :], mask[b, 0]).then_inc(mask_loaded, 16)

                load(0)
                with sp.Fori(1, BATCH) as b:
                    load(b)
                sp.wait_ge(o_kept, BATCH)
                sp.dma_start(x_sb[:], x_kept).then_inc(x_loaded, 16)
                sp.wait_ge(x_loaded, 16)

            @block.scalar
            def _(act):
                act.wait_ge(w_loaded, 32)
                split_hi(nc, wk_hi[:], w_raw[:, 0]).then_inc(w_hi_ready, 1)
                split_hi(nc, wv_hi[:], w_raw[:, 1]).then_inc(w_hi_ready, 1)

                def high(b, part, k):
                    act.wait_ge(raw_loaded[k], 16 * b + 16)
                    if k == 0:
                        wait_after(act, k_made, KU * b)
                    split_hi(nc, c_hi[:, k, slice(*PARTS[part])], raw(k)[:, slice(*PARTS[part])]).then_inc(c_hi_ready, 1)

                def keep_key(b, g, j):
                    act.wait_ge(k_made, KU * b + 4 * g + j + 1)
                    nc.scalar.activation(kT_hi[:, j * KG:(j + 1) * KG], J[:, key_bank(g, j), 0:KG], ACT.Identity,
                                         bias=bk_sb[:, g:g + 1]).then_inc(k_hi_ready, 1)

                def widen_mask(b):
                    act.wait_ge(mask_loaded, 32 * b + 32)
                    wait_after(act, masked, SU * b)
                    nc.scalar.activation(m[:, 0:KEYS], m8, ACT.Copy, scale=MASKED).then_inc(m_ready, 1)

                def exps(b, g, i):
                    act.wait_ge(max_ready, 2 * (GR * b + g) + i + 1)
                    nc.scalar.activation(pr[:, i, :], pr[:, i, :], ACT.Exp, bias=nm[:, i:i + 1],
                                         accum_out=rs[:, i:i + 1]).then_inc(exp_done, 1)

                def copy_turned(b, g, i):
                    act.wait_ge(turned, TU * b + TG * g + i + 1)
                    n0, n1 = T_GROUPS[i]
                    r = rows(n1 - 1)
                    nc.scalar.activation(pT[0:r, n0:n1, :], T[0:r, 0, 0:(n1 - n0) * 2 * P].rearrange("p (n c) -> p n c", c=2 * P),
                                         ACT.Copy).then_inc(t_act, 1)

                def keep_result(b, g):
                    act.wait_ge(o_made, GR * b + g + 1)
                    if g == 0:
                        wait_after(act, o_kept, b)
                    nc.scalar.activation(o[:, g, :], J[:, RESULT_BANK[g], 0:SEQ], ACT.Copy).then_inc(o_stored, 1)

                act.wait_ge(cleared, 1)
                act.wait_ge(small_loaded, 32)
                for part in range(2):
                    for k in range(KC):
                        high(0, part, k)

                def batch(b, more):
                    for g in range(GR):
                        old = before(b, g)
                        for j in range(4):
                            if old and j == 3:
                                copy_turned(*old, AMID)
                            keep_key(b, g, j)
                            if g == 0 and j == 0:
                                widen_mask(b)
                            if old:
                                for i in TURNS[j]:
                                    if i in ACT_T:
                                        copy_turned(*old, i)
                        load_next = more and g == GR - 1
                        if load_next:
                            for k in range(KC):
                                high(b + 1, 0, k)
                        exps(b, g, 0)
                        if load_next:
                            high(b + 1, 1, 0)
                            high(b + 1, 1, 1)
                        if old:
                            keep_result(*old)
                        exps(b, g, 1)
                        if load_next:
                            high(b + 1, 1, 2)
                            high(b + 1, 1, 3)

                batch(0, True)
                with act.Fori(1, BATCH - 1) as b:
                    batch(b, True)
                batch(BATCH - 1, False)
                for i in ACT_T:
                    copy_turned(BATCH - 1, GR - 1, i)
                keep_result(BATCH - 1, GR - 1)

            @block.vector
            def _(dve):
                for part in (c_hi, c_lo):
                    last = nc.vector.memset(part[:, :, KEYS:KP].bitcast(F32), 0.0)
                nc.vector.memset(m[:, KEYS:KP], NEVER)
                nc.vector.memset(q_hi[:].bitcast(F32), 0.0)
                nc.vector.memset(q_lo[:].bitcast(F32), 0.0).then_inc(cleared, 1)
                dve.wait_ge(w_hi_ready, 2)
                nc.vector.tensor_tensor(wk_lo[:], w_raw[:, 0], wk_hi[:].bitcast(F32), ALU.subtract).then_inc(w_lo_ready, 1)
                nc.vector.tensor_tensor(wv_lo[:], w_raw[:, 1], wv_hi[:].bitcast(F32), ALU.subtract).then_inc(w_lo_ready, 1)
                dve.wait_ge(cleared, 1)

                def low(b, part, k):
                    dve.wait_ge(c_hi_ready, 2 * KC * b + KC * part + k + 1)
                    js = slice(*PARTS[part])
                    split_lo(nc, c_lo[:, k, js], raw(k)[:, js], c_hi[:, k, js]).then_inc(c_lo_ready, 1)

                def queries(b):
                    wait_after(dve, scored, SU * b)
                    for part in (q_hi, q_lo):
                        for h in range(HG):
                            hs = slice(HEAD * h, HEAD * (h + 1))
                            to = part[hs, :, h // 2, SEQ * (h % 2):SEQ * (h % 2 + 1)]
                            now = qoT[hs, :, bass.ds(b * SEQ, SEQ)]
                            if part is q_hi:
                                last = nc.vector.tensor_copy(to, now)
                            else:
                                rounded = q_hi[hs, :, h // 2, SEQ * (h % 2):SEQ * (h % 2 + 1)]
                                last = nc.vector.tensor_tensor(to, now, rounded.bitcast(F32), ALU.subtract)
                        if part is q_hi:
                            last.then_inc(q_hi_ready, 1)
                            dve.wait_ge(q_hi_ready, b + 1)
                    last.then_inc(q_ready, 1)

                def keep_key(b, g, j):
                    dve.wait_ge(k_hi_ready, KU * b + 4 * g + j + 1)
                    ks = slice(j * KG, (j + 1) * KG)
                    nc.vector.scalar_tensor_tensor(out=kT_lo[:, ks], in0=J[:, key_bank(g, j), 0:KG], scalar=bk_sb[:, g:g + 1],
                                                   in1=kT_hi[:, ks].bitcast(F32), op0=ALU.add, op1=ALU.subtract).then_inc(k_lo_ready, 1)

                def mask_scores(b, g, i):
                    for h in range(2):
                        half = dve.to_reg(SU * b + 4 * g + 2 * i + h + 1)
                        dve.wait_ge(cleared, 1)
                        dve.wait_ge(scored, half)
                        ks = slice(2 * KG * h, 2 * KG * (h + 1))
                        nc.vector.tensor_tensor_reduce(out=pr[:, i, ks].rearrange("p (a c) -> p a c", c=KG), in0=S[:, 2 * h:2 * h + 2, 0:KG],
                                                       in1=m[:, ks].rearrange("p (a c) -> p a c", c=KG), scale=1.0, scalar=NEVER,
                                                       op0=ALU.add, op1=ALU.max, accum_out=mx[:, i, h:h + 1]).then_inc(masked, 1)
                    dve.wait_ge(masked, SU * b + 4 * g + 2 * i + 2)
                    wait_after(dve, exp_done, 2 * (GR * b + g))
                    nc.vector.tensor_reduce(nm[:, i:i + 1], mx[:, i, :], AX.X, ALU.max, negate=True).then_inc(max_ready, 1)

                def normalise(b, g, i):
                    dve.wait_ge(exp_done, 2 * (GR * b + g) + i + 1)
                    nc.vector.reciprocal(ri[:, i:i + 1], rs[:, i:i + 1]).then_inc(inv_ready, 1)
                    dve.wait_ge(inv_ready, 2 * (GR * b + g) + i + 1)
                    nc.vector.tensor_scalar(pr[:, i, :], pr[:, i, :], ri[:, i:i + 1], None, ALU.mult).then_inc(scaled, 1)

                def keep_values(b, n):
                    dve.wait_ge(v_made, VU * b + n + 1)
                    nc.vector.tensor_tensor(v[0:rows(n), n, :], J[0:rows(n), value_bank(n), :], bv_sb[0:rows(n), :], ALU.add)\
                        .then_inc(v_stored, 1)

                def copy_turned(b, g, i):
                    dve.wait_ge(turned, TU * b + TG * g + i + 1)
                    n0, n1 = T_GROUPS[i]
                    nc.vector.tensor_copy(pT[:, n0:n1, :], T[:, 1, :].rearrange("p (n c) -> p n c", c=2 * P)).then_inc(t_dve, 1)

                def keep_results(b):
                    dve.wait_ge(o_stored, GR * b + GR)
                    nc.vector.tensor_copy(qoT[:, :, bass.ds(b * SEQ, SEQ)], o).then_inc(o_kept, 1)

                for part in range(2):
                    for k in range(DVE_CHUNKS):
                        low(0, part, k)
                dve.wait_ge(small_loaded, 32)

                def batch(b, more):
                    for g in range(GR):
                        old = before(b, g)
                        for j in range(4):
                            if g == 0 and j == 3:
                                dve.wait_ge(m_ready, b + 1)
                            keep_key(b, g, j)
                            if g == 0 and j == 0:
                                queries(b)
                            if old:
                                for i in TURNS[j]:
                                    if i in DVE_T:
                                        copy_turned(*old, i)
                        load_next = more and g == GR - 1
                        mask_scores(b, g, 0)
                        if load_next:
                            low(b + 1, 0, 0)
                            low(b + 1, 0, 1)
                        mask_scores(b, g, 1)
                        normalise(b, g, 0)
                        if load_next:
                            low(b + 1, 1, 0)
                            low(b + 1, 1, 1)
                        normalise(b, g, 1)
                        if g == 0:
                            for n in range(KT):
                                keep_values(b, n)
                            if old:
                                keep_results(old[0])

                batch(0, True)
                with dve.Fori(1, BATCH - 1) as b:
                    batch(b, True)
                batch(BATCH - 1, False)
                for i in DVE_T:
                    copy_turned(BATCH - 1, GR - 1, i)
                keep_results(BATCH - 1)

            @block.gpsimd
            def _(pool):
                def low_of_last_chunks(b):
                    for part, (j0, j1) in enumerate(PARTS):
                        for k in range(DVE_CHUNKS, KC):
                            pool.wait_ge(c_hi_ready, 2 * KC * b + KC * part + k + 1)
                            nc.gpsimd.tensor_tensor(c_lo[:, k, j0:j1], raw(k)[:, j0:j1], c_hi[:, k, j0:j1].bitcast(F32), ALU.subtract)\
                                .then_inc(c_lo_pool, 1)

                pool.wait_ge(cleared, 1)
                low_of_last_chunks(0)
                with pool.Fori(1, BATCH) as b:
                    low_of_last_chunks(b)

            @block.tensor
            def _(pe):
                pe.wait_ge(w_lo_ready, 2)

                def bank_free(b, unit):
                    if unit < 2:
                        if not before(b, 0):
                            return
                        b = b - 1
                    kind, g, j = UNITS[unit - 2 if unit >= 2 else LAST_IN_BANK[unit]]
                    if kind == "k":
                        pe.wait_ge(k_lo_ready, KU * b + 4 * g + j + 1)
                    elif kind == "v":
                        pe.wait_ge(v_stored, VU * b + j + 1)
                    elif g == GR - 1:
                        wait_after(pe, o_stored, GR * b)
                    else:
                        pe.wait_ge(o_stored, GR * b + g + 1)

                def key_tile(b, g, j):
                    bank_free(b, UNITS.index(("k", g, j)))
                    for k in range(KC):
                        if k == KC // 2 and j == 3 and before(b, g):
                            turn(*before(b, g), AMID)
                        if g == 0 and j % 2 == 0:
                            wait_low(pe, b, j // 2, k)
                        last = product(pe, J[:, key_bank(g, j), 0:KG], wk_hi[:, k, g * P:(g + 1) * P], wk_lo[:, k, g * P:(g + 1) * P],
                                       c_hi[:, k, j * KG:(j + 1) * KG], c_lo[:, k, j * KG:(j + 1) * KG], k == 0, k == KC - 1)
                    last.then_inc(k_made, 1)

                def values(b):
                    for n in range(KT):
                        bank_free(b, UNITS.index(("v", 0, n)))
                        w = min(P, KP - n * P)
                        for k in range(KC):
                            last = product(pe, J[0:w, value_bank(n), :], c_hi[:, k, n * P:n * P + w], c_lo[:, k, n * P:n * P + w],
                                           wv_hi[:, k, :], wv_lo[:, k, :], k == 0, k == KC - 1)
                        last.then_inc(v_made, 1)

                def scores(b, g, i):
                    if g == 0 and i == 0:
                        pe.wait_ge(q_ready, b + 1)
                    for j in range(4):
                        if i == 0:
                            pe.wait_ge(k_lo_ready, KU * b + 4 * g + j + 1)
                        if j % 2 == 0:
                            if g == 0 and i == 0:
                                wait_after(pe, masked, SU * b)
                            else:
                                wait_after(pe, masked, SU * b + 4 * g + 2 * i + j // 2 - 1)
                        ks = slice(j * KG, (j + 1) * KG)
                        last = product(pe, S[:, j, 0:KG], q_hi[:, g, i, :], q_lo[:, g, i, :], kT_hi[:, ks], kT_lo[:, ks], True, True)
                        if j % 2 == 1:
                            last.then_inc(scored, 1)

                def turn(b, g, i):
                    if i == 0:
                        pe.wait_ge(scaled, 2 * (GR * b + g) + 2)
                    wait_after(pe, t_dve if i % 2 else t_act, (len(DVE_T) if i % 2 else len(ACT_T)) * (GR * b + g) + i // 2)
                    n0, n1 = T_GROUPS[i]
                    for n in range(n0, n1):
                        r = rows(n)
                        for a in range(2):
                            last = pe.transpose(T[0:r, i % 2, (2 * (n - n0) + a) * P:(2 * (n - n0) + a + 1) * P],
                                                pr[:, a, n * P:n * P + r], ident[:])
                    last.then_inc(turned, 1)

                def result(b, g):
                    if g == 0:
                        pe.wait_ge(v_stored, VU * b + VU)
                    if g == GR - 1:
                        if isinstance(b, int) and b == BATCH - 1:
                            pe.wait_ge(o_stored, GR * b + g)
                        pe.wait_ge(k_lo_ready, KU * (b + 1) + 4 if not (isinstance(b, int) and b == BATCH - 1) else KU * BATCH)
                    else:
                        bank_free(b, UNITS.index(("o", g, 0)))
                    for i, (n0, n1) in enumerate(T_GROUPS):
                        pe.wait_ge(t_dve if i % 2 else t_act, (len(DVE_T) if i % 2 else len(ACT_T)) * (GR * b + g) + i // 2 + 1)
                        for n in range(n0, n1):
                            r = rows(n)
                            for h in range(HG):
                                hs = slice(HEAD * h, HEAD * (h + 1))
                                last = pe.matmul(J[hs, RESULT_BANK[g], 0:SEQ], v[0:r, n, g * P + HEAD * h:g * P + HEAD * (h + 1)],
                                                 pT[0:r, n, SEQ * h:SEQ * (h + 1)], start=(n == 0), stop=(n == KT - 1))
                    last.then_inc(o_made, 1)

                def batch(b):
                    for g in range(GR):
                        old = before(b, g)
                        for j in range(4):
                            key_tile(b, g, j)
                            if old:
                                for i in TURNS[j]:
                                    turn(*old, i)
                        scores(b, g, 0)
                        if old:
                            result(*old)
                        scores(b, g, 1)
                        if g == 0:
                            values(b)

                batch(0)
                with pe.Fori(1, BATCH) as b:
                    batch(b)
                for i in range(TG):
                    turn(BATCH - 1, GR - 1, i)
                result(BATCH - 1, GR - 1)


UNITS = ([("k", 0, j) for j in range(4)] + [("o", 3, 0)] + [("v", 0, n) for n in range(KT)] + [("k", 1, j) for j in range(4)]
         + [("o", 0, 0)] + [("k", 2, j) for j in range(4)] + [("o", 1, 0)] + [("k", 3, j) for j in range(4)] + [("o", 2, 0)])
RESULT_BANK = [UNITS.index(("o", g, 0)) % 2 for g in range(GR)]
LAST_IN_BANK = [max(u for u in range(len(UNITS)) if u % 2 == bank) for bank in range(2)]


def key_bank(g, j):
    return UNITS.index(("k", g, j)) % 2


def value_bank(n):
    return UNITS.index(("v", 0, n)) % 2


def cross_layer(nc, x_sb, ident, ctx_cols, mask, Wq, bq, Wk, bk, Wv, bv, Wo, bo):
    x_kept = nc.dram_tensor("x_kept", (P, TILES, D), F32, kind="Internal").ap()
    with ExitStack() as ctx:
        qoT = Space(nc, ctx, "cross").sb("qoT", [P, KC, TOKENS])
        with ExitStack() as inner:
            s = Space(nc, inner, "crossq")
            a_hi, a_lo = s.sb("a_hi", [P, KC, TOKENS], F32R), s.sb("a_lo", [P, KC, TOKENS], F32R)
            with ExitStack() as inner2:
                xn = Space(nc, inner2, "crossx").sb("xn", [P, TILES, D])
                norm_stage(nc, "n3", x_sb, xn, ident, hi=a_hi, lo=a_lo)
            project_stage(nc, "pj2", a_hi, a_lo, [(FEATURES, Wq, bq, HEAD**-0.5, qoT)])
        cross_attention_stage(nc, qoT, x_sb, x_kept, ctx_cols, mask, Wk, bk, Wv, bv, ident)
        with ExitStack() as inner:
            s = Space(nc, inner, "crosso")
            o_hi, o_lo = s.sb("o_hi", [P, KC, TOKENS], F32R), s.sb("o_lo", [P, KC, TOKENS], F32R)
            split_stage(nc, "sp0", qoT, o_hi, o_lo)
            project_stage(nc, "pj3", o_hi, o_lo, [(RESIDUAL, Wo, bo, 1.0, x_sb)])


def split_stage(nc, stage, x, hi, lo):
    with ExitStack() as ctx:
        hi_ready = Space(nc, ctx, stage).sem("hi_ready")
        with nc.Block() as block:

            @block.scalar
            def _(act):
                for k in range(KC):
                    split_hi(nc, hi[:, k, :], x[:, k, :]).then_inc(hi_ready, 1)

            @block.vector
            def _(dve):
                for k in range(KC):
                    dve.wait_ge(hi_ready, k + 1)
                    split_lo(nc, lo[:, k, :], x[:, k, :], hi[:, k, :])


QH, QD = 32, 16
VH, VD = 16, 32
FLT_MAX = 3.4028234663852886e38
LAMBDA_INIT = 0.8 - 0.6 * 0.7408182206817179


def differential_stage(nc, q, k, v, out, lq1, lk1, lq2, lk2, ident):
    DB = 4
    NB = QD // DB
    POOL_BLOCKS = (1, 3)
    with ExitStack() as ctx:
        s = Space(nc, ctx, "df")
        prod = s.sb("prod", [P, NB, DB, QH, QH])
        vprod = s.sb("vprod", [P, VH, VH, VD])
        pos, sc = s.sb("pos", [P, QH, QH]), s.sb("sc", [P, QH, QH])
        e = s.sb("e", [P, QH, QH])
        mx, den, inv = s.sb("mx", [P, QH]), s.sb("den", [P, QH]), s.sb("inv", [P, QH])
        att, att2 = s.sb("att", [P, VH, VH]), s.sb("att2", [P, VH, VH])
        lam_in = s.sb("lam_in", [P, 4, QD])
        lam_prod, lam_sum, lam_exp, lam = s.sb("lam_prod", [P, 2, QD]), s.sb("lam_sum", [P, 2]), s.sb("lam_exp", [P, 2]), s.sb("lam", [P, 1])
        sq = s.sb("sq", [P, 2, D])
        ms, r0, r1, r2 = (s.sb(n, [P, TILES * VH]) for n in ("ms", "r0", "r1", "r2"))
        S = s.ps("S", [P, 2, 2, 512])
        (lam_loaded, lam_summed, lam_exp_ready, chain, prod_pool, prod_dve, summed, clamped, shifted, exp_done, out_ready, squared,
         sq_summed, ms_ready, root_ready, att_ready, vprod_pool) = (s.sem(n) for n in (
             "lam_loaded", "lam_summed", "lam_exp_ready", "chain", "prod_pool", "prod_dve", "summed", "clamped", "shifted",
             "exp_done", "out_ready", "squared", "sq_summed", "ms_ready", "root_ready", "att_ready", "vprod_pool"))

        def multiply(eng, t, n):
            cols = slice(n * DB * QH, (n + 1) * DB * QH)
            a = q[:, t, cols].rearrange("p (d i) -> p d i", d=DB)[:, :, :, None].to_broadcast([P, DB, QH, QH])
            b = k[:, t, cols].rearrange("p (d j) -> p d j", d=DB)[:, :, None, :].to_broadcast([P, DB, QH, QH])
            return eng.tensor_tensor(prod[:, n], a, b, ALU.mult)

        def weigh(eng, t, half):
            hs = slice(half * VH // 2, (half + 1) * VH // 2)
            a = att[:, :, hs].rearrange("p a h -> p h a")[:, :, :, None].to_broadcast([P, VH // 2, VH, VD])
            b = v[:, t, :].rearrange("p (h d) -> p h d", h=VH)[:, hs, None, :].to_broadcast([P, VH // 2, VH, VD])
            return eng.tensor_tensor(vprod[:, hs], a, b, ALU.mult)

        with nc.Block() as block:

            @block.sync
            def _(sp):
                for i, vec in enumerate((lq1, lk1, lq2, lk2)):
                    sp.dma_start(lam_in[:, i, :], rows_of(vec, P)).then_inc(lam_loaded, 16)

            @block.gpsimd
            def _(pool):
                def products(t):
                    for n in POOL_BLOCKS:
                        if t:
                            pool.wait_ge(summed, NB * (t - 1) + n + 1)
                        multiply(nc.gpsimd, t, n).then_inc(prod_pool, 1)

                products(0)
                products(1)
                for t in range(TILES):
                    pool.wait_ge(att_ready, t + 1)
                    if t:
                        pool.wait_ge(out_ready, t)
                    weigh(nc.gpsimd, t, 1).then_inc(vprod_pool, 1)
                    if t + 2 < TILES:
                        products(t + 2)

            @block.tensor
            def _(pe):
                for t in range(TILES):
                    if t >= 2:
                        pe.wait_ge(clamped, t - 1)
                    for n in range(NB):
                        if n in POOL_BLOCKS:
                            pe.wait_ge(prod_pool, len(POOL_BLOCKS) * t + POOL_BLOCKS.index(n) + 1)
                        else:
                            pe.wait_ge(prod_dve, (NB - len(POOL_BLOCKS)) * t + n // 2 + 1)
                        for d in range(DB):
                            for h in range(2):
                                last = pe.matmul(S[:, t % 2, h, :], ident[:], prod[:, n, d, h * 16:(h + 1) * 16, :],
                                                 start=(n == 0 and d == 0), stop=(n == NB - 1 and d == DB - 1))
                        last.then_inc(summed, 1)

            @block.scalar
            def _(act):
                def square(t):
                    act.wait_ge(out_ready, t + 1)
                    if t >= 2:
                        act.wait_ge(sq_summed, t - 1)
                    nc.scalar.activation(sq[:, t % 2, :], out[:, t, :], ACT.Square).then_inc(squared, 1)

                act.wait_ge(lam_summed, 1)
                nc.scalar.activation(lam_exp[:], lam_sum[:], ACT.Exp).then_inc(lam_exp_ready, 1)
                for t in range(TILES):
                    act.wait_ge(shifted, t + 1)
                    nc.scalar.activation(e[:], sc[:], ACT.Exp).then_inc(exp_done, 1)
                    if t:
                        square(t - 1)
                square(TILES - 1)
                act.wait_ge(ms_ready, 1)
                nc.scalar.activation(r0[:], ms[:], ACT.Sqrt).then_inc(root_ready, 1)

            @block.vector
            def _(dve):
                step = [0]

                def link(ins):
                    step[0] += 1
                    ins.then_inc(chain, 1)
                    dve.wait_ge(chain, step[0])

                def products(t):
                    for n in range(NB):
                        if n not in POOL_BLOCKS:
                            if t:
                                dve.wait_ge(summed, NB * (t - 1) + n + 1)
                            multiply(nc.vector, t, n).then_inc(prod_dve, 1)

                def sum_squares(t):
                    dve.wait_ge(squared, t + 1)
                    nc.vector.reduce_sum(ms[:, t * VH:(t + 1) * VH], sq[:, t % 2, :].rearrange("p (a d) -> p a d", a=VH), AX.X).then_inc(sq_summed, 1)

                dve.wait_ge(lam_loaded, 64)
                link(nc.vector.tensor_tensor(lam_prod[:], lam_in[:].rearrange("p (a b) d -> p a b d", b=2)[:, :, 0, :],
                                             lam_in[:].rearrange("p (a b) d -> p a b d", b=2)[:, :, 1, :], ALU.mult))
                nc.vector.reduce_sum(lam_sum[:], lam_prod[:], AX.X).then_inc(lam_summed, 1)
                products(0)
                dve.wait_ge(lam_exp_ready, 1)
                link(nc.vector.tensor_tensor(lam[:], lam_exp[:, 0:1], lam_exp[:, 1:2], ALU.subtract))
                link(nc.vector.tensor_scalar(lam[:], lam[:], LAMBDA_INIT, None, ALU.add))

                def front(t):
                    dve.wait_ge(summed, NB * t + NB)
                    flat = S[:, t % 2].rearrange("p h (i j) -> p (h i) j", j=QH)
                    link(nc.vector.tensor_scalar(pos[:], flat, 0.0, FLT_MAX, ALU.max, ALU.min))
                    if t:
                        dve.wait_ge(exp_done, t)
                    nc.vector.scalar_tensor_tensor(out=sc[:], in0=flat, scalar=0.0, in1=pos[:], op0=ALU.min, op1=ALU.add).then_inc(clamped, 1)
                    dve.wait_ge(clamped, t + 1)
                    link(nc.vector.tensor_reduce(mx[:], sc[:], AX.X, ALU.max))
                    link(nc.vector.tensor_scalar(mx[:], mx[:], -FLT_MAX, None, ALU.max))
                    nc.vector.scalar_tensor_tensor(out=sc[:], in0=sc[:], scalar=-FLT_MAX, in1=mx[:][:, :, None].to_broadcast([P, QH, QH]),
                                                   op0=ALU.max, op1=ALU.subtract).then_inc(shifted, 1)

                def weights(t):
                    dve.wait_ge(exp_done, t + 1)
                    link(nc.vector.reduce_sum(den[:], e[:], AX.X))
                    link(nc.vector.reciprocal(inv[:], den[:]))
                    link(nc.vector.tensor_scalar(inv[:, VH:QH], inv[:, VH:QH], lam[:, 0:1], None, ALU.mult))
                    link(nc.vector.tensor_tensor(att[:], e[:, 0:VH, 0:VH], inv[:, 0:VH][:, :, None].to_broadcast([P, VH, VH]), ALU.mult))
                    link(nc.vector.tensor_tensor(att2[:], e[:, VH:QH, VH:QH], inv[:, VH:QH][:, :, None].to_broadcast([P, VH, VH]), ALU.mult))
                    nc.vector.tensor_tensor(att[:], att[:], att2[:], ALU.subtract).then_inc(att_ready, 1)

                def add_up(t):
                    dve.wait_ge(vprod_pool, t + 1)
                    for n in (8, 4, 2):
                        link(nc.vector.tensor_tensor(vprod[:, 0:n], vprod[:, 0:n], vprod[:, n:2 * n], ALU.add))
                    nc.vector.tensor_tensor(out[:, t, :].rearrange("p (a d) -> p a d", a=VH), vprod[:, 0], vprod[:, 1], ALU.add).then_inc(out_ready, 1)

                products(1)
                front(0)
                for t in range(TILES):
                    weights(t)
                    dve.wait_ge(att_ready, t + 1)
                    link(weigh(nc.vector, t, 0))
                    if t + 2 < TILES:
                        products(t + 2)
                    if t + 1 < TILES:
                        front(t + 1)
                    add_up(t)
                    dve.wait_ge(out_ready, t + 1)
                    if t:
                        sum_squares(t - 1)
                sum_squares(TILES - 1)
                dve.wait_ge(sq_summed, TILES)
                nc.vector.tensor_scalar(ms[:], ms[:], 1.0 / VD, EPS, ALU.mult, ALU.add).then_inc(ms_ready, 1)
                dve.wait_ge(root_ready, 1)
                link(nc.vector.reciprocal(r1[:], r0[:]))
                link(nc.vector.tensor_tensor(r0[:], r1[:], r1[:], ALU.mult))
                link(nc.vector.tensor_tensor(r2[:], r0[:], ms[:], ALU.mult))
                link(nc.vector.tensor_scalar(r2[:], r2[:], -0.5 * (1.0 - LAMBDA_INIT), 1.5 * (1.0 - LAMBDA_INIT), ALU.mult, ALU.add))
                link(nc.vector.tensor_tensor(r0[:], r1[:], r2[:], ALU.mult))
                for t in range(TILES):
                    o = out[:, t, :].rearrange("p (a d) -> p a d", a=VH)
                    nc.vector.tensor_tensor(o, o, r0[:, t * VH:(t + 1) * VH][:, :, None].to_broadcast([P, VH, VD]), ALU.mult)


def turn_stage(nc, stage, x, hi, lo, ident):
    with ExitStack() as ctx:
        s = Space(nc, ctx, stage)
        T = s.ps("T", [P, 4, 512])
        turned, hi_ready, lo_ready = s.sem("turned"), s.sem("hi_ready"), s.sem("lo_ready")
        with nc.Block() as block:

            @block.tensor
            def _(pe):
                for t in range(TILES):
                    if t >= 4:
                        pe.wait_ge(lo_ready, t - 3)
                    for k in range(KC):
                        last = pe.transpose(T[:, t % 4, k * P:(k + 1) * P], x[:, t, k * P:(k + 1) * P], ident[:])
                    last.then_inc(turned, 1)

            @block.scalar
            def _(act):
                for t in range(TILES):
                    act.wait_ge(turned, t + 1)
                    split_hi(nc, hi[:, :, t * P:(t + 1) * P], T[:, t % 4, :].rearrange("p (k c) -> p k c", k=KC)).then_inc(hi_ready, 1)

            @block.vector
            def _(dve):
                for t in range(TILES):
                    dve.wait_ge(hi_ready, t + 1)
                    split_lo(nc, lo[:, :, t * P:(t + 1) * P], T[:, t % 4, :].rearrange("p (k c) -> p k c", k=KC),
                             hi[:, :, t * P:(t + 1) * P]).then_inc(lo_ready, 1)


def relu_mlp_stage(nc, x_sb, x_old, a_hi, a_lo, W1, b1, W2, b2):
    FF = W1.shape[1]
    N = FF // HID
    UNITS = HALVES * HC
    w1_slices = W1.rearrange("(k p) (n h) -> n p k h", p=P, h=HID)
    w2_slices = W2.rearrange("(n c p) d -> n p c d", p=P, c=HC)
    with ExitStack() as ctx:
        s = Space(nc, ctx, "ml")
        raw1, raw2 = s.sb("raw1", [P, KC, HID]), s.sb("raw2", [P, HC, D])
        w1_hi, w1_lo = s.sb("w1_hi", [P, KC, HID], F32R), s.sb("w1_lo", [P, KC, HID], F32R)
        w2_hi, w2_lo = s.sb("w2_hi", [P, HC, D], F32R), s.sb("w2_lo", [P, HC, D], F32R)
        b1_sb, b1_now, b2_sb = s.sb("b1", [P, N * HC]), s.sb("b1_now", [P, HC]), s.sb("b2", [P, D])
        h32 = s.sb("h32", [P, 2, HALF])
        h_hi, h_lo = s.sb("h_hi", [P, HC, TOKENS], F32R), s.sb("h_lo", [P, HC, TOKENS], F32R)
        H, O = s.ps("H", [P, 2, 512]), s.ps("O", [P, 4, 512])
        (small_loaded, w1_loaded, w2_loaded, w1_hi_ready, w1_lo_ready, w2_hi_ready, w2_lo_ready, b1_ready, h_produced, h32_ready,
         h_hi_ready, h_lo_ready, o_produced, added, biased) = (s.sem(n) for n in (
             "small_loaded", "w1_loaded", "w2_loaded", "w1_hi_ready", "w1_lo_ready", "w2_hi_ready", "w2_lo_ready", "b1_ready",
             "h_produced", "h32_ready", "h_hi_ready", "h_lo_ready", "o_produced", "added", "biased"))

        def hidden(buf, u):
            return buf[:, u % HC, (u // HC) * HALF:(u // HC + 1) * HALF]

        with nc.Block() as block:

            @block.sync
            def _(sp):
                with nc.allow_non_contiguous_dma(reason="2048 values, once"):
                    sp.dma_start(b1_sb[:], b1.rearrange("(c p) -> p c", p=P)).then_inc(small_loaded, 16)
                sp.dma_start(b2_sb[:], rows_of(b2, P)).then_inc(small_loaded, 16)
                def load(n):
                    wait_after(sp, w1_lo_ready, n)
                    sp.dma_start(raw1[:], w1_slices[n]).then_inc(w1_loaded, 16)
                    wait_after(sp, w2_lo_ready, n)
                    sp.dma_start(raw2[:], w2_slices[n]).then_inc(w2_loaded, 16)

                load(0)
                with sp.Fori(1, N) as n:
                    load(n)

            @block.gpsimd
            def _(pool):
                pool.wait_ge(small_loaded, 32)
                for t in range(TILES):
                    nc.gpsimd.tensor_tensor(x_sb[:, t, :], x_sb[:, t, :], x_old[:, t, :], ALU.add).then_inc(biased, 1)
                    pool.wait_ge(biased, 2 * t + 1)
                    nc.gpsimd.tensor_tensor(x_sb[:, t, :], x_sb[:, t, :], b2_sb[:], ALU.add).then_inc(biased, 1)

            @block.scalar
            def _(act):
                def split1(n):
                    act.wait_ge(w1_loaded, 16 * n + 16)
                    wait_after(act, h_produced, UNITS * n)
                    split_hi(nc, w1_hi[:], raw1[:]).then_inc(w1_hi_ready, 1)

                def mlp_slice(n, more):
                    act.wait_ge(w2_loaded, 16 * n + 16)
                    wait_after(act, o_produced, TILES * n)
                    split_hi(nc, w2_hi[:], raw2[:]).then_inc(w2_hi_ready, 1)
                    act.wait_ge(b1_ready, n + 1)
                    for u in range(UNITS):
                        act.wait_ge(h_produced, UNITS * n + u + 1)
                        wait_after(act, h_lo_ready, UNITS * n + max(u - 1, 0))
                        nc.scalar.activation(h32[:, u % 2, :], H[:, u % 2, :], ACT.Relu, bias=b1_now[:, u % HC:u % HC + 1]).then_inc(h32_ready, 1)
                        act.wait_ge(h32_ready, UNITS * n + u + 1)
                        split_hi(nc, hidden(h_hi, u), h32[:, u % 2, :]).then_inc(h_hi_ready, 1)
                    if more:
                        split1(n + 1)

                split1(0)
                mlp_slice(0, True)
                with act.Fori(1, N - 1) as n:
                    mlp_slice(n, True)
                mlp_slice(N - 1, False)

            @block.vector
            def _(dve):
                def split1(n):
                    dve.wait_ge(w1_hi_ready, n + 1)
                    split_lo(nc, w1_lo[:], raw1[:], w1_hi[:]).then_inc(w1_lo_ready, 1)

                def mlp_slice(n, more):
                    wait_after(dve, h32_ready, UNITS * n)
                    nc.vector.tensor_copy(b1_now[:], b1_sb[:, bass.ds(n * HC, HC)]).then_inc(b1_ready, 1)
                    dve.wait_ge(w2_hi_ready, n + 1)
                    split_lo(nc, w2_lo[:], raw2[:], w2_hi[:]).then_inc(w2_lo_ready, 1)
                    for u in range(UNITS):
                        dve.wait_ge(h_hi_ready, UNITS * n + u + 1)
                        split_lo(nc, hidden(h_lo, u), h32[:, u % 2, :], hidden(h_hi, u)).then_inc(h_lo_ready, 1)
                    if more:
                        split1(n + 1)
                    for t in range(TILES):
                        dve.wait_ge(o_produced, TILES * n + t + 1)
                        nc.vector.tensor_tensor(x_sb[:, t, :], O[:, t % 4, :], x_sb[:, t, :], ALU.add).then_inc(added, 1)

                split1(0)
                dve.wait_ge(small_loaded, 32)
                dve.wait_ge(biased, 2 * TILES)
                mlp_slice(0, True)
                with dve.Fori(1, N - 1) as n:
                    mlp_slice(n, True)
                mlp_slice(N - 1, False)

            @block.tensor
            def _(pe):
                def mlp_slice(n):
                    pe.wait_ge(w1_lo_ready, n + 1)
                    for u in range(UNITS):
                        th, m = u // HC, u % HC
                        wait_after(pe, h32_ready, UNITS * n + max(u - 1, 0))
                        for k in range(KC):
                            last = product(pe, H[:, u % 2, :], w1_hi[:, k, m * P:(m + 1) * P], w1_lo[:, k, m * P:(m + 1) * P],
                                           a_hi[:, k, th * HALF:(th + 1) * HALF], a_lo[:, k, th * HALF:(th + 1) * HALF],
                                           k == 0, k == KC - 1)
                        last.then_inc(h_produced, 1)
                    pe.wait_ge(w2_lo_ready, n + 1)
                    for t in range(TILES):
                        pe.wait_ge(h_lo_ready, UNITS * n + (t // 4) * HC + HC)
                        wait_after(pe, added, TILES * n + max(t - 3, 0))
                        for m in range(HC):
                            last = product(pe, O[:, t % 4, :], h_hi[:, m, t * P:(t + 1) * P], h_lo[:, m, t * P:(t + 1) * P],
                                           w2_hi[:, m, :], w2_lo[:, m, :], m == 0, m == HC - 1)
                        last.then_inc(o_produced, 1)

                mlp_slice(0)
                with pe.Fori(1, N) as n:
                    mlp_slice(n)


def copy_stage(nc, stage, dst, src):
    with nc.Block() as block:

        @block.vector
        def _(dve):
            for t in range(TILES):
                nc.vector.tensor_copy(dst[:, t, :], src[:, t, :])


def differential_layer(nc, x_sb, ident, Wq, Wk, Wv, lq1, lq2, lk1, lk2, Wo, bo, g1, be1, g2, be2, W1, b1, W2, b2):
    with ExitStack() as ctx:
        s = Space(nc, ctx, "diff")
        x_old = s.sb("x_old", [P, TILES, D])
        copy_stage(nc, "cp", x_old, x_sb)
        norm_stage(nc, "n6", x_old, x_sb, ident)
        with ExitStack() as mid:
            i = Space(nc, mid, "diffq")
            q, k, v = i.sb("q", [P, TILES, D]), i.sb("k", [P, TILES, D]), i.sb("v", [P, TILES, D])
            with ExitStack() as inner:
                a = Space(nc, inner, "diffa")
                a_hi, a_lo = a.sb("a_hi", [P, KC, TOKENS], F32R), a.sb("a_lo", [P, KC, TOKENS], F32R)
                with ExitStack() as inner2:
                    b = Space(nc, inner2, "diffx")
                    xn, y = b.sb("xn", [P, TILES, D]), b.sb("y", [P, TILES, D])
                    norm_stage(nc, "n4", x_sb, xn, ident, gamma=g1, beta=be1, y=y, hi=a_hi, lo=a_lo)
                project_stage(nc, "pj4", a_hi, a_lo, [(TOKENWISE, Wq, None, QD**-0.5, q), (TOKENWISE, Wk, None, 1.0, k),
                                                     (TOKENWISE, Wv, None, 1.0, v)])
            differential_stage(nc, q, k, v, q, lq1, lk1, lq2, lk2, ident)
            with ExitStack() as inner:
                a = Space(nc, inner, "diffo")
                o_hi, o_lo = a.sb("o_hi", [P, KC, TOKENS], F32R), a.sb("o_lo", [P, KC, TOKENS], F32R)
                turn_stage(nc, "tu0", q, o_hi, o_lo, ident)
                project_stage(nc, "pj5", o_hi, o_lo, [(RESIDUAL, Wo, bo, 1.0, x_sb)])
        a_hi, a_lo = s.sb("a_hi", [P, KC, TOKENS], F32R), s.sb("a_lo", [P, KC, TOKENS], F32R)
        with ExitStack() as inner:
            i = Space(nc, inner, "diffy")
            xn, y = i.sb("xn", [P, TILES, D]), i.sb("y", [P, TILES, D])
            norm_stage(nc, "n5", x_sb, xn, ident, gamma=g2, beta=be2, y=y, hi=a_hi, lo=a_lo)
        relu_mlp_stage(nc, x_sb, x_old, a_hi, a_lo, W1, b1, W2, b2)


LEAST = 1e-5


def spread_rows(nc, pe, diag_ready, ones, diag, out):
    pe.wait_ge(*diag_ready)
    return pe.matmul(out, ones, diag, start=True, stop=True)


CH = 2048


def load_weight(sp, raw, wT, loaded):
    src = wT.rearrange("(k p) n -> p k n", p=P)
    n = src.shape[2]
    dst = raw.rearrange("p (k n) -> p k n", n=n)
    step = CH // n
    for c, sem in enumerate(loaded):
        sp.dma_start(dst[:, c * step:(c + 1) * step, :], src[:, c * step:(c + 1) * step, :]).then_inc(sem, 16)


def quantise_stage(nc, xn, ident, raw1, raw2, w1_loaded, w2_loaded, w1q, xqT, dq1_row, mean_w2, scale_w2):
    loaded = w1_loaded + w2_loaded
    NCH = len(loaded)
    COUNT = P * (NCH // 2) * CH
    with ExitStack() as ctx:
        s = Space(nc, ctx, "qs")
        absum, mean, scale = s.sb("absum", [P, 2]), s.sb("mean", [P, 2]), s.sb("scale", [P, 2])
        ones = s.sb("ones", [P, P])
        junk = s.sb("junk", [P, 2, CH])
        part = s.sb("part", [P, NCH])
        amax, ax, sx, dq = (s.sb(n, [P, TILES]) for n in ("amax", "ax", "sx", "dq"))
        xs = s.sb("xs", [P, 2, D])
        xq = s.sb("xq", [P, 2, D], BF16)
        ident16 = s.sb("ident16", [P, P], BF16)
        diag = s.sb("diag", [P, TILES, P])
        M = s.ps("M", [P, 512])
        R = s.ps("R", [P, 2, 512])
        X = s.ps("X", [P, 2, 1024], BF16)
        (ones_ready, summed_abs, absum_ready, mean_made, scale_ready, shifted, chain, amax_done, xs_ready, xq_ready,
         x_turned, x_kept, diag_ready, row_made) = (s.sem(n) for n in (
             "ones_ready", "summed_abs", "absum_ready", "mean_made", "scale_ready", "shifted", "chain", "amax_done",
             "xs_ready", "xq_ready", "x_turned", "x_kept", "diag_ready", "row_made"))
        w1q_flat = w1q[:].rearrange("p k n -> p (k n)")

        def piece(c):
            raw, i = (raw1, c) if c < NCH // 2 else (raw2, c - NCH // 2)
            return raw[:, i * CH:(i + 1) * CH]

        with nc.Block() as block:

            @block.gpsimd
            def _(pool):
                nc.gpsimd.memset(ones[:], 1.0).then_inc(ones_ready, 1)

            @block.scalar
            def _(act):
                for c in range(NCH):
                    act.wait_ge(loaded[c], 16)
                    if c >= 2:
                        act.wait_ge(summed_abs, c - 1)
                    nc.scalar.activation(junk[:, c % 2, :], piece(c), ACT.Abs, accum_out=part[:, c:c + 1]).then_inc(summed_abs, 1)
                for t in range(TILES):
                    act.wait_ge(x_turned, t + 1)
                    nc.scalar.activation(xqT[:, :, t * P:(t + 1) * P], X[:, t % 2, 0:D].rearrange("p (k c) -> p k c", k=KC), ACT.Copy)\
                        .then_inc(x_kept, 1)
                for c in range(NCH // 2):
                    act.wait_ge(shifted, c + 1)
                    nc.scalar.activation(w1q_flat[:, c * CH:(c + 1) * CH], piece(c), ACT.Copy, bias=-ROUND)
                for h in range(HALVES):
                    act.wait_ge(row_made, h + 1)
                    nc.scalar.activation(dq1_row[:, h * HALF:(h + 1) * HALF], R[:, h, :], ACT.Copy)

            @block.vector
            def _(dve):
                step = [0]

                def link(ins):
                    step[0] += 1
                    ins.then_inc(chain, 1)
                    dve.wait_ge(chain, step[0])

                link(nc.vector.tensor_copy(ident16[:], ident[:]))
                for t in range(TILES):
                    last = nc.vector.tensor_reduce(amax[:, t:t + 1], xn[:, t, :], AX.X, ALU.max, apply_absolute_value=True)
                link(last)
                link(nc.vector.tensor_scalar(ax[:], amax[:], LEAST, None, ALU.max))
                link(nc.vector.reciprocal(sx[:], ax[:]))
                link(nc.vector.tensor_scalar(sx[:], sx[:], 127.0, None, ALU.mult))
                for t in range(TILES):
                    if t >= 2:
                        dve.wait_ge(x_turned, t - 1)
                    link(nc.vector.tensor_scalar(xs[:, t % 2, :], xn[:, t, :], sx[:, t:t + 1], ROUND, ALU.mult, ALU.add))
                    link(nc.vector.tensor_scalar(xs[:, t % 2, :], xs[:, t % 2, :], ROUND + 127.0, ROUND - 128.0, ALU.min, ALU.max))
                    nc.vector.tensor_scalar(xq[:, t % 2, :], xs[:, t % 2, :], -ROUND, None, ALU.add).then_inc(xq_ready, 1)
                dve.wait_ge(summed_abs, NCH)
                nc.vector.reduce_sum(absum[:], part[:].rearrange("p (w c) -> p w c", w=2), AX.X).then_inc(absum_ready, 1)
                dve.wait_ge(mean_made, 1)
                link(nc.vector.tensor_scalar(mean[:], M[:, 0:2], 1.0 / COUNT, LEAST, ALU.mult, ALU.max))
                link(nc.vector.reciprocal(scale[:], mean[:]))
                nc.vector.tensor_copy(mean_w2[:], mean[:, 1:2])
                nc.vector.tensor_copy(scale_w2[:], scale[:, 1:2])
                link(nc.vector.tensor_scalar(dq[:], ax[:], mean[:, 0:1], 1.0 / 127.0, ALU.mult, ALU.mult))
                for t in range(TILES):
                    nc.vector.tensor_scalar(diag[:, t, :], ident[:], dq[:, t:t + 1], None, ALU.mult).then_inc(diag_ready, 1)
                for c in range(NCH // 2):
                    link(nc.vector.tensor_scalar(piece(c), piece(c), scale[:, 0:1], ROUND, ALU.mult, ALU.add))
                    nc.vector.tensor_scalar(piece(c), piece(c), ROUND + 1.0, ROUND - 1.0, ALU.min, ALU.max).then_inc(shifted, 1)

            @block.tensor
            def _(pe):
                for t in range(TILES):
                    pe.wait_ge(xq_ready, t + 1)
                    if t >= 2:
                        pe.wait_ge(x_kept, t - 1)
                    for k in range(KC):
                        last = pe.transpose(X[:, t % 2, k * P:(k + 1) * P], xq[:, t % 2, k * P:(k + 1) * P], ident16[:])
                    last.then_inc(x_turned, 1)
                pe.wait_ge(ones_ready, 1)
                pe.wait_ge(absum_ready, 1)
                pe.matmul(M[:, 0:2], ones[:], absum[:], start=True, stop=True).then_inc(mean_made, 1)
                for t in range(TILES):
                    last = spread_rows(nc, pe, (diag_ready, t + 1), ones[:], diag[:, t, :], R[:, t // 4, (t % 4) * P:(t % 4 + 1) * P])
                    if t % 4 == 3:
                        last.then_inc(row_made, 1)


def hidden_stage(nc, xqT, w1q, dq1_row, conv_w, conv_b, hs, mx, raw2, scale_w2, w2q):
    FCH = hs.shape[1]
    with ExitStack() as ctx:
        s = Space(nc, ctx, "hd")
        cw, cb = s.sb("cw", [P, FCH, 3]), s.sb("cb", [P, FCH])
        h = s.sb("h", [P, 2, TOKENS])
        y = s.sb("y", [P, 2, TOKENS])
        size = s.sb("size", [P, 2, TOKENS])
        H = s.ps("H", [P, 2, 2, 512])
        (conv_loaded, produced, h_ready, y_ready, left_done, right_done, hs_ready, mx_done, size_ready, w2_steps) = (s.sem(n) for n in (
            "conv_loaded", "produced", "h_ready", "y_ready", "left_done", "right_done", "hs_ready", "mx_done", "size_ready", "w2_steps"))

        def by_batch(ap):
            return ap.rearrange("p (b s) -> p b s", s=SEQ)

        with nc.Block() as block:

            @block.sync
            def _(sp):
                with nc.allow_non_contiguous_dma(reason="four values for each hidden unit, once"):
                    sp.dma_start(cw[:], conv_w.rearrange("(c p) a w -> p c (a w)", p=P)).then_inc(conv_loaded, 16)
                    sp.dma_start(cb[:], conv_b.rearrange("(c p) -> p c", p=P)).then_inc(conv_loaded, 16)

            @block.gpsimd
            def _(pool):
                w2q_flat = w2q[:].rearrange("p k n -> p (k n)")
                for c in range(w2q_flat.shape[1] // CH):
                    piece = raw2[:, c * CH:(c + 1) * CH]
                    nc.gpsimd.tensor_scalar(piece, piece, scale_w2[:, 0:1], ROUND, ALU.mult, ALU.add).then_inc(w2_steps, 1)
                    pool.wait_ge(w2_steps, 2 * c + 1)
                    nc.gpsimd.tensor_scalar(piece, piece, ROUND + 1.0, ROUND - 1.0, ALU.min, ALU.max).then_inc(w2_steps, 1)
                    pool.wait_ge(w2_steps, 2 * c + 2)
                    nc.gpsimd.tensor_scalar(w2q_flat[:, c * CH:(c + 1) * CH], piece, -ROUND, None, ALU.add)

            @block.tensor
            def _(pe):
                for c in range(FCH):
                    if c >= 2:
                        pe.wait_ge(h_ready, c - 1)
                    for th in range(HALVES):
                        for k in range(KC):
                            last = pe.matmul(H[:, c % 2, th, :], w1q[:, k, c * P:(c + 1) * P], xqT[:, k, th * HALF:(th + 1) * HALF],
                                             start=(k == 0), stop=(k == KC - 1))
                    last.then_inc(produced, 1)

            @block.vector
            def _(dve):
                def scale(c):
                    dve.wait_ge(produced, c + 1)
                    if c >= 2:
                        dve.wait_ge(right_done, c - 1)
                    nc.vector.tensor_tensor(h[:, c % 2, :], H[:, c % 2].rearrange("p h n -> p (h n)"), dq1_row[:], ALU.mult).then_inc(h_ready, 1)

                def largest(c):
                    dve.wait_ge(size_ready, c + 1)
                    dve.wait_ge(mx_done, c + 1)
                    nc.vector.tensor_tensor(mx[:], size[:, c % 2, :], mx[:], ALU.max).then_inc(mx_done, 1)

                nc.vector.memset(mx[:], 0.0).then_inc(mx_done, 1)
                dve.wait_ge(conv_loaded, 32)
                scale(0)
                for c in range(FCH):
                    if c + 1 < FCH:
                        scale(c + 1)
                    dve.wait_ge(y_ready, c + 1)
                    yb, hb = by_batch(y[:, c % 2, :]), by_batch(h[:, c % 2, :])
                    nc.vector.scalar_tensor_tensor(out=yb[:, :, 1:SEQ], in0=hb[:, :, 0:SEQ - 1], scalar=cw[:, c, 0:1], in1=yb[:, :, 1:SEQ],
                                                   op0=ALU.mult, op1=ALU.add).then_inc(left_done, 1)
                    dve.wait_ge(left_done, c + 1)
                    nc.vector.scalar_tensor_tensor(out=yb[:, :, 0:SEQ - 1], in0=hb[:, :, 1:SEQ], scalar=cw[:, c, 2:3], in1=yb[:, :, 0:SEQ - 1],
                                                   op0=ALU.mult, op1=ALU.add).then_inc(right_done, 1)
                    if c:
                        largest(c - 1)
                largest(FCH - 1)

            @block.scalar
            def _(act):
                act.wait_ge(conv_loaded, 32)

                def middle(c):
                    act.wait_ge(h_ready, c + 1)
                    if c >= 2:
                        act.wait_ge(hs_ready, c - 1)
                    nc.scalar.activation(y[:, c % 2, :], h[:, c % 2, :], ACT.Identity, bias=cb[:, c:c + 1], scale=cw[:, c, 1:2]).then_inc(y_ready, 1)

                middle(0)
                for c in range(FCH):
                    if c + 1 < FCH:
                        middle(c + 1)
                    act.wait_ge(right_done, c + 1)
                    nc.scalar.activation(hs[:, c, :], y[:, c % 2, :], ACT.Silu).then_inc(hs_ready, 1)
                    act.wait_ge(hs_ready, c + 1)
                    if c >= 2:
                        act.wait_ge(mx_done, c)
                    nc.scalar.activation(size[:, c % 2, :], hs[:, c, :], ACT.Abs).then_inc(size_ready, 1)


def token_scale_stage(nc, mx, ident, mean_w2, s2_row, dq2):
    with ExitStack() as ctx:
        s = Space(nc, ctx, "ts")
        ones, diag = s.sb("ones", [P, P]), s.sb("diag", [P, TILES, P])
        amax, ax, sx = (s.sb(n, [P, TILES]) for n in ("amax", "ax", "sx"))
        T, R = s.ps("T", [P, 2, 512]), s.ps("R", [P, 2, 512])
        turned, chain, ones_ready, diag_ready, row_made = (s.sem(n) for n in ("turned", "chain", "ones_ready", "diag_ready", "row_made"))
        with nc.Block() as block:

            @block.gpsimd
            def _(pool):
                nc.gpsimd.memset(ones[:], 1.0).then_inc(ones_ready, 1)

            @block.tensor
            def _(pe):
                for t in range(TILES):
                    last = pe.transpose(T[:, t // 4, (t % 4) * P:(t % 4 + 1) * P], mx[:, t * P:(t + 1) * P], ident[:])
                last.then_inc(turned, 1)
                pe.wait_ge(ones_ready, 1)
                for t in range(TILES):
                    last = spread_rows(nc, pe, (diag_ready, t + 1), ones[:], diag[:, t, :], R[:, t // 4, (t % 4) * P:(t % 4 + 1) * P])
                    if t % 4 == 3:
                        last.then_inc(row_made, 1)

            @block.vector
            def _(dve):
                step = [0]

                def link(ins):
                    step[0] += 1
                    ins.then_inc(chain, 1)
                    dve.wait_ge(chain, step[0])

                dve.wait_ge(turned, 1)
                link(nc.vector.tensor_reduce(amax[:], T[:].rearrange("p h (t c) -> p (h t) c", c=P), AX.X, ALU.max))
                link(nc.vector.tensor_scalar(ax[:], amax[:], LEAST, None, ALU.max))
                link(nc.vector.reciprocal(sx[:], ax[:]))
                link(nc.vector.tensor_scalar(sx[:], sx[:], 127.0, None, ALU.mult))
                for t in range(TILES):
                    nc.vector.tensor_scalar(diag[:, t, :], ident[:], sx[:, t:t + 1], None, ALU.mult).then_inc(diag_ready, 1)
                nc.vector.tensor_scalar(dq2[:], ax[:], mean_w2[:, 0:1], 1.0 / 127.0, ALU.mult, ALU.mult)
                for h in range(HALVES):
                    dve.wait_ge(row_made, h + 1)
                    nc.vector.tensor_copy(s2_row[:, h * HALF:(h + 1) * HALF], R[:, h, :])


def ternary_out_stage(nc, x_sb, hs, s2_row, w2q, dq2):
    FCH = hs.shape[1]
    POOL_CHUNKS = [c for c in range(FCH) if c % 3 == 2]
    with ExitStack() as ctx:
        s = Space(nc, ctx, "to")
        hq = s.sb("hq", [P, 2, TOKENS], BF16)
        O = s.ps("O", [P, TILES, 512])
        by_pool, by_dve, rounded, clipped, hq_ready, used = (s.sem(n) for n in ("by_pool", "by_dve", "rounded", "clipped", "hq_ready", "used"))
        with nc.Block() as block:

            @block.gpsimd
            def _(pool):
                for c in POOL_CHUNKS:
                    nc.gpsimd.tensor_tensor(hs[:, c, :], hs[:, c, :], s2_row[:], ALU.mult).then_inc(by_pool, 1)

            @block.vector
            def _(dve):
                def scale(c):
                    if c not in POOL_CHUNKS:
                        nc.vector.tensor_tensor(hs[:, c, :], hs[:, c, :], s2_row[:], ALU.mult).then_inc(by_dve, 1)

                scale(0)
                for c in range(FCH):
                    if c + 1 < FCH:
                        scale(c + 1)
                    dve.wait_ge(rounded, c + 1)
                    nc.vector.tensor_scalar(hs[:, c, :], hs[:, c, :], ROUND + 127.0, ROUND - 128.0, ALU.min, ALU.max).then_inc(clipped, 1)
                for t in range(TILES):
                    dve.wait_ge(used, FCH * TILES - TILES + t + 1)
                    nc.vector.scalar_tensor_tensor(out=x_sb[:, t, :], in0=O[:, t, :], scalar=dq2[:, t:t + 1], in1=x_sb[:, t, :],
                                                   op0=ALU.mult, op1=ALU.add)

            @block.scalar
            def _(act):
                def rounding(c):
                    if c in POOL_CHUNKS:
                        act.wait_ge(by_pool, POOL_CHUNKS.index(c) + 1)
                    else:
                        act.wait_ge(by_dve, sum(i not in POOL_CHUNKS for i in range(c + 1)))
                    nc.scalar.activation(hs[:, c, :], hs[:, c, :], ACT.Copy, bias=ROUND).then_inc(rounded, 1)

                rounding(0)
                for c in range(FCH):
                    if c + 1 < FCH:
                        rounding(c + 1)
                    act.wait_ge(clipped, c + 1)
                    if c >= 2:
                        act.wait_ge(used, TILES * (c - 1))
                    nc.scalar.activation(hq[:, c % 2, :], hs[:, c, :], ACT.Copy, bias=-ROUND).then_inc(hq_ready, 1)

            @block.tensor
            def _(pe):
                for c in range(FCH):
                    pe.wait_ge(hq_ready, c + 1)
                    for t in range(TILES):
                        pe.matmul(O[:, t, :], hq[:, c % 2, t * P:(t + 1) * P], w2q[:, c, :], start=(c == 0), stop=(c == FCH - 1)).then_inc(used, 1)


def ternary_layer(nc, x_sb, ident, w1T, conv_w, conv_b, w2T):
    FCH = w1T.shape[1] // P
    with ExitStack() as ctx:
        s = Space(nc, ctx, "tern")
        w1q, w2q = s.sb("w1q", [P, KC, w1T.shape[1]], BF16), s.sb("w2q", [P, FCH, D], BF16)
        mean_w2, scale_w2, dq2 = s.sb("mean_w2", [P, 1]), s.sb("scale_w2", [P, 1]), s.sb("dq2", [P, TILES])
        xqT = s.sb("xqT", [P, KC, TOKENS], BF16)
        row, mx = s.sb("row", [P, TOKENS]), s.sb("mx", [P, TOKENS])
        raw2 = s.sb("raw2", [P, FCH * D])
        w1_loaded = [s.sem(f"w1_loaded{c}") for c in range(FCH * D // CH)]
        w2_loaded = [s.sem(f"w2_loaded{c}") for c in range(FCH * D // CH)]
        with ExitStack() as inner:
            i = Space(nc, inner, "ternx")
            raw1, xn = i.sb("raw1", [P, FCH * D]), i.sb("xn", [P, TILES, D])

            def load_weights(sp):
                load_weight(sp, raw1[:], w1T, w1_loaded)
                load_weight(sp, raw2[:], w2T, w2_loaded)

            norm_stage(nc, "n7", x_sb, xn, ident, prefetch=load_weights)
            quantise_stage(nc, xn, ident, raw1, raw2, w1_loaded, w2_loaded, w1q, xqT, row, mean_w2, scale_w2)
        hs = s.sb("hs", [P, FCH, TOKENS])
        hidden_stage(nc, xqT, w1q, row, conv_w, conv_b, hs, mx, raw2, scale_w2, w2q)
        token_scale_stage(nc, mx, ident, mean_w2, row, dq2)
        ternary_out_stage(nc, x_sb, hs, row, w2q, dq2)


def start_stage(nc, x_sb, ident, x):
    with ExitStack() as ctx:
        s = Space(nc, ctx, "start")
        x_loaded, ident_ready = s.sem("x_loaded"), s.sem("ident_ready")
        with nc.Block() as block:

            @block.sync
            def _(sp):
                sp.dma_start(x_sb[:], x.rearrange("(t a) s d -> (a s) t d", a=2)).then_inc(x_loaded, 16)
                sp.wait_ge(x_loaded, 16)

            @block.gpsimd
            def _(pool):
                nc.gpsimd.memset(ident[:], 0.0).then_inc(ident_ready, 1)
                pool.wait_ge(ident_ready, 1)
                nc.gpsimd.affine_select(out=ident[:], in_=ident[:], compare_op=ALU.not_equal, fill=1.0, base=0,
                                        pattern=[[-1, P]], channel_multiplier=1).then_inc(ident_ready, 1)


def end_stage(nc, x_sb, out):
    with ExitStack() as ctx:
        stored = Space(nc, ctx, "end").sem("stored")
        with nc.Block() as block:

            @block.sync
            def _(sp):
                sp.dma_start(out.rearrange("(t a) s d -> (a s) t d", a=2), x_sb[:]).then_inc(stored, 16)
                sp.wait_ge(stored, 16)


def clear_stage(nc):
    free = nc.free_semaphores
    numbers = range(min(free), max(free) + 1)
    assert len(free) == len(numbers)
    with nc.Block() as block:

        @block.gpsimd
        def _(pool):
            pool.sem_clear(numbers)


def perceiver(nc, a, out):
    with ExitStack() as ctx:
        s = Space(nc, ctx, "main")
        x_sb = s.sb("x", [P, TILES, D])
        ident = s.sb("ident", [P, P])

        def of(layer, *names):
            return [a[f"{layer}_{n}"] for n in names]

        start_stage(nc, x_sb, ident, a["x"])
        bidaf_layer(nc, x_sb, ident, a["ctx"], a["ctx_cols"], *of("L0_xattn", "w_sim", "b_sim", "W_qv", "b_qv"))
        causal_layer(nc, x_sb, ident, *of("L0_attn", "Wq", "bq", "Wk", "bk", "Wv", "bv", "Wo", "bo"))
        experts_layer(nc, x_sb, ident, *of("L0_ffn", "router_w", "router_b"), of("L0_ffn", "routed_w1", "routed_w3", "routed_w2"),
                      of("L0_ffn", "shared_w1", "shared_w3", "shared_w2"))
        clear_stage(nc)
        cross_layer(nc, x_sb, ident, a["ctx_cols"], a["mask"], *of("L1_xattn", "Wq", "bq", "Wk", "bk", "Wv", "bv", "Wo", "bo"))
        clear_stage(nc)
        differential_layer(nc, x_sb, ident, *of("L1_attn", "Wq", "Wk", "Wv", "lq1", "lq2", "lk1", "lk2", "Wo", "bo",
                                                "ln1_g", "ln1_b", "ln2_g", "ln2_b", "W1", "b1", "W2", "b2"))
        clear_stage(nc)
        ternary_layer(nc, x_sb, ident, *of("L1_ffn", "w1", "conv_w", "conv_b", "w2"))
        end_stage(nc, x_sb, out)




def kernel(**inputs):
    import numpy as np
    import concourse.bacc as bacc
    from concourse.bass_utils import run_bass_kernel_spmd as run

    arrays = {}
    for name in inputs:
        if name[:3] in ("L0_", "L1_") or name == "x":
            arrays[name] = np.asarray(inputs[name])
    arrays["ctx"] = np.asarray(inputs["ctx_1024"])
    arrays["ctx_cols"] = arrays["ctx"].transpose(0, 2, 1)
    arrays["mask"] = np.asarray(inputs["mask_Bx1xSxS2_bk1"])
    for name in ("L1_attn_Wv", "L1_attn_Wo", "L1_attn_W1", "L1_attn_W2", "L1_ffn_w1", "L1_ffn_w2"):
        arrays[name] = arrays[name].T
    for name in ("L1_attn_Wq", "L1_attn_Wk"):
        arrays[name] = arrays[name].T.reshape(D, 16, 16, 2).transpose(0, 2, 3, 1).reshape(D, D)

    nc = bacc.Bacc("TRN2", target_bir_lowering=False, num_devices=1)
    feed, aps = {}, {}
    for name, array in arrays.items():
        array = np.ascontiguousarray(array)
        feed[f"in_{name}"] = array
        aps[name] = nc.dram_tensor(f"in_{name}", array.shape, mybir.dt.from_np(array.dtype), kind="ExternalInput").ap()
    out = nc.dram_tensor("out_x", (BATCH, SEQ, D), F32, kind="ExternalOutput").ap()
    perceiver(nc, aps, out)
    return run(nc, [feed], core_ids=[0]).results[0]["out_x"]
```

```python
from contextlib import ExitStack

import concourse.bass as bass
from concourse import mybir

ALU = mybir.AluOpType
ACT = mybir.ActivationFunctionType
AX = mybir.AxisListType
F32 = mybir.dt.float32
F32R = mybir.dt.float32r
BF16 = mybir.dt.bfloat16
U8 = mybir.dt.uint8
U32 = mybir.dt.uint32

P = 128
D = 512
KC = D // P
BATCH, SEQ, KEYS = 16, 64, 1601
TOKENS = BATCH * SEQ
TILES = TOKENS // P
HALF = 512
HALVES = TOKENS // HALF
EPS = 1e-5
ROUND = 1.5 * 2.0**23


class Space:

    def __init__(self, nc, ctx, stage):
        self.nc, self.ctx, self.stage = nc, ctx, stage

    def sb(self, name, shape, dt=F32):
        return self.ctx.enter_context(self.nc.sbuf_tensor(f"{self.stage}_{name}", shape, dt))

    def ps(self, name, shape, dt=F32):
        return self.ctx.enter_context(self.nc.psum_tensor(f"{self.stage}_{name}", shape, dt))

    def sem(self, name):
        return self.ctx.enter_context(self.nc.semaphore(f"{self.stage}_{name}"))


def wait_after(engine, semaphore, count):
    if not isinstance(count, int) or count > 0:
        engine.wait_ge(semaphore, count)


def product(pe, out, w_hi, w_lo, x_hi, x_lo, first, last):
    pe.matmul(out, w_hi, x_hi, start=first, stop=False)
    pe.matmul(out, w_hi, x_lo, start=False, stop=False)
    return pe.matmul(out, w_lo, x_hi, start=False, stop=last)


def rows_of(ap, n):
    return ap.rearrange("(a d) -> a d", a=1).to_broadcast([n, ap.shape[0]])


def split_hi(nc, hi, x):
    return nc.scalar.activation(hi, x, ACT.Copy)


def split_lo(nc, lo, x, hi):
    return nc.vector.tensor_tensor(lo, x, hi.bitcast(F32), ALU.subtract)


def norm_stage(nc, stage, x_sb, xn, ident, gamma=None, beta=None, y=None, yT=None, hi=None, lo=None,
               prefetch=None):
    with ExitStack() as ctx:
        s = Space(nc, ctx, stage)
        stats = s.sb("stats", [P, TILES, 6])
        mv = s.sb("mv", [P, TILES, 2])
        table = s.sb("table", [P, 1])
        ve = s.sb("ve", [P, TILES])
        sd = s.sb("sd", [P, TILES])
        r0 = s.sb("r0", [P, TILES])
        r1 = s.sb("r1", [P, TILES])
        r2 = s.sb("r2", [P, TILES])
        rstd = s.sb("rstd", [P, TILES])
        g_sb = s.sb("gamma", [P, D]) if gamma is not None else None
        b_sb = s.sb("beta", [P, D]) if beta is not None else None
        turned = s.ps("turned", [P, 4, D])
        affine_loaded, var_ready, sd_ready = s.sem("affine_loaded"), s.sem("var_ready"), s.sem("sd_ready")
        chain, normed, mid = s.sem("chain"), s.sem("normed"), s.sem("mid")
        turned_ready, hi_ready, lo_ready = s.sem("turned_ready"), s.sem("hi_ready"), s.sem("lo_ready")
        src = y if y is not None else xn
        transposed = yT is not None or hi is not None

        with nc.Block() as block:

            @block.sync
            def _(sp):
                if gamma is not None:
                    sp.dma_start(g_sb[:], rows_of(gamma, P)).then_inc(affine_loaded, 16)
                    sp.dma_start(b_sb[:], rows_of(beta, P)).then_inc(affine_loaded, 16)
                if prefetch is not None:
                    prefetch(sp)

            @block.vector
            def _(dve):
                step = [0]

                def link(ins):
                    step[0] += 1
                    ins.then_inc(chain, 1)
                    dve.wait_ge(chain, step[0])

                for t in range(TILES):
                    last = nc.vector.bn_stats(stats[:, t, :], x_sb[:, t, :])
                link(last)
                for t in range(TILES):
                    last = nc.vector.bn_aggr(mv[:, t, :], stats[:, t, :])
                link(last)
                nc.vector.tensor_scalar(ve[:], mv[:, :, 1], EPS, None, ALU.add).then_inc(var_ready, 1)
                dve.wait_ge(sd_ready, 1)
                link(nc.vector.reciprocal(r0[:], sd[:]))
                link(nc.vector.tensor_tensor(r1[:], r0[:], r0[:], ALU.mult))
                link(nc.vector.tensor_tensor(r2[:], r1[:], ve[:], ALU.mult))
                link(nc.vector.tensor_scalar(r1[:], r2[:], -0.5, 1.5, ALU.mult, ALU.add))
                link(nc.vector.tensor_tensor(rstd[:], r0[:], r1[:], ALU.mult))
                if gamma is not None:
                    dve.wait_ge(affine_loaded, 32)
                for t in range(TILES):
                    ins = nc.vector.tensor_scalar(xn[:, t, :], x_sb[:, t, :], mv[:, t, 0:1], rstd[:, t:t + 1],
                                                  ALU.subtract, ALU.mult)
                    if gamma is None:
                        ins.then_inc(normed, 1)
                        continue
                    ins.then_inc(mid, 1)
                    dve.wait_ge(mid, 2 * t + 1)
                    nc.vector.tensor_tensor(y[:, t, :], xn[:, t, :], g_sb[:], ALU.mult).then_inc(mid, 1)
                    dve.wait_ge(mid, 2 * t + 2)
                    nc.vector.tensor_tensor(y[:, t, :], y[:, t, :], b_sb[:], ALU.add).then_inc(normed, 1)
                if hi is not None:
                    for t in range(TILES):
                        dve.wait_ge(hi_ready, t + 1)
                        split_lo(nc, lo[:, :, t * P:(t + 1) * P], turned[:, t % 4, :].rearrange("p (k c) -> p k c", k=KC),
                                 hi[:, :, t * P:(t + 1) * P]).then_inc(lo_ready, 1)

            @block.scalar
            def _(act):
                nc.scalar.activation(table[:], ident[:, 0:1], ACT.Sqrt)
                act.wait_ge(var_ready, 1)
                nc.scalar.activation(sd[:], ve[:], ACT.Sqrt).then_inc(sd_ready, 1)
                if transposed:
                    for t in range(TILES):
                        act.wait_ge(turned_ready, t + 1)
                        out = yT if yT is not None else hi
                        split_hi(nc, out[:, :, t * P:(t + 1) * P],
                                 turned[:, t % 4, :].rearrange("p (k c) -> p k c", k=KC)).then_inc(hi_ready, 1)

            @block.tensor
            def _(pe):
                if transposed:
                    for t in range(TILES):
                        pe.wait_ge(normed, t + 1)
                        if t >= 4:
                            pe.wait_ge(hi_ready, t - 3)
                            if hi is not None:
                                pe.wait_ge(lo_ready, t - 3)
                        for k in range(KC):
                            last = pe.transpose(turned[:, t % 4, k * P:(k + 1) * P], src[:, t, k * P:(k + 1) * P], ident[:])
                        last.then_inc(turned_ready, 1)


GROUP = 401
GROUPS = 4
GROUP_W = [GROUP] * 3 + [KEYS - 3 * GROUP]
KT = -(-KEYS // P)
TAIL = KEYS - (KT - 1) * P
BUNCH = [(0, 4), (4, 8), (8, 12), (12, 13)]


def rows(n):
    return TAIL if n == KT - 1 else P


def bidaf_scores_stage(nc, hcwT, ident, ctx_rows, ctx_cols, hq, neg_max, hc, w1_sb, w1_loaded, sc, prefetch):
    with ExitStack() as ctx:
        s = Space(nc, ctx, "bs")
        cols0 = s.sb("cols0", [P, GROUPS, KC, GROUP])
        cols1 = s.sb("cols1", [P, KC, KEYS])
        rws = s.sb("rows", [P, 2, KT, D])
        q = s.sb("q", [P, KC, P])
        a = s.sb("a", [P, KEYS])
        aT = s.sb("aT", [P, KT, P])
        mx = s.sb("mx", [P, GROUPS])
        nm = s.sb("nm", [P, 1])
        rs = s.sb("rs", [P, GROUPS])
        rsum = s.sb("rsum", [P, 1])
        rinv = s.sb("rinv", [P, 1])
        hcw1 = s.sb("hcw1", [P, 2, D])
        S = s.ps("S", [P, GROUPS, 512])
        turned = s.ps("turned", [P, 3, 512])
        hqp = s.ps("hqp", [P, 512])
        cols_loaded = [s.sem(f"cols_loaded{g}") for g in range(GROUPS)]
        rows0_loaded = [s.sem(f"rows0_loaded{g}") for g in range(GROUPS)]
        rows1_loaded = [s.sem(f"rows1_loaded{g}") for g in range(GROUPS)]
        q_staged, scored, max_ready, exp_done = s.sem("q_staged"), s.sem("scored"), s.sem("max_ready"), s.sem("exp_done")
        unit_turned, kept_act, kept_dve = s.sem("unit_turned"), s.sem("kept_act"), s.sem("kept_dve")
        summed, hq_stored, chain = s.sem("summed"), s.sem("hq_stored"), s.sem("chain")
        hcw1_ready, hcw1_summed = s.sem("hcw1_ready"), s.sem("hcw1_summed")
        CHAIN = 4

        UNITS = KT + GROUPS
        ACT_UNITS, DVE_UNITS = (UNITS + 1) // 2, UNITS // 2
        REACH = [0] + [-(-min((g + 1) * GROUP, KEYS) // P) for g in range(GROUPS)]

        def bank(u):
            return u % 3

        def wait_kept(engine, t, u):
            if u % 2:
                engine.wait_ge(kept_dve, DVE_UNITS * t + u // 2 + 1)
            else:
                engine.wait_ge(kept_act, ACT_UNITS * t + u // 2 + 1)

        def keep(copy, u):
            if u < KT:
                r = rows(u)
                return copy(cols1[:, :, u * P:u * P + r], turned[:, bank(u), :].rearrange("p (k c) -> p k c", c=P)[:, :, 0:r])
            n0, n1 = BUNCH[u - KT]
            r = rows(n1 - 1)
            return copy(aT[0:r, n0:n1, :], turned[0:r, bank(u), 0:(n1 - n0) * P].rearrange("p (n c) -> p n c", c=P))

        with nc.Block() as block:

            @block.sync
            def _(sp):
                def load_cols(pair, g):
                    w = GROUP_W[g]
                    src = ctx_cols[2 * pair].rearrange("(k p) j -> p k j", p=P)[:, :, g * GROUP:g * GROUP + w]
                    sp.dma_start(cols0[:, g, :, 0:w], src).then_inc(cols_loaded[g], 16)

                def load_rows(pair, b, g):
                    n0, n1 = BUNCH[g]
                    loaded = (rows0_loaded, rows1_loaded)[b][g]
                    if g == GROUPS - 1:
                        sp.dma_start(rws[0:TAIL, b, n0, :], ctx_rows[2 * pair + b][n0 * P:KEYS, :]).then_inc(loaded, 16)
                    else:
                        src = ctx_rows[2 * pair + b][n0 * P:n1 * P, :].rearrange("(n p) d -> p n d", p=P)
                        sp.dma_start(rws[:, b, n0:n1, :], src).then_inc(loaded, 16)

                for g in range(GROUPS):
                    load_rows(0, 1, g)
                    load_cols(0, g)
                for g in range(GROUPS):
                    load_rows(0, 0, g)
                with sp.Fori(0, TILES - 1) as t:
                    for g in range(GROUPS):
                        sp.wait_ge(scored, GROUPS * t + g + 1)
                        load_cols(t + 1, g)
                    for g in range(GROUPS):
                        sp.wait_ge(summed, GROUPS * t + g + 1)
                        load_rows(t + 1, 1, g)
                    for g in range(GROUPS):
                        load_rows(t + 1, 0, g)
                prefetch(sp)

            @block.tensor
            def _(pe):
                def bank_free(t, u):
                    if u >= 3:
                        wait_kept(pe, t, u - 3)
                    elif not (isinstance(t, int) and t == 0):
                        wait_kept(pe, t - 1, max(v for v in range(UNITS) if bank(v) == bank(u)))

                def turn_keys(t, g):
                    for n in range(REACH[g], REACH[g + 1]):
                        bank_free(t, n)
                        r = rows(n)
                        pe.wait_ge(rows1_loaded[n // 4], 16 * t + 16)
                        for k in range(KC):
                            last = pe.transpose(turned[:, bank(n), k * P:k * P + r], rws[0:r, 1, n, k * P:(k + 1) * P], ident[0:r, 0:r])
                        last.then_inc(unit_turned, 1)

                def pair(t):
                    turn_keys(t, 0)
                    for g in range(GROUPS):
                        if g + 1 < GROUPS:
                            turn_keys(t, g + 1)
                        if g == 0:
                            pe.wait_ge(q_staged, t + 1)
                            wait_after(pe, exp_done, GROUPS * t)
                        w = GROUP_W[g]
                        pe.wait_ge(cols_loaded[g], 16 * t + 16)
                        for n in (REACH[g + 1] - 2, REACH[g + 1] - 1):
                            wait_kept(pe, t, n)
                        for k in range(KC):
                            for b in range(2):
                                c = cols1[:, k, g * GROUP:g * GROUP + w] if b else cols0[:, g, k, 0:w]
                                last = pe.matmul(S[64 * b:64 * b + 64, g, 0:w], q[:, k, 64 * b:64 * b + 64], c,
                                                 start=(k == 0), stop=(k == KC - 1))
                        last.then_inc(scored, 1)
                    for g, (n0, n1) in enumerate(BUNCH):
                        pe.wait_ge(exp_done, GROUPS * t + -(-min(n1 * P, KEYS) // GROUP))
                        bank_free(t, KT + g)
                        for n in range(n0, n1):
                            r = rows(n)
                            last = pe.transpose(turned[0:r, bank(KT + g), (n - n0) * P:(n - n0 + 1) * P], a[:, n * P:n * P + r], ident[:])
                        last.then_inc(unit_turned, 1)
                    wait_after(pe, hq_stored, t)
                    for g, (n0, n1) in enumerate(BUNCH):
                        wait_kept(pe, t, KT + g)
                        pe.wait_ge(rows0_loaded[g], 16 * t + 16)
                        for n in range(n0, n1):
                            r = rows(n)
                            for b in range(2):
                                last = pe.matmul(hqp[64 * b:64 * b + 64, :], aT[0:r, n, 64 * b:64 * b + 64],
                                                 rws[0:r, b, n, :], start=(n == 0), stop=(n == KT - 1))
                        last.then_inc(summed, 1)

                pair(0)
                with pe.Fori(1, TILES) as t:
                    pair(t)

            @block.vector
            def _(dve):
                def keep_unit(t, u):
                    dve.wait_ge(unit_turned, UNITS * t + u + 1)
                    keep(nc.vector.tensor_copy, u).then_inc(kept_dve, 1)

                def pair(t):
                    wait_after(dve, scored, GROUPS * t)
                    nc.vector.tensor_copy(q[:], hcwT[:, :, bass.ds(t * P, P)]).then_inc(q_staged, 1)
                    kept = 1
                    for g in range(GROUPS):
                        while kept < (REACH[g + 2] if g + 2 <= GROUPS else KT):
                            keep_unit(t, kept)
                            kept += 2
                        dve.wait_ge(scored, GROUPS * t + g + 1)
                        last = nc.vector.reduce_max(mx[:, g:g + 1], S[:, g, 0:GROUP_W[g]], AX.X)
                    last.then_inc(chain, 1)
                    dve.wait_ge(chain, CHAIN * t + 1)
                    nc.vector.tensor_reduce(nm[:], mx[:], AX.X, ALU.max, negate=True).then_inc(max_ready, 1)
                    dve.wait_ge(max_ready, t + 1)
                    nc.vector.tensor_copy(neg_max[:, bass.ds(t, 1)], nm[:]).then_inc(chain, 1)
                    dve.wait_ge(exp_done, GROUPS * t + GROUPS)
                    nc.vector.reduce_sum(rsum[:], rs[:], AX.X).then_inc(chain, 1)
                    dve.wait_ge(chain, CHAIN * t + 3)
                    nc.vector.reciprocal(rinv[:], rsum[:]).then_inc(chain, 1)
                    for u in range(kept, UNITS, 2):
                        keep_unit(t, u)
                    dve.wait_ge(chain, CHAIN * t + 4)
                    dve.wait_ge(summed, GROUPS * t + GROUPS)
                    nc.vector.tensor_scalar(hq[:, bass.ds(t * D, D)], hqp[:], rinv[:], None, ALU.mult).then_inc(hq_stored, 1)

                dve.wait_ge(w1_loaded, 16)
                for t in range(TILES):
                    if t >= 2:
                        dve.wait_ge(hcw1_summed, t - 1)
                    nc.vector.tensor_tensor(hcw1[:, t % 2, :], hc[:, t, :], w1_sb[:], ALU.mult).then_inc(hcw1_ready, 1)
                    dve.wait_ge(hcw1_ready, t + 1)
                    nc.vector.reduce_sum(sc[:, t:t + 1], hcw1[:, t % 2, :], AX.X).then_inc(hcw1_summed, 1)

                pair(0)
                with dve.Fori(1, TILES) as t:
                    pair(t)

            @block.scalar
            def _(act):
                def keep_unit(t, u):
                    act.wait_ge(unit_turned, UNITS * t + u + 1)
                    keep(lambda o, i: nc.scalar.activation(o, i, ACT.Copy), u).then_inc(kept_act, 1)

                def pair(t):
                    for u in range(0, KT, 2):
                        keep_unit(t, u)
                    act.wait_ge(max_ready, t + 1)
                    for g in range(GROUPS):
                        w = GROUP_W[g]
                        nc.scalar.activation(a[:, g * GROUP:g * GROUP + w], S[:, g, 0:w], ACT.Exp, bias=nm[:, 0:1],
                                             accum_out=rs[:, g:g + 1]).then_inc(exp_done, 1)
                    for u in range(KT + KT % 2, UNITS, 2):
                        keep_unit(t, u)

                pair(0)
                with act.Fori(1, TILES) as t:
                    pair(t)


def load_merge_weight(sp, w_raw, w_loaded, W, c):
    sp.dma_start(w_raw[:, c % 2], W[c * D:(c + 1) * D, :].rearrange("(k p) n -> p k n", p=P)).then_inc(w_loaded[c % 2], 16)


def bidaf_merge_stage(nc, x_sb, hc, hq, neg_max, sc, ident, b_sim, W, bias, w_raw, w_loaded):
    FC = 4 * KC
    with ExitStack() as ctx:
        s = Space(nc, ctx, "bm")
        w_hi, w_lo = s.sb("w_hi", [P, FC, D], F32R), s.sb("w_lo", [P, FC, D], F32R)
        f_hi, f_lo = s.sb("f_hi", [P, 2, FC, P], F32R), s.sb("f_lo", [P, 2, FC, P], F32R)
        hh, hb = s.sb("hh", [P, 2, D]), s.sb("hb", [P, 2, D])
        bias_sb, bsim_sb = s.sb("bias", [P, D]), s.sb("bsim", [P, 1])
        m, batt = s.sb("m", [P, TILES]), s.sb("batt", [P, TILES])
        blocks = s.sb("blocks", [P, P])
        mix = s.sb("mix", [P, 2, P])
        mT, eT = s.sb("mT", [TILES, P]), s.sb("eT", [TILES, P])
        mm, es, er = s.sb("mm", [TILES, 2]), s.sb("es", [TILES, 2]), s.sb("er", [TILES, 2])
        turned = s.ps("turned", [P, 4, 512])
        out = s.ps("out", [P, 2, 512])
        bar = s.ps("bar", [P, 512])
        small = s.ps("small", [P, 512])
        small_loaded = s.sem("small_loaded")
        w_hi_ready, w_lo_ready = s.sem("w_hi_ready"), s.sem("w_lo_ready")
        chain, blocks_ready, biased = s.sem("chain"), s.sem("blocks_ready"), s.sem("biased")
        m_ready, m_turned, max_sub, exp_done, e_ready, batt_turned = (s.sem(n) for n in
            ("m_ready", "m_turned", "max_sub", "exp_done", "e_ready", "batt_turned"))
        mix_ready, bar_ready, feats_ready, f_turned, f_hi_ready, f_lo_ready, out_ready, added = (s.sem(n) for n in
            ("mix_ready", "bar_ready", "feats_ready", "f_turned", "f_hi_ready", "f_lo_ready", "out_ready", "added"))

        with nc.Block() as block:

            @block.sync
            def _(sp):
                sp.dma_start(bsim_sb[:], rows_of(b_sim, P)).then_inc(small_loaded, 16)
                sp.dma_start(bias_sb[:], rows_of(bias, P)).then_inc(small_loaded, 16)
                for c in (2, 3):
                    sp.wait_ge(w_hi_ready, c - 1)
                    sp.wait_ge(w_lo_ready, c - 1)
                    load_merge_weight(sp, w_raw, w_loaded, W, c)

            @block.gpsimd
            def _(pool):
                nc.gpsimd.memset(blocks[:], 0.0).then_inc(blocks_ready, 1)
                pool.wait_ge(blocks_ready, 1)
                nc.gpsimd.memset(blocks[0:64, 0:64], 1.0).then_inc(blocks_ready, 1)
                nc.gpsimd.memset(blocks[64:128, 64:128], 1.0).then_inc(blocks_ready, 1)
                pool.wait_ge(blocks_ready, 3)
                pool.wait_ge(small_loaded, 32)
                for t in range(TILES):
                    nc.gpsimd.tensor_tensor(x_sb[:, t, :], x_sb[:, t, :], bias_sb[:], ALU.add).then_inc(biased, 1)

            @block.vector
            def _(dve):
                step = [0]

                def link(ins):
                    step[0] += 1
                    ins.then_inc(chain, 1)
                    dve.wait_ge(chain, step[0])

                dve.wait_ge(small_loaded, 32)
                link(nc.vector.tensor_tensor(m[:], sc[:], neg_max[:], ALU.subtract))
                nc.vector.tensor_scalar(m[:], m[:], bsim_sb[:, 0:1], None, ALU.add).then_inc(m_ready, 1)
                dve.wait_ge(m_turned, 1)
                link(nc.vector.tensor_copy(mT[:], small[0:TILES, 0:P]))
                link(nc.vector.tensor_reduce(mm[:], mT[:].rearrange("t (b i) -> t b i", b=2), AX.X, ALU.max))
                for b in range(2):
                    last = nc.vector.tensor_scalar(mT[:, 64 * b:64 * b + 64], mT[:, 64 * b:64 * b + 64], mm[:, b:b + 1], None, ALU.subtract)
                    last.then_inc(max_sub, 1)
                dve.wait_ge(exp_done, 1)
                link(nc.vector.reduce_sum(es[:], eT[:].rearrange("t (b i) -> t b i", b=2), AX.X))
                link(nc.vector.reciprocal(er[:], es[:]))
                for b in range(2):
                    nc.vector.tensor_scalar(eT[:, 64 * b:64 * b + 64], eT[:, 64 * b:64 * b + 64], er[:, b:b + 1], None, ALU.mult)\
                        .then_inc(e_ready, 1)
                dve.wait_ge(batt_turned, 1)
                link(nc.vector.tensor_copy(batt[:], small[:, 256:256 + TILES]))
                dve.wait_ge(blocks_ready, 3)

                def lows(t):
                    for c in range(4):
                        dve.wait_ge(f_hi_ready, 4 * t + c + 1)
                        nc.vector.tensor_tensor(f_lo[:, t % 2, 4 * c:4 * c + 4, :], turned[:, c, :].rearrange("p (k c) -> p k c", c=P),
                                                f_hi[:, t % 2, 4 * c:4 * c + 4, :].bitcast(F32), ALU.subtract).then_inc(f_lo_ready, 1)

                def feats(t):
                    if t >= 2:
                        dve.wait_ge(bar_ready, t - 1)
                        dve.wait_ge(f_turned, 4 * t - 4)
                    nc.vector.tensor_scalar(mix[:, t % 2, :], blocks[:], batt[:, t:t + 1], None, ALU.mult).then_inc(mix_ready, 1)
                    nc.vector.tensor_tensor(hh[:, t % 2, :], hc[:, t, :], hq[:, t * D:(t + 1) * D], ALU.mult).then_inc(feats_ready, 1)
                    dve.wait_ge(bar_ready, t + 1)
                    nc.vector.tensor_tensor(hb[:, t % 2, :], hc[:, t, :], bar[:], ALU.mult).then_inc(feats_ready, 1)

                def add(t):
                    dve.wait_ge(out_ready, t + 1)
                    dve.wait_ge(biased, t + 1)
                    nc.vector.tensor_tensor(x_sb[:, t, :], out[:, t % 2, :], x_sb[:, t, :], ALU.add).then_inc(added, 1)

                def w_low(c):
                    dve.wait_ge(w_hi_ready, c + 1)
                    split_lo(nc, w_lo[:, 4 * c:4 * c + 4, :], w_raw[:, c % 2], w_hi[:, 4 * c:4 * c + 4, :]).then_inc(w_lo_ready, 1)

                w_low(0)
                w_low(1)
                feats(0)
                lows(0)
                feats(1)
                w_low(2)
                w_low(3)
                for t in range(TILES):
                    if t + 1 < TILES:
                        if t:
                            feats(t + 1)
                        lows(t + 1)
                    add(t)

            @block.scalar
            def _(act):
                act.wait_ge(max_sub, 2)
                nc.scalar.activation(eT[:], mT[:], ACT.Exp).then_inc(exp_done, 1)
                def w_high(c):
                    act.wait_ge(w_loaded[c % 2], 16 * (c // 2) + 16)
                    split_hi(nc, w_hi[:, 4 * c:4 * c + 4, :], w_raw[:, c % 2]).then_inc(w_hi_ready, 1)

                w_high(0)
                w_high(1)
                for t in range(TILES):
                    if t >= 2:
                        act.wait_ge(out_ready, t - 1)
                    for c in range(4):
                        act.wait_ge(f_turned, 4 * t + c + 1)
                        split_hi(nc, f_hi[:, t % 2, 4 * c:4 * c + 4, :], turned[:, c, :].rearrange("p (k c) -> p k c", c=P))\
                            .then_inc(f_hi_ready, 1)
                    if t == 0:
                        w_high(2)
                        w_high(3)

            @block.tensor
            def _(pe):
                pe.wait_ge(m_ready, 1)
                pe.transpose(small[0:TILES, 0:P], m[:], ident[:]).then_inc(m_turned, 1)
                pe.wait_ge(e_ready, 2)
                pe.transpose(small[:, 256:256 + TILES], eT[:], ident[0:TILES, 0:TILES]).then_inc(batt_turned, 1)

                def mixing(t):
                    pe.wait_ge(mix_ready, t + 1)
                    if t >= 1:
                        pe.wait_ge(feats_ready, 2 * t)
                    pe.matmul(bar[:], mix[:, t % 2, :], hc[:, t, :], start=True, stop=True).then_inc(bar_ready, 1)

                def turn(t):
                    for c in range(4):
                        if c == 2:
                            pe.wait_ge(feats_ready, 2 * t + 1)
                        if c == 3:
                            pe.wait_ge(feats_ready, 2 * t + 2)
                        if t:
                            pe.wait_ge(f_hi_ready, 4 * (t - 1) + c + 1)
                            pe.wait_ge(f_lo_ready, 4 * (t - 1) + c + 1)
                        src = (hc[:, t, :], hq[:, t * D:(t + 1) * D], hh[:, t % 2, :], hb[:, t % 2, :])[c]
                        for k in range(KC):
                            last = pe.transpose(turned[:, c, k * P:(k + 1) * P], src[:, k * P:(k + 1) * P], ident[:])
                        last.then_inc(f_turned, 1)

                mixing(0)
                turn(0)
                for t in range(TILES):
                    if t + 1 < TILES:
                        mixing(t + 1)
                        turn(t + 1)
                    if t >= 2:
                        pe.wait_ge(added, t - 1)
                    for f in range(FC):
                        if f % 4 == 0:
                            if t == 0:
                                pe.wait_ge(w_lo_ready, f // 4 + 1)
                            pe.wait_ge(f_lo_ready, 4 * t + f // 4 + 1)
                        last = product(pe, out[:, t % 2, :], f_hi[:, t % 2, f, :], f_lo[:, t % 2, f, :],
                                       w_hi[:, f, :], w_lo[:, f, :], f == 0, f == FC - 1)
                    last.then_inc(out_ready, 1)


def bidaf_layer(nc, x_sb, ident, ctx_rows, ctx_cols, w_sim, b_sim, W, bias):
    with ExitStack() as ctx:
        s = Space(nc, ctx, "bidaf")
        hc = s.sb("hc", [P, TILES, D])
        hq = s.sb("hq", [P, TILES * D])
        neg_max, sc = s.sb("neg_max", [P, TILES]), s.sb("sc", [P, TILES])
        w_raw, w_loaded = s.sb("w_raw", [P, 2, KC, D]), [s.sem("w_loaded0"), s.sem("w_loaded1")]

        def load_first(sp):
            for c in range(2):
                load_merge_weight(sp, w_raw, w_loaded, W, c)

        with ExitStack() as inner:
            i = Space(nc, inner, "bidafq")
            hcwT, w1_sb, w1_loaded = i.sb("hcwT", [P, KC, TOKENS]), i.sb("w1", [P, D]), i.sem("w1_loaded")

            def load_w1(sp):
                sp.dma_start(w1_sb[:], rows_of(w_sim[0:D], P)).then_inc(w1_loaded, 16)

            with ExitStack() as inner2:
                hcw = Space(nc, inner2, "bidafw").sb("hcw", [P, TILES, D])
                norm_stage(nc, "n0", x_sb, hc, ident, gamma=w_sim[2 * D:3 * D], beta=w_sim[D:2 * D], y=hcw, yT=hcwT, prefetch=load_w1)
            bidaf_scores_stage(nc, hcwT, ident, ctx_rows, ctx_cols, hq, neg_max, hc, w1_sb, w1_loaded, sc, load_first)
        bidaf_merge_stage(nc, x_sb, hc, hq, neg_max, sc, ident, b_sim, W, bias, w_raw, w_loaded)


FEATURES, TOKENWISE, RESIDUAL = range(3)


def project_stage(nc, stage, a_hi, a_lo, jobs, prefetch=None, source=None):
    N = len(jobs)
    UNITS = 8
    with ExitStack() as ctx:
        s = Space(nc, ctx, stage)
        raw = s.sb("raw", [P, 2, KC, D])
        w_hi, w_lo = s.sb("w_hi", [P, 2, KC, D], F32R), s.sb("w_lo", [P, 2, KC, D], F32R)
        bias_col = s.sb("bias_col", [P, N, KC])
        bias_scaled = s.sb("bias_scaled", [P, N, KC])
        bias_row = s.sb("bias_row", [P, N, D])
        out_ps = s.ps("out", [P, 4, 512])
        w_loaded = [s.sem("w_loaded0"), s.sem("w_loaded1")]
        first_loaded = [s.sem(f"first_loaded{k}") for k in range(KC)]
        bias_loaded, bias_ready = s.sem("bias_loaded"), s.sem("bias_ready")
        a_hi_ready, a_lo_ready = s.sem("a_hi_ready"), s.sem("a_lo_ready")
        w_hi_ready, w_lo_ready = s.sem("w_hi_ready"), s.sem("w_lo_ready")
        produced, stored_act, stored_dve = s.sem("produced"), s.sem("stored_act"), s.sem("stored_dve")
        n_bias = sum(b is not None for _, _, b, _, _ in jobs)
        biased = [j[2] is not None for j in jobs]

        def stored_before(j):
            act = UNITS * sum(jobs[i][0] == FEATURES for i in range(j))
            return act, UNITS * j - act

        with nc.Block() as block:

            @block.sync
            def _(sp):
                for k in range(KC):
                    sp.dma_start(raw[:, 0, k, :], jobs[0][1][k * P:(k + 1) * P, :]).then_inc(first_loaded[k], 16)
                for j, (kind, W, bias, scale, out) in enumerate(jobs):
                    if bias is not None:
                        if kind == FEATURES:
                            with nc.allow_non_contiguous_dma(reason="512 values, once"):
                                sp.dma_start(bias_col[:, j, :], bias.rearrange("(k p) -> p k", p=P)).then_inc(bias_loaded, 16)
                        else:
                            sp.dma_start(bias_row[:, j, :], rows_of(bias, P)).then_inc(bias_loaded, 16)
                    if j >= 2:
                        sp.wait_ge(w_hi_ready, KC + j - 2)
                        sp.wait_ge(w_lo_ready, KC + j - 2)
                    if j:
                        sp.dma_start(raw[:, j % 2, :, :], W.rearrange("(k p) n -> p k n", p=P)).then_inc(w_loaded[j % 2], 16)
                if prefetch is not None:
                    prefetch(sp)

            @block.scalar
            def _(act):
                def take(j):
                    act.wait_ge(w_loaded[j % 2], 16 * ((j - 1) // 2) + 16)
                    if j >= 2:
                        act.wait_ge(produced, UNITS * (j - 1))
                    split_hi(nc, w_hi[:, j % 2, :, :], raw[:, j % 2, :, :]).then_inc(w_hi_ready, 1)

                if source is not None:
                    for k in range(KC):
                        split_hi(nc, a_hi[:, k, :], source[:, k, :]).then_inc(a_hi_ready, 1)
                for k in range(KC):
                    act.wait_ge(first_loaded[k], 16)
                    split_hi(nc, w_hi[:, 0, k, :], raw[:, 0, k, :]).then_inc(w_hi_ready, 1)
                for j, (kind, W, bias, scale, out) in enumerate(jobs):
                    if j + 1 < N:
                        take(j + 1)
                    if kind == FEATURES:
                        if n_bias:
                            act.wait_ge(bias_ready, 1)
                        for u in range(UNITS):
                            act.wait_ge(produced, UNITS * j + u + 1)
                            m, h = u // HALVES, u % HALVES
                            nc.scalar.activation(out[:, m, h * HALF:(h + 1) * HALF], out_ps[:, u % 4, :], ACT.Identity,
                                                 bias=bias_scaled[:, j, m:m + 1] if biased[j] else 0.0,
                                                 scale=scale).then_inc(stored_act, 1)

            @block.vector
            def _(dve):
                if source is not None:
                    for k in range(KC):
                        dve.wait_ge(a_hi_ready, k + 1)
                        split_lo(nc, a_lo[:, k, :], source[:, k, :], a_hi[:, k, :]).then_inc(a_lo_ready, 1)
                for k in range(KC):
                    dve.wait_ge(w_hi_ready, k + 1)
                    split_lo(nc, w_lo[:, 0, k, :], raw[:, 0, k, :], w_hi[:, 0, k, :]).then_inc(w_lo_ready, 1)
                if n_bias:
                    dve.wait_ge(bias_loaded, 16 * n_bias)
                    for j, (kind, W, bias, scale, out) in enumerate(jobs):
                        if kind == FEATURES and biased[j]:
                            last = nc.vector.tensor_scalar(bias_scaled[:, j, :], bias_col[:, j, :], scale, None, ALU.mult)
                            last_is = last
                    if any(k == FEATURES and b is not None for k, _, b, _, _ in jobs):
                        last_is.then_inc(bias_ready, 1)

                def take(j):
                    dve.wait_ge(w_hi_ready, KC + j)
                    split_lo(nc, w_lo[:, j % 2, :, :], raw[:, j % 2, :, :], w_hi[:, j % 2, :, :]).then_inc(w_lo_ready, 1)

                for j, (kind, W, bias, scale, out) in enumerate(jobs):
                    if j + 1 < N:
                        take(j + 1)
                    if kind == FEATURES:
                        continue
                    for u in range(UNITS):
                        dve.wait_ge(produced, UNITS * j + u + 1)
                        if kind == TOKENWISE and not biased[j]:
                            nc.vector.tensor_scalar(out[:, u, :], out_ps[:, u % 4, :], scale, None, ALU.mult).then_inc(stored_dve, 1)
                        elif kind == TOKENWISE:
                            nc.vector.tensor_tensor(out[:, u, :], out_ps[:, u % 4, :], bias_row[:, j, :], ALU.add).then_inc(stored_dve, 1)
                        else:
                            dve.wait_ge(bias_ready, u + 1)
                            nc.vector.tensor_tensor(out[:, u, :], out_ps[:, u % 4, :], out[:, u, :], ALU.add).then_inc(stored_dve, 1)

            @block.gpsimd
            def _(pool):
                for j, (kind, W, bias, scale, out) in enumerate(jobs):
                    if kind == RESIDUAL:
                        pool.wait_ge(bias_loaded, 16 * n_bias)
                        for u in range(TILES):
                            nc.gpsimd.tensor_tensor(out[:, u, :], out[:, u, :], bias_row[:, j, :], ALU.add).then_inc(bias_ready, 1)

            @block.tensor
            def _(pe):
                for j, (kind, W, bias, scale, out) in enumerate(jobs):
                    if j:
                        pe.wait_ge(w_lo_ready, KC + j)
                    for u in range(UNITS):
                        if UNITS * j + u >= 4:
                            v = UNITS * j + u - 4
                            by_act, by_dve = stored_before(v // UNITS)
                            if jobs[v // UNITS][0] == FEATURES:
                                pe.wait_ge(stored_act, by_act + v % UNITS + 1)
                            else:
                                pe.wait_ge(stored_dve, by_dve + v % UNITS + 1)
                        for k in range(KC):
                            if j == 0 and u == 0:
                                if source is not None:
                                    pe.wait_ge(a_lo_ready, k + 1)
                                pe.wait_ge(w_lo_ready, k + 1)
                            if kind == FEATURES:
                                m, h = u // HALVES, u % HALVES
                                ws = slice(m * P, (m + 1) * P)
                                xs = slice(h * HALF, (h + 1) * HALF)
                                last = product(pe, out_ps[:, u % 4, :], w_hi[:, j % 2, k, ws], w_lo[:, j % 2, k, ws],
                                               a_hi[:, k, xs], a_lo[:, k, xs], k == 0, k == KC - 1)
                            else:
                                xs = slice(u * P, (u + 1) * P)
                                last = product(pe, out_ps[:, u % 4, :], a_hi[:, k, xs], a_lo[:, k, xs],
                                               w_hi[:, j % 2, k, :], w_lo[:, j % 2, k, :], k == 0, k == KC - 1)
                        last.then_inc(produced, 1)


def causal_attention_stage(nc, qT, kT, v, ident, c_hi, c_lo):
    NEVER = -1e30
    with ExitStack() as ctx:
        s = Space(nc, ctx, "ca")
        causal = s.sb("causal", [P, P])
        sc = s.sb("sc", [P, 2, P])
        pr = s.sb("pr", [P, 2, P])
        pT = s.sb("pT", [P, 2, P])
        nm, rs, ri = s.sb("nm", [P, TILES]), s.sb("rs", [P, TILES]), s.sb("ri", [P, TILES])
        S = s.ps("S", [P, 2, 512])
        T = s.ps("T", [P, 2, 512])
        C = s.ps("C", [P, 2, 512])
        (mask_steps, scored, masked, max_ready, exp_done, inv_ready, scaled, turned, pT_ready, summed, hi_ready,
         lo_ready) = (s.sem(n) for n in ("mask_steps", "scored", "masked", "max_ready", "exp_done", "inv_ready", "scaled",
                                         "turned", "pT_ready", "summed", "hi_ready", "lo_ready"))
        with nc.Block() as block:

            @block.gpsimd
            def _(pool):
                nc.gpsimd.memset(causal[:], 0.0).then_inc(mask_steps, 1)
                pool.wait_ge(mask_steps, 1)
                nc.gpsimd.affine_select(out=causal[:], in_=causal[:], compare_op=ALU.is_ge, fill=NEVER, base=0,
                                        pattern=[[-1, P]], channel_multiplier=1).then_inc(mask_steps, 1)
                pool.wait_ge(mask_steps, 2)
                nc.gpsimd.memset(causal[SEQ:P, 0:SEQ], NEVER).then_inc(mask_steps, 1)

            @block.tensor
            def _(pe):
                def scores(t):
                    if t >= 2:
                        pe.wait_ge(masked, t - 1)
                    for k in range(KC):
                        last = pe.matmul(S[:, t % 2, 0:P], qT[:, k, t * P:(t + 1) * P], kT[:, k, t * P:(t + 1) * P],
                                         start=(k == 0), stop=(k == KC - 1))
                    last.then_inc(scored, 1)

                scores(0)
                for t in range(TILES):
                    if t + 1 < TILES:
                        scores(t + 1)
                    pe.wait_ge(scaled, t + 1)
                    if t >= 2:
                        pe.wait_ge(pT_ready, t - 1)
                    pe.transpose(T[:, t % 2, 0:P], pr[:, t % 2, :], ident[:]).then_inc(turned, 1)
                    pe.wait_ge(pT_ready, t + 1)
                    if t >= 2:
                        pe.wait_ge(hi_ready, t - 1)
                        pe.wait_ge(lo_ready, t - 1)
                    for m in range(KC):
                        last = pe.matmul(C[:, t % 2, m * P:(m + 1) * P], v[:, t, m * P:(m + 1) * P], pT[:, t % 2, :],
                                         start=True, stop=True)
                    last.then_inc(summed, 1)

            @block.vector
            def _(dve):
                dve.wait_ge(mask_steps, 3)

                def front(t):
                    dve.wait_ge(scored, t + 1)
                    if t >= 2:
                        dve.wait_ge(exp_done, t - 1)
                    nc.vector.tensor_tensor(sc[:, t % 2, :], S[:, t % 2, 0:P], causal[:], ALU.add).then_inc(masked, 1)
                    dve.wait_ge(masked, t + 1)
                    nc.vector.tensor_reduce(nm[:, t:t + 1], sc[:, t % 2, :], AX.X, ALU.max, negate=True).then_inc(max_ready, 1)

                def back(t):
                    dve.wait_ge(exp_done, t + 1)
                    nc.vector.reciprocal(ri[:, t:t + 1], rs[:, t:t + 1]).then_inc(inv_ready, 1)
                    dve.wait_ge(inv_ready, t + 1)
                    nc.vector.tensor_scalar(pr[:, t % 2, :], pr[:, t % 2, :], ri[:, t:t + 1], None, ALU.mult).then_inc(scaled, 1)
                    dve.wait_ge(turned, t + 1)
                    if t >= 2:
                        dve.wait_ge(summed, t - 1)
                    nc.vector.tensor_copy(pT[:, t % 2, :], T[:, t % 2, 0:P]).then_inc(pT_ready, 1)
                    dve.wait_ge(hi_ready, t + 1)
                    split_lo(nc, c_lo[:, :, t * P:(t + 1) * P], C[:, t % 2, :].rearrange("p (k c) -> p k c", c=P),
                             c_hi[:, :, t * P:(t + 1) * P]).then_inc(lo_ready, 1)

                front(0)
                for t in range(TILES):
                    if t + 1 < TILES:
                        front(t + 1)
                    back(t)

            @block.scalar
            def _(act):
                def front(t):
                    act.wait_ge(max_ready, t + 1)
                    if t >= 2:
                        act.wait_ge(turned, t - 1)
                    nc.scalar.activation(pr[:, t % 2, :], sc[:, t % 2, :], ACT.Exp, bias=nm[:, t:t + 1],
                                         accum_out=rs[:, t:t + 1]).then_inc(exp_done, 1)

                front(0)
                for t in range(TILES):
                    if t + 1 < TILES:
                        front(t + 1)
                    act.wait_ge(summed, t + 1)
                    split_hi(nc, c_hi[:, :, t * P:(t + 1) * P], C[:, t % 2, :].rearrange("p (k c) -> p k c", c=P)).then_inc(hi_ready, 1)


def causal_layer(nc, x_sb, ident, Wq, bq, Wk, bk, Wv, bv, Wo, bo):
    with ExitStack() as ctx:
        s = Space(nc, ctx, "attn0")
        a_hi, a_lo = s.sb("a_hi", [P, KC, TOKENS], F32R), s.sb("a_lo", [P, KC, TOKENS], F32R)
        with ExitStack() as inner:
            xn = Space(nc, inner, "attn0x").sb("xn", [P, TILES, D])
            norm_stage(nc, "n1", x_sb, xn, ident, hi=a_hi, lo=a_lo)
        with ExitStack() as inner:
            i = Space(nc, inner, "attn0i")
            qT, kT, v = i.sb("qT", [P, KC, TOKENS]), i.sb("kT", [P, KC, TOKENS]), i.sb("v", [P, TILES, D])
            project_stage(nc, "pj0", a_hi, a_lo, [(FEATURES, Wq, bq, D**-0.5, qT), (FEATURES, Wk, bk, 1.0, kT),
                                                 (TOKENWISE, Wv, bv, 1.0, v)])
            causal_attention_stage(nc, qT, kT, v, ident, a_hi, a_lo)
        project_stage(nc, "pj1", a_hi, a_lo, [(RESIDUAL, Wo, bo, 1.0, x_sb)])


EXPERTS, SHARED, HID = 8, 2, 256
HC = HID // P


def router_stage(nc, a_hi, a_lo, ident, raw, b_sb, w_loaded, gates):
    with ExitStack() as ctx:
        s = Space(nc, ctx, "rt")
        w_hi, w_lo = s.sb("w_hi", [P, KC, P], F32R), s.sb("w_lo", [P, KC, P], F32R)
        lT = s.sb("lT", [EXPERTS, TOKENS])
        lg = s.sb("lg", [P, TILES, EXPERTS])
        top = s.sb("top", [P, TILES, 8])
        at = s.sb("at", [P, TILES, 8], U32)
        at_f = s.sb("at_f", [P, TILES, 8])
        diff, e1, den, g0, g1 = (s.sb(n, [P, TILES]) for n in ("diff", "e1", "den", "g0", "g1"))
        number = s.sb("number", [P, EXPERTS])
        first, second = s.sb("first", [P, TILES, EXPERTS]), s.sb("second", [P, TILES, EXPERTS])
        L = s.ps("L", [P, HALVES, 512])
        T = s.ps("T", [P, 512])
        (cleared, w_hi_ready, w_lo_ready, l_ready, lT_ready, turned, chain, diff_ready, e1_ready, number_ready) = (
            s.sem(n) for n in ("cleared", "w_hi_ready", "w_lo_ready", "l_ready", "lT_ready", "turned", "chain",
                               "diff_ready", "e1_ready", "number_ready"))
        with nc.Block() as block:

            @block.gpsimd
            def _(pool):
                nc.gpsimd.iota(number[:], [[1, EXPERTS]], base=0, channel_multiplier=0,
                               allow_small_or_imprecise_dtypes=True).then_inc(number_ready, 1)

            @block.scalar
            def _(act):
                act.wait_ge(w_loaded, 32)
                act.wait_ge(cleared, 2)
                split_hi(nc, w_hi[:, :, 0:EXPERTS], raw[:]).then_inc(w_hi_ready, 1)
                for h in range(HALVES):
                    act.wait_ge(l_ready, h + 1)
                    nc.scalar.activation(lT[:, h * HALF:(h + 1) * HALF], L[0:EXPERTS, h, :], ACT.Identity, bias=b_sb[:, 0:1])\
                        .then_inc(lT_ready, 1)
                act.wait_ge(diff_ready, 1)
                nc.scalar.activation(e1[:], diff[:], ACT.Exp).then_inc(e1_ready, 1)

            @block.tensor
            def _(pe):
                pe.wait_ge(w_lo_ready, 1)
                for h in range(HALVES):
                    for k in range(KC):
                        last = product(pe, L[:, h, :], w_hi[:, k, :], w_lo[:, k, :], a_hi[:, k, h * HALF:(h + 1) * HALF],
                                       a_lo[:, k, h * HALF:(h + 1) * HALF], k == 0, k == KC - 1)
                    last.then_inc(l_ready, 1)
                pe.wait_ge(lT_ready, 2)
                for t in range(TILES):
                    last = pe.transpose(T[:, t * EXPERTS:(t + 1) * EXPERTS], lT[:, t * P:(t + 1) * P], ident[0:EXPERTS, 0:EXPERTS])
                last.then_inc(turned, 1)

            @block.vector
            def _(dve):
                step = [0]

                def link(ins):
                    step[0] += 1
                    ins.then_inc(chain, 1)
                    dve.wait_ge(chain, step[0])

                nc.vector.memset(w_hi[:].bitcast(F32), 0.0).then_inc(cleared, 1)
                nc.vector.memset(w_lo[:].bitcast(F32), 0.0).then_inc(cleared, 1)
                dve.wait_ge(w_hi_ready, 1)
                split_lo(nc, w_lo[:, :, 0:EXPERTS], raw[:], w_hi[:, :, 0:EXPERTS]).then_inc(w_lo_ready, 1)
                dve.wait_ge(turned, 1)
                link(nc.vector.tensor_copy(lg[:], T[:, 0:TILES * EXPERTS].rearrange("p (t e) -> p t e", e=EXPERTS)))
                for t in range(TILES):
                    last = nc.vector.max(top[:, t, :], lg[:, t, :])
                link(last)
                for t in range(TILES):
                    last = nc.vector.max_index(at[:, t, :], top[:, t, :], lg[:, t, :])
                link(last)
                link(nc.vector.tensor_copy(at_f[:], at[:]))
                nc.vector.tensor_tensor(diff[:], top[:, :, 1], top[:, :, 0], ALU.subtract).then_inc(diff_ready, 1)
                dve.wait_ge(e1_ready, 1)
                link(nc.vector.tensor_scalar(den[:], e1[:], 1.0, None, ALU.add))
                link(nc.vector.reciprocal(g0[:], den[:]))
                link(nc.vector.tensor_tensor(g1[:], e1[:], g0[:], ALU.mult))
                dve.wait_ge(number_ready, 1)
                for t in range(TILES):
                    nc.vector.tensor_scalar(first[:, t, :], number[:], at_f[:, t, 0:1], g0[:, t:t + 1], ALU.is_equal, ALU.mult)
                    last = nc.vector.tensor_scalar(second[:, t, :], number[:], at_f[:, t, 1:2], g1[:, t:t + 1], ALU.is_equal, ALU.mult)
                link(last)
                nc.vector.memset(gates[:, :, EXPERTS:EXPERTS + SHARED], 1.0)
                nc.vector.tensor_tensor(gates[:, :, 0:EXPERTS], first[:], second[:], ALU.add).then_inc(chain, 1)


def load_expert(sp, raw13, raw2, w13_loaded, w2_loaded, e, w1, w3, w2, between=None):
    sp.dma_start(raw13[:, 0, :, :], w1[e].rearrange("(k p) h -> p k h", p=P)).then_inc(w13_loaded, 16)
    sp.dma_start(raw13[:, 1, :, :], w3[e].rearrange("(k p) h -> p k h", p=P)).then_inc(w13_loaded, 16)
    if between is not None:
        between(sp)
    sp.dma_start(raw2[:], w2[e].rearrange("(k p) n -> p k n", p=P)).then_inc(w2_loaded, 16)


def experts_stage(nc, x_sb, a_hi, a_lo, gates, routed, shared, raw13, raw2, w13_loaded, w2_loaded):
    N = EXPERTS + SHARED
    UNITS = HALVES * HC
    with ExitStack() as ctx:
        s = Space(nc, ctx, "ex")
        w13_hi, w13_lo = s.sb("w13_hi", [P, 2, KC, HID], F32R), s.sb("w13_lo", [P, 2, KC, HID], F32R)
        w2_hi, w2_lo = s.sb("w2_hi", [P, HC, D], F32R), s.sb("w2_lo", [P, HC, D], F32R)
        act1, h32 = s.sb("act1", [P, 2, HALF]), s.sb("h32", [P, 2, HALF])
        h_hi, h_lo = s.sb("h_hi", [P, HC, TOKENS], F32R), s.sb("h_lo", [P, HC, TOKENS], F32R)
        gate = s.sb("gate", [P, TILES])
        H = s.ps("H", [P, 2, 2, 512])
        O = s.ps("O", [P, 4, 512])
        (w13_hi_ready, w13_lo_ready, w2_hi_ready, w2_lo_ready, h_produced, silu_ready, h32_ready,
         h_hi_ready, h_lo_ready, o_produced, added, gate_ready) = (s.sem(n) for n in (
             "w13_hi_ready", "w13_lo_ready", "w2_hi_ready", "w2_lo_ready", "h_produced",
             "silu_ready", "h32_ready", "h_hi_ready", "h_lo_ready", "o_produced", "added", "gate_ready"))

        def hidden(buf, u):
            return buf[:, u % HC, (u // HC) * HALF:(u // HC + 1) * HALF]

        with nc.Block() as block:

            @block.sync
            def _(sp):
                def load(n, e, w1, w3, w2):
                    sp.wait_ge(w13_lo_ready, n)
                    load_expert(sp, raw13, raw2, w13_loaded, w2_loaded, e, w1, w3, w2,
                                between=lambda sp: sp.wait_ge(w2_lo_ready, n))

                with sp.Fori(1, EXPERTS) as e:
                    load(e, e, *routed)
                with sp.Fori(0, SHARED) as e:
                    load(e + EXPERTS, e, *shared)

            @block.scalar
            def _(act):
                def split13(n):
                    act.wait_ge(w13_loaded, 32 * n + 32)
                    wait_after(act, h_produced, UNITS * n)
                    split_hi(nc, w13_hi[:], raw13[:]).then_inc(w13_hi_ready, 1)

                def expert(n, more):
                    act.wait_ge(w2_loaded, 16 * n + 16)
                    wait_after(act, o_produced, TILES * n)
                    split_hi(nc, w2_hi[:], raw2[:]).then_inc(w2_hi_ready, 1)

                    def high(u):
                        act.wait_ge(h32_ready, UNITS * n + u + 1)
                        split_hi(nc, hidden(h_hi, u), h32[:, u % 2, :]).then_inc(h_hi_ready, 1)

                    for u in range(UNITS):
                        act.wait_ge(h_produced, UNITS * n + u + 1)
                        nc.scalar.activation(act1[:, u % 2, :], H[:, u % 2, 0, :], ACT.Silu).then_inc(silu_ready, 1)
                        if u:
                            high(u - 1)
                    high(UNITS - 1)
                    if more:
                        split13(n + 1)

                split13(0)
                expert(0, True)
                with act.Fori(1, N - 1) as n:
                    expert(n, True)
                expert(N - 1, False)

            @block.vector
            def _(dve):
                def split13(n):
                    dve.wait_ge(w13_hi_ready, n + 1)
                    split_lo(nc, w13_lo[:], raw13[:], w13_hi[:]).then_inc(w13_lo_ready, 1)

                def expert(n, more):
                    wait_after(dve, added, TILES * n)
                    nc.vector.tensor_copy(gate[:], gates[:, :, bass.ds(n, 1)].rearrange("p t e -> p (t e)")).then_inc(gate_ready, 1)
                    dve.wait_ge(w2_hi_ready, n + 1)
                    split_lo(nc, w2_lo[:], raw2[:], w2_hi[:]).then_inc(w2_lo_ready, 1)

                    def low(u):
                        dve.wait_ge(h_hi_ready, UNITS * n + u + 1)
                        split_lo(nc, hidden(h_lo, u), h32[:, u % 2, :], hidden(h_hi, u)).then_inc(h_lo_ready, 1)

                    for u in range(UNITS):
                        dve.wait_ge(silu_ready, UNITS * n + u + 1)
                        if u >= 2:
                            dve.wait_ge(h_lo_ready, UNITS * n + u - 1)
                        nc.vector.tensor_tensor(h32[:, u % 2, :], act1[:, u % 2, :], H[:, u % 2, 1, :], ALU.mult).then_inc(h32_ready, 1)
                        if u:
                            low(u - 1)
                    low(UNITS - 1)
                    if more:
                        split13(n + 1)
                    dve.wait_ge(gate_ready, n + 1)
                    for t in range(TILES):
                        dve.wait_ge(o_produced, TILES * n + t + 1)
                        nc.vector.scalar_tensor_tensor(out=x_sb[:, t, :], in0=O[:, t % 4, :], scalar=gate[:, t:t + 1],
                                                       in1=x_sb[:, t, :], op0=ALU.mult, op1=ALU.add).then_inc(added, 1)

                split13(0)
                expert(0, True)
                with dve.Fori(1, N - 1) as n:
                    expert(n, True)
                expert(N - 1, False)

            @block.tensor
            def _(pe):
                def expert(n):
                    pe.wait_ge(w13_lo_ready, n + 1)
                    for u in range(UNITS):
                        th, m = u // HC, u % HC
                        if u >= 2:
                            pe.wait_ge(h32_ready, UNITS * n + u - 1)
                        else:
                            wait_after(pe, h32_ready, UNITS * n)
                        for j in range(2):
                            for k in range(KC):
                                last = product(pe, H[:, u % 2, j, :], w13_hi[:, j, k, m * P:(m + 1) * P], w13_lo[:, j, k, m * P:(m + 1) * P],
                                               a_hi[:, k, th * HALF:(th + 1) * HALF], a_lo[:, k, th * HALF:(th + 1) * HALF],
                                               k == 0, k == KC - 1)
                        last.then_inc(h_produced, 1)
                    pe.wait_ge(w2_lo_ready, n + 1)
                    for t in range(TILES):
                        pe.wait_ge(h_lo_ready, UNITS * n + (t // 4) * HC + HC)
                        if t >= 4:
                            pe.wait_ge(added, TILES * n + t - 3)
                        else:
                            wait_after(pe, added, TILES * n)
                        for m in range(HC):
                            last = product(pe, O[:, t % 4, :], h_hi[:, m, t * P:(t + 1) * P], h_lo[:, m, t * P:(t + 1) * P],
                                           w2_hi[:, m, :], w2_lo[:, m, :], m == 0, m == HC - 1)
                        last.then_inc(o_produced, 1)

                expert(0)
                with pe.Fori(1, N) as n:
                    expert(n)


def experts_layer(nc, x_sb, ident, router_w, router_b, routed, shared):
    with ExitStack() as ctx:
        s = Space(nc, ctx, "moe")
        a_hi, a_lo = s.sb("a_hi", [P, KC, TOKENS], F32R), s.sb("a_lo", [P, KC, TOKENS], F32R)
        gates = s.sb("gates", [P, TILES, EXPERTS + SHARED])
        raw13, raw2 = s.sb("raw13", [P, 2, KC, HID]), s.sb("raw2", [P, HC, D])
        router_raw, router_bias = s.sb("router", [P, KC, EXPERTS]), s.sb("router_bias", [EXPERTS, 1])
        router_loaded, w13_loaded, w2_loaded = s.sem("router_loaded"), s.sem("w13_loaded"), s.sem("w2_loaded")

        def load_first(sp):
            sp.dma_start(router_raw[:], router_w.rearrange("(k p) e -> p k e", p=P)).then_inc(router_loaded, 16)
            sp.dma_start(router_bias[:], router_b.rearrange("(e a) -> e a", a=1)).then_inc(router_loaded, 16)
            load_expert(sp, raw13, raw2, w13_loaded, w2_loaded, 0, *routed)

        with ExitStack() as inner:
            xn = Space(nc, inner, "moex").sb("xn", [P, TILES, D])
            norm_stage(nc, "n2", x_sb, xn, ident, hi=a_hi, lo=a_lo, prefetch=load_first)
        router_stage(nc, a_hi, a_lo, ident, router_raw, router_bias, router_loaded, gates)
        experts_stage(nc, x_sb, a_hi, a_lo, gates, routed, shared, raw13, raw2, w13_loaded, w2_loaded)


HEADS, HEAD = 16, 32
HG = P // HEAD
GR = HEADS // HG
KG = 402
KP = 4 * KG
NEVER = -3e38
MASKED = -1e15


class CrossLoads:

    def __init__(self, nc, ctx, x_sb, x_kept, ctx_cols, mask, Wk, bk, Wv, bv):
        s = Space(nc, ctx, "cl")
        self.x_sb, self.x_kept, self.ctx_cols, self.mask = x_sb, x_kept, ctx_cols, mask
        self.Wk, self.bk, self.Wv, self.bv = Wk, bk, Wv, bv
        self.v = s.sb("v", [P, KT, D])
        self.w_raw = self.v[:, 0:2 * KC, :].rearrange("p (w k) n -> p w k n", w=2)
        self.own_raw = s.sb("raw", [P, 2, KEYS])
        self.bk_sb, self.bv_sb = s.sb("bk", [P, KC]), s.sb("bv", [P, D])
        lent = x_sb[:].rearrange("p t d -> p (t d)")
        m8_at, o_at = 2 * KEYS, 2 * KEYS + -(-KEYS // 4)
        self.lent_raw = lent[:, 0:m8_at].rearrange("p (k j) -> p k j", k=2)
        self.m8 = lent[:, m8_at:o_at].bitcast(U8)[:, 0:KEYS]
        self.o = lent[:, o_at:o_at + GR * SEQ].rearrange("p (g i) -> p g i", g=GR)
        self.wk_loaded, self.wv_loaded, self.small_loaded, self.x_stored, self.mask_loaded = (
            s.sem(n) for n in ("wk_loaded", "wv_loaded", "small_loaded", "x_stored", "mask_loaded"))
        self.raw_loaded = [s.sem(f"raw_loaded{k}") for k in range(KC)]

    def raw(self, k):
        return self.own_raw[:, k, :] if k < 2 else self.lent_raw[:, k - 2, :]

    def load_weights(self, sp):
        sp.dma_start(self.w_raw[:, 0], self.Wk.rearrange("(k p) n -> p k n", p=P)).then_inc(self.wk_loaded, 16)
        sp.dma_start(self.w_raw[:, 1], self.Wv.rearrange("(k p) n -> p k n", p=P)).then_inc(self.wv_loaded, 16)
        sp.dma_start(self.x_kept, self.x_sb[:]).then_inc(self.x_stored, 16)

    def load_chunk(self, sp, b, k):
        sp.dma_start(self.raw(k), self.ctx_cols[b, k * P:(k + 1) * P, :]).then_inc(self.raw_loaded[k], 16)

    def load_mask(self, sp, b):
        for i in range(2):
            sp.dma_start(self.m8[SEQ * i:SEQ * i + SEQ, :], self.mask[b, 0]).then_inc(self.mask_loaded, 16)

    def load_first(self, sp):
        sp.wait_ge(self.x_stored, 16)
        for k in range(KC):
            self.load_chunk(sp, 0, k)
        self.load_mask(sp, 0)


def cross_attention_stage(nc, loads, qoT, ident):
    T_GROUPS = [(n, min(n + 2, KT)) for n in range(0, KT, 2)]
    ACT_T = [i for i in range(len(T_GROUPS)) if i % 2 == 0]
    DVE_T = [i for i in range(len(T_GROUPS)) if i % 2 == 1]
    TG = len(T_GROUPS)
    TURNS = ((), (0, 1), (2, 3), (5, 6))
    AMID = 4
    DVE_CHUNKS = 2
    PARTS = ((0, 2 * KG), (2 * KG, KEYS))
    with ExitStack() as ctx:
        s = Space(nc, ctx, "xa")
        wk_hi, wk_lo = s.sb("wk_hi", [P, KC, D], F32R), s.sb("wk_lo", [P, KC, D], F32R)
        wv_hi, wv_lo = s.sb("wv_hi", [P, KC, D], F32R), s.sb("wv_lo", [P, KC, D], F32R)
        bk_sb, bv_sb, raw, w_raw, v, m8, o = loads.bk_sb, loads.bv_sb, loads.raw, loads.w_raw, loads.v, loads.m8, loads.o
        small_loaded, raw_loaded, mask_loaded = loads.small_loaded, loads.raw_loaded, loads.mask_loaded
        c_hi, c_lo = s.sb("c_hi", [P, KC, KP], F32R), s.sb("c_lo", [P, KC, KP], F32R)
        kT_hi, kT_lo = s.sb("kT_hi", [P, KP], F32R), s.sb("kT_lo", [P, KP], F32R)
        m = s.sb("m", [P, KP])
        pr = s.sb("pr", [P, 2, KP])
        pT = s.sb("pT", [P, KT, 2 * P])
        q_hi, q_lo = s.sb("q_hi", [P, GR, 2, P], F32R), s.sb("q_lo", [P, GR, 2, P], F32R)
        mx, nm, rs, ri = s.sb("mx", [P, 2, 2]), s.sb("nm", [P, 2]), s.sb("rs", [P, 2]), s.sb("ri", [P, 2])
        S = s.ps("S", [P, 4, 512])
        J = s.ps("J", [P, 2, 512])
        T = s.ps("T", [P, 2, 512])
        w_hi_ready, w_lo_ready, cleared, x_loaded = (s.sem(n) for n in ("w_hi_ready", "w_lo_ready", "cleared", "x_loaded"))
        c_hi_ready, c_lo_ready, m_ready, q_hi_ready, q_ready, c_lo_pool = (s.sem(n) for n in (
            "c_hi_ready", "c_lo_ready", "m_ready", "q_hi_ready", "q_ready", "c_lo_pool"))
        k_made, v_made, k_hi_ready, k_lo_ready, v_stored, scored, masked, max_ready, exp_done, inv_ready, scaled = (s.sem(n) for n in (
            "k_made", "v_made", "k_hi_ready", "k_lo_ready", "v_stored", "scored", "masked", "max_ready", "exp_done", "inv_ready", "scaled"))
        turned, t_act, t_dve, o_made, o_stored, o_kept = (s.sem(n) for n in (
            "turned", "t_act", "t_dve", "o_made", "o_stored", "o_kept"))
        KU, VU = GR * 4, KT
        SU = GR * 2 * 2
        TU = GR * TG
        CLEARED = 5

        def wait_low(engine, b, part, k):
            if k < DVE_CHUNKS:
                engine.wait_ge(c_lo_ready, DVE_CHUNKS * (2 * b + part) + k + 1)
            else:
                engine.wait_ge(c_lo_pool, (KC - DVE_CHUNKS) * (2 * b + part) + k - DVE_CHUNKS + 1)

        def before(b, g):
            if g:
                return b, g - 1
            return None if isinstance(b, int) and b == 0 else (b - 1, GR - 1)

        def query_blocks(part, b, h):
            hs = slice(HEAD * h, HEAD * (h + 1))
            return part[hs, :, h // 2, SEQ * (h % 2):SEQ * (h % 2 + 1)], qoT[hs, :, bass.ds(b * SEQ, SEQ)]

        with nc.Block() as block:

            @block.sync
            def _(sp):
                with nc.allow_non_contiguous_dma(reason="512 values, once"):
                    sp.dma_start(bk_sb[:], loads.bk.rearrange("(k p) -> p k", p=P)).then_inc(small_loaded, 16)
                sp.dma_start(bv_sb[:], rows_of(loads.bv, P)).then_inc(small_loaded, 16)

                with sp.Fori(1, BATCH) as b:
                    for k in range(KC):
                        wait_low(sp, b - 1, 1, k)
                        loads.load_chunk(sp, b, k)
                    sp.wait_ge(small_loaded, 32)
                    sp.wait_ge(m_ready, b)
                    loads.load_mask(sp, b)
                sp.wait_ge(o_kept, BATCH)
                sp.dma_start(loads.x_sb[:], loads.x_kept).then_inc(x_loaded, 16)
                sp.wait_ge(x_loaded, 16)

            @block.scalar
            def _(act):
                act.wait_ge(loads.wk_loaded, 16)
                split_hi(nc, wk_hi[:], w_raw[:, 0]).then_inc(w_hi_ready, 1)

                def high(b, part, k):
                    act.wait_ge(raw_loaded[k], 16 * b + 16)
                    if k == 0:
                        wait_after(act, k_made, KU * b)
                    split_hi(nc, c_hi[:, k, slice(*PARTS[part])], raw(k)[:, slice(*PARTS[part])]).then_inc(c_hi_ready, 1)

                def keep_key(b, g, j):
                    act.wait_ge(k_made, KU * b + 4 * g + j + 1)
                    nc.scalar.activation(kT_hi[:, j * KG:(j + 1) * KG], J[:, key_bank(g, j), 0:KG], ACT.Identity,
                                         bias=bk_sb[:, g:g + 1]).then_inc(k_hi_ready, 1)

                def queries_high(b):
                    wait_after(act, scored, SU * b)
                    for h in range(HG):
                        last = split_hi(nc, *query_blocks(q_hi, b, h))
                    last.then_inc(q_hi_ready, 1)

                def widen_mask(b):
                    act.wait_ge(mask_loaded, 32 * b + 32)
                    wait_after(act, masked, SU * b)
                    nc.scalar.activation(m[:, 0:KEYS], m8, ACT.Copy, scale=MASKED).then_inc(m_ready, 1)

                def exps(b, g, i):
                    act.wait_ge(max_ready, 2 * (GR * b + g) + i + 1)
                    nc.scalar.activation(pr[:, i, :], pr[:, i, :], ACT.Exp, bias=nm[:, i:i + 1],
                                         accum_out=rs[:, i:i + 1]).then_inc(exp_done, 1)

                def copy_turned(b, g, i):
                    act.wait_ge(turned, TU * b + TG * g + i + 1)
                    n0, n1 = T_GROUPS[i]
                    r = rows(n1 - 1)
                    nc.scalar.activation(pT[0:r, n0:n1, :], T[0:r, 0, 0:(n1 - n0) * 2 * P].rearrange("p (n c) -> p n c", c=2 * P),
                                         ACT.Copy).then_inc(t_act, 1)

                def keep_result(b, g):
                    act.wait_ge(o_made, GR * b + g + 1)
                    if g == 0:
                        wait_after(act, o_kept, b)
                    nc.scalar.activation(o[:, g, :], J[:, RESULT_BANK[g], 0:SEQ], ACT.Copy).then_inc(o_stored, 1)

                for k in range(KC):
                    high(0, 0, k)
                act.wait_ge(loads.wv_loaded, 16)
                split_hi(nc, wv_hi[:], w_raw[:, 1]).then_inc(w_hi_ready, 1)
                for k in range(KC):
                    high(0, 1, k)
                act.wait_ge(small_loaded, 32)
                act.wait_ge(cleared, CLEARED)

                def batch(b, more):
                    for g in range(GR):
                        old = before(b, g)
                        for j in range(4):
                            if old and j == 3:
                                copy_turned(*old, AMID)
                            keep_key(b, g, j)
                            if g == 0 and j == 0:
                                queries_high(b)
                                widen_mask(b)
                            if old:
                                for i in TURNS[j]:
                                    if i in ACT_T:
                                        copy_turned(*old, i)
                        load_next = more and g == GR - 1
                        if load_next:
                            for k in range(KC):
                                high(b + 1, 0, k)
                        exps(b, g, 0)
                        if old:
                            keep_result(*old)
                        if load_next:
                            for k in range(3):
                                high(b + 1, 1, k)
                        exps(b, g, 1)
                        if load_next:
                            high(b + 1, 1, 3)

                batch(0, True)
                with act.Fori(1, BATCH - 1) as b:
                    batch(b, True)
                batch(BATCH - 1, False)
                for i in ACT_T:
                    copy_turned(BATCH - 1, GR - 1, i)
                keep_result(BATCH - 1, GR - 1)

            @block.vector
            def _(dve):
                def low(b, part, k):
                    dve.wait_ge(c_hi_ready, 2 * KC * b + KC * part + k + 1)
                    js = slice(*PARTS[part])
                    split_lo(nc, c_lo[:, k, js], raw(k)[:, js], c_hi[:, k, js]).then_inc(c_lo_ready, 1)

                def queries_low(b):
                    dve.wait_ge(q_hi_ready, b + 1)
                    for h in range(HG):
                        to, now = query_blocks(q_lo, b, h)
                        last = nc.vector.tensor_tensor(to, now, query_blocks(q_hi, b, h)[0].bitcast(F32), ALU.subtract)
                    last.then_inc(q_ready, 1)

                def keep_key(b, g, j):
                    dve.wait_ge(k_hi_ready, KU * b + 4 * g + j + 1)
                    ks = slice(j * KG, (j + 1) * KG)
                    nc.vector.scalar_tensor_tensor(out=kT_lo[:, ks], in0=J[:, key_bank(g, j), 0:KG], scalar=bk_sb[:, g:g + 1],
                                                   in1=kT_hi[:, ks].bitcast(F32), op0=ALU.add, op1=ALU.subtract).then_inc(k_lo_ready, 1)

                def mask_scores(b, g, i):
                    for h in range(2):
                        half = dve.to_reg(SU * b + 4 * g + 2 * i + h + 1)
                        dve.wait_ge(cleared, CLEARED)
                        dve.wait_ge(scored, half)
                        ks = slice(2 * KG * h, 2 * KG * (h + 1))
                        nc.vector.tensor_tensor_reduce(out=pr[:, i, ks].rearrange("p (a c) -> p a c", c=KG), in0=S[:, 2 * h:2 * h + 2, 0:KG],
                                                       in1=m[:, ks].rearrange("p (a c) -> p a c", c=KG), scale=1.0, scalar=NEVER,
                                                       op0=ALU.add, op1=ALU.max, accum_out=mx[:, i, h:h + 1]).then_inc(masked, 1)
                    dve.wait_ge(masked, SU * b + 4 * g + 2 * i + 2)
                    wait_after(dve, exp_done, 2 * (GR * b + g))
                    nc.vector.tensor_reduce(nm[:, i:i + 1], mx[:, i, :], AX.X, ALU.max, negate=True).then_inc(max_ready, 1)

                def normalise(b, g, i):
                    dve.wait_ge(exp_done, 2 * (GR * b + g) + i + 1)
                    nc.vector.reciprocal(ri[:, i:i + 1], rs[:, i:i + 1]).then_inc(inv_ready, 1)
                    dve.wait_ge(inv_ready, 2 * (GR * b + g) + i + 1)
                    nc.vector.tensor_scalar(pr[:, i, :], pr[:, i, :], ri[:, i:i + 1], None, ALU.mult).then_inc(scaled, 1)

                def keep_values(b, n):
                    dve.wait_ge(v_made, VU * b + n + 1)
                    nc.vector.tensor_tensor(v[0:rows(n), n, :], J[0:rows(n), value_bank(n), :], bv_sb[0:rows(n), :], ALU.add)\
                        .then_inc(v_stored, 1)

                def copy_turned(b, g, i):
                    dve.wait_ge(turned, TU * b + TG * g + i + 1)
                    n0, n1 = T_GROUPS[i]
                    nc.vector.tensor_copy(pT[:, n0:n1, :], T[:, 1, :].rearrange("p (n c) -> p n c", c=2 * P)).then_inc(t_dve, 1)

                def keep_results(b):
                    dve.wait_ge(o_stored, GR * b + GR)
                    nc.vector.tensor_copy(qoT[:, :, bass.ds(b * SEQ, SEQ)], o).then_inc(o_kept, 1)

                dve.wait_ge(w_hi_ready, 1)
                split_lo(nc, wk_lo[:], w_raw[:, 0], wk_hi[:]).then_inc(w_lo_ready, 1)
                for k in range(DVE_CHUNKS):
                    low(0, 0, k)
                dve.wait_ge(w_hi_ready, 2)
                split_lo(nc, wv_lo[:], w_raw[:, 1], wv_hi[:]).then_inc(w_lo_ready, 1)
                for k in range(DVE_CHUNKS):
                    low(0, 1, k)
                dve.wait_ge(cleared, CLEARED)
                dve.wait_ge(small_loaded, 32)

                def batch(b, more):
                    for g in range(GR):
                        old = before(b, g)
                        for j in range(4):
                            if g == 0 and j == 3:
                                dve.wait_ge(m_ready, b + 1)
                            keep_key(b, g, j)
                            if g == 0 and j == 2:
                                queries_low(b)
                            if old:
                                for i in TURNS[j]:
                                    if i in DVE_T:
                                        copy_turned(*old, i)
                        load_next = more and g == GR - 1
                        mask_scores(b, g, 0)
                        if load_next:
                            low(b + 1, 0, 0)
                            low(b + 1, 0, 1)
                        mask_scores(b, g, 1)
                        normalise(b, g, 0)
                        if load_next:
                            low(b + 1, 1, 0)
                        normalise(b, g, 1)
                        if load_next:
                            low(b + 1, 1, 1)
                        if g == 0:
                            for n in range(KT):
                                keep_values(b, n)
                            if old:
                                keep_results(old[0])

                batch(0, True)
                with dve.Fori(1, BATCH - 1) as b:
                    batch(b, True)
                batch(BATCH - 1, False)
                for i in DVE_T:
                    copy_turned(BATCH - 1, GR - 1, i)
                keep_results(BATCH - 1)

            @block.gpsimd
            def _(pool):
                def low_of_last_chunks(b):
                    for part, (j0, j1) in enumerate(PARTS):
                        for k in range(DVE_CHUNKS, KC):
                            pool.wait_ge(c_hi_ready, 2 * KC * b + KC * part + k + 1)
                            nc.gpsimd.tensor_tensor(c_lo[:, k, j0:j1], raw(k)[:, j0:j1], c_hi[:, k, j0:j1].bitcast(F32), ALU.subtract)\
                                .then_inc(c_lo_pool, 1)

                for region, value in ((c_hi[:, :, KEYS:KP].bitcast(F32), 0.0), (c_lo[:, :, KEYS:KP].bitcast(F32), 0.0),
                                      (m[:, KEYS:KP], NEVER), (q_hi[:].bitcast(F32), 0.0), (q_lo[:].bitcast(F32), 0.0)):
                    nc.gpsimd.memset(region, value).then_inc(cleared, 1)
                low_of_last_chunks(0)
                with pool.Fori(1, BATCH) as b:
                    low_of_last_chunks(b)

            @block.tensor
            def _(pe):
                pe.wait_ge(cleared, CLEARED)
                pe.wait_ge(w_lo_ready, 1)

                def bank_free(b, unit):
                    if unit < 2:
                        if not before(b, 0):
                            return
                        b = b - 1
                    kind, g, j = UNITS[unit - 2 if unit >= 2 else LAST_IN_BANK[unit]]
                    if kind == "k":
                        pe.wait_ge(k_lo_ready, KU * b + 4 * g + j + 1)
                    elif kind == "v":
                        pe.wait_ge(v_stored, VU * b + j + 1)
                    elif g == GR - 1:
                        wait_after(pe, o_stored, GR * b)
                    else:
                        pe.wait_ge(o_stored, GR * b + g + 1)

                def key_tile(b, g, j):
                    bank_free(b, UNITS.index(("k", g, j)))
                    for k in range(KC):
                        if k == KC // 2 and j == 3 and before(b, g):
                            turn(*before(b, g), AMID)
                        if g == 0 and j % 2 == 0:
                            wait_low(pe, b, j // 2, k)
                        last = product(pe, J[:, key_bank(g, j), 0:KG], wk_hi[:, k, g * P:(g + 1) * P], wk_lo[:, k, g * P:(g + 1) * P],
                                       c_hi[:, k, j * KG:(j + 1) * KG], c_lo[:, k, j * KG:(j + 1) * KG], k == 0, k == KC - 1)
                    last.then_inc(k_made, 1)

                def values(b):
                    pe.wait_ge(w_lo_ready, 2)
                    for n in range(KT):
                        bank_free(b, UNITS.index(("v", 0, n)))
                        w = min(P, KP - n * P)
                        for k in range(KC):
                            last = product(pe, J[0:w, value_bank(n), :], c_hi[:, k, n * P:n * P + w], c_lo[:, k, n * P:n * P + w],
                                           wv_hi[:, k, :], wv_lo[:, k, :], k == 0, k == KC - 1)
                        last.then_inc(v_made, 1)

                def scores(b, g, i):
                    if g == 0 and i == 0:
                        pe.wait_ge(q_ready, b + 1)
                    for j in range(4):
                        if i == 0:
                            pe.wait_ge(k_lo_ready, KU * b + 4 * g + j + 1)
                        if j % 2 == 0:
                            if g == 0 and i == 0:
                                wait_after(pe, masked, SU * b)
                            else:
                                wait_after(pe, masked, SU * b + 4 * g + 2 * i + j // 2 - 1)
                        ks = slice(j * KG, (j + 1) * KG)
                        last = product(pe, S[:, j, 0:KG], q_hi[:, g, i, :], q_lo[:, g, i, :], kT_hi[:, ks], kT_lo[:, ks], True, True)
                        if j % 2 == 1:
                            last.then_inc(scored, 1)

                def turn(b, g, i):
                    if i == 0:
                        pe.wait_ge(scaled, 2 * (GR * b + g) + 2)
                    wait_after(pe, t_dve if i % 2 else t_act, (len(DVE_T) if i % 2 else len(ACT_T)) * (GR * b + g) + i // 2)
                    n0, n1 = T_GROUPS[i]
                    for n in range(n0, n1):
                        r = rows(n)
                        for a in range(2):
                            last = pe.transpose(T[0:r, i % 2, (2 * (n - n0) + a) * P:(2 * (n - n0) + a + 1) * P],
                                                pr[:, a, n * P:n * P + r], ident[:])
                    last.then_inc(turned, 1)

                def result(b, g):
                    if g == 0:
                        pe.wait_ge(v_stored, VU * b + VU)
                    if g == GR - 1:
                        if isinstance(b, int) and b == BATCH - 1:
                            pe.wait_ge(o_stored, GR * b + g)
                        pe.wait_ge(k_lo_ready, KU * (b + 1) + 4 if not (isinstance(b, int) and b == BATCH - 1) else KU * BATCH)
                    else:
                        bank_free(b, UNITS.index(("o", g, 0)))
                    for i, (n0, n1) in enumerate(T_GROUPS):
                        pe.wait_ge(t_dve if i % 2 else t_act, (len(DVE_T) if i % 2 else len(ACT_T)) * (GR * b + g) + i // 2 + 1)
                        for n in range(n0, n1):
                            r = rows(n)
                            for h in range(HG):
                                hs = slice(HEAD * h, HEAD * (h + 1))
                                last = pe.matmul(J[hs, RESULT_BANK[g], 0:SEQ], v[0:r, n, g * P + HEAD * h:g * P + HEAD * (h + 1)],
                                                 pT[0:r, n, SEQ * h:SEQ * (h + 1)], start=(n == 0), stop=(n == KT - 1))
                    last.then_inc(o_made, 1)

                def batch(b):
                    for g in range(GR):
                        old = before(b, g)
                        for j in range(4):
                            key_tile(b, g, j)
                            if old:
                                for i in TURNS[j]:
                                    turn(*old, i)
                        scores(b, g, 0)
                        if old:
                            result(*old)
                        scores(b, g, 1)
                        if g == 0:
                            values(b)

                batch(0)
                with pe.Fori(1, BATCH) as b:
                    batch(b)
                for i in range(TG):
                    turn(BATCH - 1, GR - 1, i)
                result(BATCH - 1, GR - 1)


UNITS = ([("k", 0, j) for j in range(4)] + [("o", 3, 0)] + [("v", 0, n) for n in range(KT)] + [("k", 1, j) for j in range(4)]
         + [("o", 0, 0)] + [("k", 2, j) for j in range(4)] + [("o", 1, 0)] + [("k", 3, j) for j in range(4)] + [("o", 2, 0)])
RESULT_BANK = [UNITS.index(("o", g, 0)) % 2 for g in range(GR)]
LAST_IN_BANK = [max(u for u in range(len(UNITS)) if u % 2 == bank) for bank in range(2)]


def key_bank(g, j):
    return UNITS.index(("k", g, j)) % 2


def value_bank(n):
    return UNITS.index(("v", 0, n)) % 2


def cross_layer(nc, x_sb, ident, ctx_cols, mask, Wq, bq, Wk, bk, Wv, bv, Wo, bo):
    x_kept = nc.dram_tensor("x_kept", (P, TILES, D), F32, kind="Internal").ap()
    with ExitStack() as ctx:
        qoT = Space(nc, ctx, "cross").sb("qoT", [P, KC, TOKENS])
        with ExitStack() as held:
            loads = CrossLoads(nc, held, x_sb, x_kept, ctx_cols, mask, Wk, bk, Wv, bv)
            with ExitStack() as inner:
                s = Space(nc, inner, "crossq")
                a_hi, a_lo = s.sb("a_hi", [P, KC, TOKENS], F32R), s.sb("a_lo", [P, KC, TOKENS], F32R)
                with ExitStack() as inner2:
                    xn = Space(nc, inner2, "crossx").sb("xn", [P, TILES, D])
                    norm_stage(nc, "n3", x_sb, xn, ident, hi=a_hi, lo=a_lo, prefetch=loads.load_weights)
                project_stage(nc, "pj2", a_hi, a_lo, [(FEATURES, Wq, bq, HEAD**-0.5, qoT)], prefetch=loads.load_first)
            cross_attention_stage(nc, loads, qoT, ident)
        with ExitStack() as inner:
            s = Space(nc, inner, "crosso")
            o_hi, o_lo = s.sb("o_hi", [P, KC, TOKENS], F32R), s.sb("o_lo", [P, KC, TOKENS], F32R)
            project_stage(nc, "pj3", o_hi, o_lo, [(RESIDUAL, Wo, bo, 1.0, x_sb)], source=qoT)


QH, QD = 32, 16
VH, VD = 16, 32
FLT_MAX = 3.4028234663852886e38
LAMBDA_INIT = 0.8 - 0.6 * 0.7408182206817179


def differential_stage(nc, q, k, v, out, lq1, lk1, lq2, lk2, ident):
    DB = 4
    NB = QD // DB
    POOL_BLOCKS = (1, 3)
    with ExitStack() as ctx:
        s = Space(nc, ctx, "df")
        prod = s.sb("prod", [P, NB, DB, QH, QH])
        vprod = s.sb("vprod", [P, VH, VH, VD])
        pos, sc = s.sb("pos", [P, QH, QH]), s.sb("sc", [P, QH, QH])
        e = s.sb("e", [P, QH, QH])
        mx, den, inv = s.sb("mx", [P, QH]), s.sb("den", [P, QH]), s.sb("inv", [P, QH])
        att, att2 = s.sb("att", [P, VH, VH]), s.sb("att2", [P, VH, VH])
        lam_in = s.sb("lam_in", [P, 4, QD])
        lam_prod, lam_sum, lam_exp, lam = s.sb("lam_prod", [P, 2, QD]), s.sb("lam_sum", [P, 2]), s.sb("lam_exp", [P, 2]), s.sb("lam", [P, 1])
        sq = s.sb("sq", [P, 2, D])
        ms, r0, r1, r2 = (s.sb(n, [P, TILES * VH]) for n in ("ms", "r0", "r1", "r2"))
        S = s.ps("S", [P, 2, 2, 512])
        (lam_loaded, lam_summed, lam_exp_ready, chain, prod_pool, prod_dve, summed, clamped, shifted, exp_done, out_ready, squared,
         sq_summed, ms_ready, root_ready, att_ready, vprod_pool) = (s.sem(n) for n in (
             "lam_loaded", "lam_summed", "lam_exp_ready", "chain", "prod_pool", "prod_dve", "summed", "clamped", "shifted",
             "exp_done", "out_ready", "squared", "sq_summed", "ms_ready", "root_ready", "att_ready", "vprod_pool"))

        def multiply(eng, t, n):
            cols = slice(n * DB * QH, (n + 1) * DB * QH)
            a = q[:, t, cols].rearrange("p (d i) -> p d i", d=DB)[:, :, :, None].to_broadcast([P, DB, QH, QH])
            b = k[:, t, cols].rearrange("p (d j) -> p d j", d=DB)[:, :, None, :].to_broadcast([P, DB, QH, QH])
            return eng.tensor_tensor(prod[:, n], a, b, ALU.mult)

        def weigh(eng, t, half):
            hs = slice(half * VH // 2, (half + 1) * VH // 2)
            a = att[:, :, hs].rearrange("p a h -> p h a")[:, :, :, None].to_broadcast([P, VH // 2, VH, VD])
            b = v[:, t, :].rearrange("p (h d) -> p h d", h=VH)[:, hs, None, :].to_broadcast([P, VH // 2, VH, VD])
            return eng.tensor_tensor(vprod[:, hs], a, b, ALU.mult)

        with nc.Block() as block:

            @block.sync
            def _(sp):
                for i, vec in enumerate((lq1, lk1, lq2, lk2)):
                    sp.dma_start(lam_in[:, i, :], rows_of(vec, P)).then_inc(lam_loaded, 16)

            @block.gpsimd
            def _(pool):
                def products(t):
                    for n in POOL_BLOCKS:
                        if t:
                            pool.wait_ge(summed, NB * (t - 1) + n + 1)
                        multiply(nc.gpsimd, t, n).then_inc(prod_pool, 1)

                products(0)
                products(1)
                for t in range(TILES):
                    pool.wait_ge(att_ready, t + 1)
                    if t:
                        pool.wait_ge(out_ready, t)
                    weigh(nc.gpsimd, t, 1).then_inc(vprod_pool, 1)
                    if t + 2 < TILES:
                        products(t + 2)

            @block.tensor
            def _(pe):
                for t in range(TILES):
                    if t >= 2:
                        pe.wait_ge(clamped, t - 1)
                    for n in range(NB):
                        if n in POOL_BLOCKS:
                            pe.wait_ge(prod_pool, len(POOL_BLOCKS) * t + POOL_BLOCKS.index(n) + 1)
                        else:
                            pe.wait_ge(prod_dve, (NB - len(POOL_BLOCKS)) * t + n // 2 + 1)
                        for d in range(DB):
                            for h in range(2):
                                last = pe.matmul(S[:, t % 2, h, :], ident[:], prod[:, n, d, h * 16:(h + 1) * 16, :],
                                                 start=(n == 0 and d == 0), stop=(n == NB - 1 and d == DB - 1))
                        last.then_inc(summed, 1)

            @block.scalar
            def _(act):
                def square(t):
                    act.wait_ge(out_ready, t + 1)
                    if t >= 2:
                        act.wait_ge(sq_summed, t - 1)
                    nc.scalar.activation(sq[:, t % 2, :], out[:, t, :], ACT.Square).then_inc(squared, 1)

                act.wait_ge(lam_summed, 1)
                nc.scalar.activation(lam_exp[:], lam_sum[:], ACT.Exp).then_inc(lam_exp_ready, 1)
                for t in range(TILES):
                    act.wait_ge(shifted, t + 1)
                    nc.scalar.activation(e[:], sc[:], ACT.Exp).then_inc(exp_done, 1)
                    if t:
                        square(t - 1)
                square(TILES - 1)
                act.wait_ge(ms_ready, 1)
                nc.scalar.activation(r0[:], ms[:], ACT.Sqrt).then_inc(root_ready, 1)

            @block.vector
            def _(dve):
                step = [0]

                def link(ins):
                    step[0] += 1
                    ins.then_inc(chain, 1)
                    dve.wait_ge(chain, step[0])

                def products(t):
                    for n in range(NB):
                        if n not in POOL_BLOCKS:
                            if t:
                                dve.wait_ge(summed, NB * (t - 1) + n + 1)
                            multiply(nc.vector, t, n).then_inc(prod_dve, 1)

                def sum_squares(t):
                    dve.wait_ge(squared, t + 1)
                    nc.vector.reduce_sum(ms[:, t * VH:(t + 1) * VH], sq[:, t % 2, :].rearrange("p (a d) -> p a d", a=VH), AX.X).then_inc(sq_summed, 1)

                dve.wait_ge(lam_loaded, 64)
                link(nc.vector.tensor_tensor(lam_prod[:], lam_in[:].rearrange("p (a b) d -> p a b d", b=2)[:, :, 0, :],
                                             lam_in[:].rearrange("p (a b) d -> p a b d", b=2)[:, :, 1, :], ALU.mult))
                nc.vector.reduce_sum(lam_sum[:], lam_prod[:], AX.X).then_inc(lam_summed, 1)
                products(0)
                dve.wait_ge(lam_exp_ready, 1)
                link(nc.vector.tensor_tensor(lam[:], lam_exp[:, 0:1], lam_exp[:, 1:2], ALU.subtract))
                link(nc.vector.tensor_scalar(lam[:], lam[:], LAMBDA_INIT, None, ALU.add))

                def front(t):
                    dve.wait_ge(summed, NB * t + NB)
                    flat = S[:, t % 2].rearrange("p h (i j) -> p (h i) j", j=QH)
                    link(nc.vector.tensor_scalar(pos[:], flat, 0.0, FLT_MAX, ALU.max, ALU.min))
                    if t:
                        dve.wait_ge(exp_done, t)
                    nc.vector.scalar_tensor_tensor(out=sc[:], in0=flat, scalar=0.0, in1=pos[:], op0=ALU.min, op1=ALU.add).then_inc(clamped, 1)
                    dve.wait_ge(clamped, t + 1)
                    link(nc.vector.tensor_reduce(mx[:], sc[:], AX.X, ALU.max))
                    link(nc.vector.tensor_scalar(mx[:], mx[:], -FLT_MAX, None, ALU.max))
                    nc.vector.scalar_tensor_tensor(out=sc[:], in0=sc[:], scalar=-FLT_MAX, in1=mx[:][:, :, None].to_broadcast([P, QH, QH]),
                                                   op0=ALU.max, op1=ALU.subtract).then_inc(shifted, 1)

                def weights(t):
                    dve.wait_ge(exp_done, t + 1)
                    link(nc.vector.reduce_sum(den[:], e[:], AX.X))
                    link(nc.vector.reciprocal(inv[:], den[:]))
                    link(nc.vector.tensor_scalar(inv[:, VH:QH], inv[:, VH:QH], lam[:, 0:1], None, ALU.mult))
                    link(nc.vector.tensor_tensor(att[:], e[:, 0:VH, 0:VH], inv[:, 0:VH][:, :, None].to_broadcast([P, VH, VH]), ALU.mult))
                    link(nc.vector.tensor_tensor(att2[:], e[:, VH:QH, VH:QH], inv[:, VH:QH][:, :, None].to_broadcast([P, VH, VH]), ALU.mult))
                    nc.vector.tensor_tensor(att[:], att[:], att2[:], ALU.subtract).then_inc(att_ready, 1)

                def add_up(t):
                    dve.wait_ge(vprod_pool, t + 1)
                    for n in (8, 4, 2):
                        link(nc.vector.tensor_tensor(vprod[:, 0:n], vprod[:, 0:n], vprod[:, n:2 * n], ALU.add))
                    nc.vector.tensor_tensor(out[:, t, :].rearrange("p (a d) -> p a d", a=VH), vprod[:, 0], vprod[:, 1], ALU.add).then_inc(out_ready, 1)

                products(1)
                front(0)
                for t in range(TILES):
                    weights(t)
                    dve.wait_ge(att_ready, t + 1)
                    link(weigh(nc.vector, t, 0))
                    if t + 2 < TILES:
                        products(t + 2)
                    if t + 1 < TILES:
                        front(t + 1)
                    add_up(t)
                    dve.wait_ge(out_ready, t + 1)
                    if t:
                        sum_squares(t - 1)
                sum_squares(TILES - 1)
                dve.wait_ge(sq_summed, TILES)
                nc.vector.tensor_scalar(ms[:], ms[:], 1.0 / VD, EPS, ALU.mult, ALU.add).then_inc(ms_ready, 1)
                dve.wait_ge(root_ready, 1)
                link(nc.vector.reciprocal(r1[:], r0[:]))
                link(nc.vector.tensor_tensor(r0[:], r1[:], r1[:], ALU.mult))
                link(nc.vector.tensor_tensor(r2[:], r0[:], ms[:], ALU.mult))
                link(nc.vector.tensor_scalar(r2[:], r2[:], -0.5 * (1.0 - LAMBDA_INIT), 1.5 * (1.0 - LAMBDA_INIT), ALU.mult, ALU.add))
                link(nc.vector.tensor_tensor(r0[:], r1[:], r2[:], ALU.mult))
                for t in range(TILES):
                    o = out[:, t, :].rearrange("p (a d) -> p a d", a=VH)
                    nc.vector.tensor_tensor(o, o, r0[:, t * VH:(t + 1) * VH][:, :, None].to_broadcast([P, VH, VD]), ALU.mult)


def turn_stage(nc, stage, x, hi, lo, ident):
    with ExitStack() as ctx:
        s = Space(nc, ctx, stage)
        T = s.ps("T", [P, 4, 512])
        turned, hi_ready, lo_ready = s.sem("turned"), s.sem("hi_ready"), s.sem("lo_ready")
        with nc.Block() as block:

            @block.tensor
            def _(pe):
                for t in range(TILES):
                    if t >= 4:
                        pe.wait_ge(lo_ready, t - 3)
                    for k in range(KC):
                        last = pe.transpose(T[:, t % 4, k * P:(k + 1) * P], x[:, t, k * P:(k + 1) * P], ident[:])
                    last.then_inc(turned, 1)

            @block.scalar
            def _(act):
                for t in range(TILES):
                    act.wait_ge(turned, t + 1)
                    split_hi(nc, hi[:, :, t * P:(t + 1) * P], T[:, t % 4, :].rearrange("p (k c) -> p k c", k=KC)).then_inc(hi_ready, 1)

            @block.vector
            def _(dve):
                for t in range(TILES):
                    dve.wait_ge(hi_ready, t + 1)
                    split_lo(nc, lo[:, :, t * P:(t + 1) * P], T[:, t % 4, :].rearrange("p (k c) -> p k c", k=KC),
                             hi[:, :, t * P:(t + 1) * P]).then_inc(lo_ready, 1)


def relu_mlp_stage(nc, x_sb, c, a_hi, a_lo, W1, b1, W2, b2, raw1, raw2, w1_loaded, w2_loaded):
    FF = W1.shape[1]
    N = FF // HID
    UNITS = HALVES * HC
    with ExitStack() as ctx:
        s = Space(nc, ctx, "ml")
        w1_hi, w1_lo = s.sb("w1_hi", [P, KC, HID], F32R), s.sb("w1_lo", [P, KC, HID], F32R)
        w2_hi, w2_lo = s.sb("w2_hi", [P, HC, D], F32R), s.sb("w2_lo", [P, HC, D], F32R)
        b1_sb, b1_now, b2_sb = s.sb("b1", [P, N * HC]), s.sb("b1_now", [P, HC]), s.sb("b2", [P, D])
        h32 = s.sb("h32", [P, 2, HALF])
        h_hi, h_lo = s.sb("h_hi", [P, HC, TOKENS], F32R), s.sb("h_lo", [P, HC, TOKENS], F32R)
        H, O = s.ps("H", [P, 2, 512]), s.ps("O", [P, 4, 512])
        (small_loaded, w1_hi_ready, w1_lo_ready, w2_hi_ready, w2_lo_ready, b1_ready, h_produced, h32_ready,
         h_hi_ready, h_lo_ready, o_produced, added, biased) = (s.sem(n) for n in (
             "small_loaded", "w1_hi_ready", "w1_lo_ready", "w2_hi_ready", "w2_lo_ready", "b1_ready",
             "h_produced", "h32_ready", "h_hi_ready", "h_lo_ready", "o_produced", "added", "biased"))

        def hidden(buf, u):
            return buf[:, u % HC, (u // HC) * HALF:(u // HC + 1) * HALF]

        with nc.Block() as block:

            @block.sync
            def _(sp):
                with nc.allow_non_contiguous_dma(reason="2048 values, once"):
                    sp.dma_start(b1_sb[:], b1.rearrange("(c p) -> p c", p=P)).then_inc(small_loaded, 16)
                sp.dma_start(b2_sb[:], rows_of(b2, P)).then_inc(small_loaded, 16)
                with sp.Fori(1, N) as n:
                    sp.wait_ge(w1_lo_ready, n)
                    sp.dma_start(raw1[:], w1_slices(W1)[n]).then_inc(w1_loaded, 16)
                    sp.wait_ge(w2_lo_ready, n)
                    sp.dma_start(raw2[:], w2_slices(W2)[n]).then_inc(w2_loaded, 16)

            @block.gpsimd
            def _(pool):
                pool.wait_ge(small_loaded, 32)
                for t in range(TILES):
                    nc.gpsimd.tensor_tensor(x_sb[:, t, :], x_sb[:, t, :], c[:, t, :], ALU.add).then_inc(biased, 1)
                    pool.wait_ge(biased, 2 * t + 1)
                    nc.gpsimd.tensor_tensor(x_sb[:, t, :], x_sb[:, t, :], b2_sb[:], ALU.add).then_inc(biased, 1)

            @block.scalar
            def _(act):
                def split1(n):
                    act.wait_ge(w1_loaded, 16 * n + 16)
                    wait_after(act, h_produced, UNITS * n)
                    split_hi(nc, w1_hi[:], raw1[:]).then_inc(w1_hi_ready, 1)

                def mlp_slice(n, more):
                    act.wait_ge(w2_loaded, 16 * n + 16)
                    wait_after(act, o_produced, TILES * n)
                    split_hi(nc, w2_hi[:], raw2[:]).then_inc(w2_hi_ready, 1)
                    act.wait_ge(b1_ready, n + 1)
                    for u in range(UNITS):
                        act.wait_ge(h_produced, UNITS * n + u + 1)
                        wait_after(act, h_lo_ready, UNITS * n + max(u - 1, 0))
                        nc.scalar.activation(h32[:, u % 2, :], H[:, u % 2, :], ACT.Relu, bias=b1_now[:, u % HC:u % HC + 1]).then_inc(h32_ready, 1)
                        act.wait_ge(h32_ready, UNITS * n + u + 1)
                        split_hi(nc, hidden(h_hi, u), h32[:, u % 2, :]).then_inc(h_hi_ready, 1)
                    if more:
                        split1(n + 1)

                split1(0)
                mlp_slice(0, True)
                with act.Fori(1, N - 1) as n:
                    mlp_slice(n, True)
                mlp_slice(N - 1, False)

            @block.vector
            def _(dve):
                def split1(n):
                    dve.wait_ge(w1_hi_ready, n + 1)
                    split_lo(nc, w1_lo[:], raw1[:], w1_hi[:]).then_inc(w1_lo_ready, 1)

                def mlp_slice(n, more):
                    wait_after(dve, h32_ready, UNITS * n)
                    nc.vector.tensor_copy(b1_now[:], b1_sb[:, bass.ds(n * HC, HC)]).then_inc(b1_ready, 1)
                    dve.wait_ge(w2_hi_ready, n + 1)
                    split_lo(nc, w2_lo[:], raw2[:], w2_hi[:]).then_inc(w2_lo_ready, 1)
                    for u in range(UNITS):
                        dve.wait_ge(h_hi_ready, UNITS * n + u + 1)
                        split_lo(nc, hidden(h_lo, u), h32[:, u % 2, :], hidden(h_hi, u)).then_inc(h_lo_ready, 1)
                    if more:
                        split1(n + 1)
                    for t in range(TILES):
                        if isinstance(n, int) and n == 0:
                            dve.wait_ge(biased, 2 * t + 2)
                        dve.wait_ge(o_produced, TILES * n + t + 1)
                        nc.vector.tensor_tensor(x_sb[:, t, :], O[:, t % 4, :], x_sb[:, t, :], ALU.add).then_inc(added, 1)

                split1(0)
                dve.wait_ge(small_loaded, 32)
                mlp_slice(0, True)
                with dve.Fori(1, N - 1) as n:
                    mlp_slice(n, True)
                mlp_slice(N - 1, False)

            @block.tensor
            def _(pe):
                def mlp_slice(n):
                    pe.wait_ge(w1_lo_ready, n + 1)
                    for u in range(UNITS):
                        th, m = u // HC, u % HC
                        wait_after(pe, h32_ready, UNITS * n + max(u - 1, 0))
                        for k in range(KC):
                            last = product(pe, H[:, u % 2, :], w1_hi[:, k, m * P:(m + 1) * P], w1_lo[:, k, m * P:(m + 1) * P],
                                           a_hi[:, k, th * HALF:(th + 1) * HALF], a_lo[:, k, th * HALF:(th + 1) * HALF],
                                           k == 0, k == KC - 1)
                        last.then_inc(h_produced, 1)
                    pe.wait_ge(w2_lo_ready, n + 1)
                    for t in range(TILES):
                        pe.wait_ge(h_lo_ready, UNITS * n + (t // 4) * HC + HC)
                        wait_after(pe, added, TILES * n + max(t - 3, 0))
                        for m in range(HC):
                            last = product(pe, O[:, t % 4, :], h_hi[:, m, t * P:(t + 1) * P], h_lo[:, m, t * P:(t + 1) * P],
                                           w2_hi[:, m, :], w2_lo[:, m, :], m == 0, m == HC - 1)
                        last.then_inc(o_produced, 1)

                mlp_slice(0)
                with pe.Fori(1, N) as n:
                    mlp_slice(n)


def w1_slices(W1):
    return W1.rearrange("(k p) (n h) -> n p k h", p=P, h=HID)


def w2_slices(W2):
    return W2.rearrange("(n c p) d -> n p c d", p=P, c=HC)


def differential_layer(nc, x_sb, ident, Wq, Wk, Wv, lq1, lq2, lk1, lk2, Wo, bo, g1, be1, g2, be2, W1, b1, W2, b2):
    with ExitStack() as ctx:
        s = Space(nc, ctx, "diff")
        c = s.sb("c", [P, TILES, D])
        norm_stage(nc, "n6", x_sb, c, ident)
        with ExitStack() as mid:
            i = Space(nc, mid, "diffq")
            q, k, v = i.sb("q", [P, TILES, D]), i.sb("k", [P, TILES, D]), i.sb("v", [P, TILES, D])
            with ExitStack() as inner:
                a = Space(nc, inner, "diffa")
                a_hi, a_lo = a.sb("a_hi", [P, KC, TOKENS], F32R), a.sb("a_lo", [P, KC, TOKENS], F32R)
                with ExitStack() as inner2:
                    b = Space(nc, inner2, "diffx")
                    xn, y = b.sb("xn", [P, TILES, D]), b.sb("y", [P, TILES, D])
                    norm_stage(nc, "n4", c, xn, ident, gamma=g1, beta=be1, y=y, hi=a_hi, lo=a_lo)
                project_stage(nc, "pj4", a_hi, a_lo, [(TOKENWISE, Wq, None, QD**-0.5, q), (TOKENWISE, Wk, None, 1.0, k),
                                                     (TOKENWISE, Wv, None, 1.0, v)])
            differential_stage(nc, q, k, v, q, lq1, lk1, lq2, lk2, ident)
            with ExitStack() as inner:
                a = Space(nc, inner, "diffo")
                o_hi, o_lo = a.sb("o_hi", [P, KC, TOKENS], F32R), a.sb("o_lo", [P, KC, TOKENS], F32R)
                turn_stage(nc, "tu0", q, o_hi, o_lo, ident)
                project_stage(nc, "pj5", o_hi, o_lo, [(RESIDUAL, Wo, bo, 1.0, c)])
        a_hi, a_lo = s.sb("a_hi", [P, KC, TOKENS], F32R), s.sb("a_lo", [P, KC, TOKENS], F32R)
        raw1, raw2 = s.sb("raw1", [P, KC, HID]), s.sb("raw2", [P, HC, D])
        w1_loaded, w2_loaded = s.sem("w1_loaded"), s.sem("w2_loaded")

        def load_first(sp):
            sp.dma_start(raw1[:], w1_slices(W1)[0]).then_inc(w1_loaded, 16)
            sp.dma_start(raw2[:], w2_slices(W2)[0]).then_inc(w2_loaded, 16)

        with ExitStack() as inner:
            i = Space(nc, inner, "diffy")
            xn, y = i.sb("xn", [P, TILES, D]), i.sb("y", [P, TILES, D])
            norm_stage(nc, "n5", c, xn, ident, gamma=g2, beta=be2, y=y, hi=a_hi, lo=a_lo, prefetch=load_first)
        relu_mlp_stage(nc, x_sb, c, a_hi, a_lo, W1, b1, W2, b2, raw1, raw2, w1_loaded, w2_loaded)


LEAST = 1e-5


def spread_rows(nc, pe, diag_ready, ones, diag, out):
    pe.wait_ge(*diag_ready)
    return pe.matmul(out, ones, diag, start=True, stop=True)


CH = 2048


def load_weight(sp, raw, wT, loaded):
    src = wT.rearrange("(k p) n -> p k n", p=P)
    n = src.shape[2]
    dst = raw.rearrange("p (k n) -> p k n", n=n)
    step = CH // n
    for c, sem in enumerate(loaded):
        sp.dma_start(dst[:, c * step:(c + 1) * step, :], src[:, c * step:(c + 1) * step, :]).then_inc(sem, 16)


def quantise_stage(nc, xn, ident, raw1, raw2, w1_loaded, w2_loaded, w1q, xqT, dq1_row, mean_w2, scale_w2):
    loaded = w1_loaded + w2_loaded
    NCH = len(loaded)
    COUNT = P * (NCH // 2) * CH
    with ExitStack() as ctx:
        s = Space(nc, ctx, "qs")
        absum, mean, scale = s.sb("absum", [P, 2]), s.sb("mean", [P, 2]), s.sb("scale", [P, 2])
        ones = s.sb("ones", [P, P])
        junk = s.sb("junk", [P, 2, CH])
        part = s.sb("part", [P, NCH])
        amax, ax, sx, dq = (s.sb(n, [P, TILES]) for n in ("amax", "ax", "sx", "dq"))
        xs = s.sb("xs", [P, 2, D])
        xq = s.sb("xq", [P, 2, D], BF16)
        ident16 = s.sb("ident16", [P, P], BF16)
        diag = s.sb("diag", [P, TILES, P])
        M = s.ps("M", [P, 512])
        R = s.ps("R", [P, 2, 512])
        X = s.ps("X", [P, 2, 1024], BF16)
        (ones_ready, summed_abs, absum_ready, mean_made, scale_ready, shifted, chain, amax_done, xs_ready, xq_ready,
         x_turned, x_kept, diag_ready, row_made) = (s.sem(n) for n in (
             "ones_ready", "summed_abs", "absum_ready", "mean_made", "scale_ready", "shifted", "chain", "amax_done",
             "xs_ready", "xq_ready", "x_turned", "x_kept", "diag_ready", "row_made"))
        w1q_flat = w1q[:].rearrange("p k n -> p (k n)")

        def piece(c):
            raw, i = (raw1, c) if c < NCH // 2 else (raw2, c - NCH // 2)
            return raw[:, i * CH:(i + 1) * CH]

        with nc.Block() as block:

            @block.gpsimd
            def _(pool):
                nc.gpsimd.memset(ones[:], 1.0).then_inc(ones_ready, 1)

            @block.scalar
            def _(act):
                for c in range(NCH):
                    act.wait_ge(loaded[c], 16)
                    if c >= 2:
                        act.wait_ge(summed_abs, c - 1)
                    nc.scalar.activation(junk[:, c % 2, :], piece(c), ACT.Abs, accum_out=part[:, c:c + 1]).then_inc(summed_abs, 1)
                for t in range(TILES):
                    act.wait_ge(x_turned, t + 1)
                    nc.scalar.activation(xqT[:, :, t * P:(t + 1) * P], X[:, t % 2, 0:D].rearrange("p (k c) -> p k c", k=KC), ACT.Copy)\
                        .then_inc(x_kept, 1)
                for c in range(NCH // 2):
                    act.wait_ge(shifted, c + 1)
                    nc.scalar.activation(w1q_flat[:, c * CH:(c + 1) * CH], piece(c), ACT.Copy, bias=-ROUND)
                for h in range(HALVES):
                    act.wait_ge(row_made, h + 1)
                    nc.scalar.activation(dq1_row[:, h * HALF:(h + 1) * HALF], R[:, h, :], ACT.Copy)

            @block.vector
            def _(dve):
                step = [0]

                def link(ins):
                    step[0] += 1
                    ins.then_inc(chain, 1)
                    dve.wait_ge(chain, step[0])

                link(nc.vector.tensor_copy(ident16[:], ident[:]))
                for t in range(TILES):
                    last = nc.vector.tensor_reduce(amax[:, t:t + 1], xn[:, t, :], AX.X, ALU.max, apply_absolute_value=True)
                link(last)
                link(nc.vector.tensor_scalar(ax[:], amax[:], LEAST, None, ALU.max))
                link(nc.vector.reciprocal(sx[:], ax[:]))
                link(nc.vector.tensor_scalar(sx[:], sx[:], 127.0, None, ALU.mult))
                for t in range(TILES):
                    if t >= 2:
                        dve.wait_ge(x_turned, t - 1)
                    link(nc.vector.tensor_scalar(xs[:, t % 2, :], xn[:, t, :], sx[:, t:t + 1], ROUND, ALU.mult, ALU.add))
                    link(nc.vector.tensor_scalar(xs[:, t % 2, :], xs[:, t % 2, :], ROUND + 127.0, ROUND - 128.0, ALU.min, ALU.max))
                    nc.vector.tensor_scalar(xq[:, t % 2, :], xs[:, t % 2, :], -ROUND, None, ALU.add).then_inc(xq_ready, 1)
                dve.wait_ge(summed_abs, NCH)
                nc.vector.reduce_sum(absum[:], part[:].rearrange("p (w c) -> p w c", w=2), AX.X).then_inc(absum_ready, 1)
                dve.wait_ge(mean_made, 1)
                link(nc.vector.tensor_scalar(mean[:], M[:, 0:2], 1.0 / COUNT, LEAST, ALU.mult, ALU.max))
                link(nc.vector.reciprocal(scale[:], mean[:]))
                nc.vector.tensor_copy(mean_w2[:], mean[:, 1:2])
                nc.vector.tensor_copy(scale_w2[:], scale[:, 1:2])
                link(nc.vector.tensor_scalar(dq[:], ax[:], mean[:, 0:1], 1.0 / 127.0, ALU.mult, ALU.mult))
                for t in range(TILES):
                    nc.vector.tensor_scalar(diag[:, t, :], ident[:], dq[:, t:t + 1], None, ALU.mult).then_inc(diag_ready, 1)
                for c in range(NCH // 2):
                    link(nc.vector.tensor_scalar(piece(c), piece(c), scale[:, 0:1], ROUND, ALU.mult, ALU.add))
                    nc.vector.tensor_scalar(piece(c), piece(c), ROUND + 1.0, ROUND - 1.0, ALU.min, ALU.max).then_inc(shifted, 1)

            @block.tensor
            def _(pe):
                for t in range(TILES):
                    pe.wait_ge(xq_ready, t + 1)
                    if t >= 2:
                        pe.wait_ge(x_kept, t - 1)
                    for k in range(KC):
                        last = pe.transpose(X[:, t % 2, k * P:(k + 1) * P], xq[:, t % 2, k * P:(k + 1) * P], ident16[:])
                    last.then_inc(x_turned, 1)
                pe.wait_ge(ones_ready, 1)
                pe.wait_ge(absum_ready, 1)
                pe.matmul(M[:, 0:2], ones[:], absum[:], start=True, stop=True).then_inc(mean_made, 1)
                for t in range(TILES):
                    last = spread_rows(nc, pe, (diag_ready, t + 1), ones[:], diag[:, t, :], R[:, t // 4, (t % 4) * P:(t % 4 + 1) * P])
                    if t % 4 == 3:
                        last.then_inc(row_made, 1)


def hidden_stage(nc, xqT, w1q, dq1_row, conv_w, conv_b, hs, mx, raw2, scale_w2, w2q):
    FCH = hs.shape[1]
    with ExitStack() as ctx:
        s = Space(nc, ctx, "hd")
        cw, cb = s.sb("cw", [P, FCH, 3]), s.sb("cb", [P, FCH])
        h = s.sb("h", [P, 2, TOKENS])
        y = s.sb("y", [P, 2, TOKENS])
        size = s.sb("size", [P, 2, TOKENS])
        H = s.ps("H", [P, 2, 2, 512])
        (conv_loaded, produced, h_ready, y_ready, left_done, right_done, hs_ready, mx_done, size_ready, w2_steps) = (s.sem(n) for n in (
            "conv_loaded", "produced", "h_ready", "y_ready", "left_done", "right_done", "hs_ready", "mx_done", "size_ready", "w2_steps"))

        def by_batch(ap):
            return ap.rearrange("p (b s) -> p b s", s=SEQ)

        with nc.Block() as block:

            @block.sync
            def _(sp):
                with nc.allow_non_contiguous_dma(reason="four values for each hidden unit, once"):
                    sp.dma_start(cw[:], conv_w.rearrange("(c p) a w -> p c (a w)", p=P)).then_inc(conv_loaded, 16)
                    sp.dma_start(cb[:], conv_b.rearrange("(c p) -> p c", p=P)).then_inc(conv_loaded, 16)

            @block.gpsimd
            def _(pool):
                w2q_flat = w2q[:].rearrange("p k n -> p (k n)")
                for c in range(w2q_flat.shape[1] // CH):
                    piece = raw2[:, c * CH:(c + 1) * CH]
                    nc.gpsimd.tensor_scalar(piece, piece, scale_w2[:, 0:1], ROUND, ALU.mult, ALU.add).then_inc(w2_steps, 1)
                    pool.wait_ge(w2_steps, 2 * c + 1)
                    nc.gpsimd.tensor_scalar(piece, piece, ROUND + 1.0, ROUND - 1.0, ALU.min, ALU.max).then_inc(w2_steps, 1)
                    pool.wait_ge(w2_steps, 2 * c + 2)
                    nc.gpsimd.tensor_scalar(w2q_flat[:, c * CH:(c + 1) * CH], piece, -ROUND, None, ALU.add)

            @block.tensor
            def _(pe):
                for c in range(FCH):
                    if c >= 2:
                        pe.wait_ge(h_ready, c - 1)
                    for th in range(HALVES):
                        for k in range(KC):
                            last = pe.matmul(H[:, c % 2, th, :], w1q[:, k, c * P:(c + 1) * P], xqT[:, k, th * HALF:(th + 1) * HALF],
                                             start=(k == 0), stop=(k == KC - 1))
                    last.then_inc(produced, 1)

            @block.vector
            def _(dve):
                def scale(c):
                    dve.wait_ge(produced, c + 1)
                    if c >= 2:
                        dve.wait_ge(right_done, c - 1)
                    nc.vector.tensor_tensor(h[:, c % 2, :], H[:, c % 2].rearrange("p h n -> p (h n)"), dq1_row[:], ALU.mult).then_inc(h_ready, 1)

                def largest(c):
                    dve.wait_ge(size_ready, c + 1)
                    dve.wait_ge(mx_done, c + 1)
                    nc.vector.tensor_tensor(mx[:], size[:, c % 2, :], mx[:], ALU.max).then_inc(mx_done, 1)

                nc.vector.memset(mx[:], 0.0).then_inc(mx_done, 1)
                dve.wait_ge(conv_loaded, 32)
                scale(0)
                for c in range(FCH):
                    if c + 1 < FCH:
                        scale(c + 1)
                    dve.wait_ge(y_ready, c + 1)
                    yb, hb = by_batch(y[:, c % 2, :]), by_batch(h[:, c % 2, :])
                    nc.vector.scalar_tensor_tensor(out=yb[:, :, 1:SEQ], in0=hb[:, :, 0:SEQ - 1], scalar=cw[:, c, 0:1], in1=yb[:, :, 1:SEQ],
                                                   op0=ALU.mult, op1=ALU.add).then_inc(left_done, 1)
                    dve.wait_ge(left_done, c + 1)
                    nc.vector.scalar_tensor_tensor(out=yb[:, :, 0:SEQ - 1], in0=hb[:, :, 1:SEQ], scalar=cw[:, c, 2:3], in1=yb[:, :, 0:SEQ - 1],
                                                   op0=ALU.mult, op1=ALU.add).then_inc(right_done, 1)
                    if c:
                        largest(c - 1)
                largest(FCH - 1)

            @block.scalar
            def _(act):
                act.wait_ge(conv_loaded, 32)

                def middle(c):
                    act.wait_ge(h_ready, c + 1)
                    if c >= 2:
                        act.wait_ge(hs_ready, c - 1)
                    nc.scalar.activation(y[:, c % 2, :], h[:, c % 2, :], ACT.Identity, bias=cb[:, c:c + 1], scale=cw[:, c, 1:2]).then_inc(y_ready, 1)

                middle(0)
                for c in range(FCH):
                    if c + 1 < FCH:
                        middle(c + 1)
                    act.wait_ge(right_done, c + 1)
                    nc.scalar.activation(hs[:, c, :], y[:, c % 2, :], ACT.Silu).then_inc(hs_ready, 1)
                    act.wait_ge(hs_ready, c + 1)
                    if c >= 2:
                        act.wait_ge(mx_done, c)
                    nc.scalar.activation(size[:, c % 2, :], hs[:, c, :], ACT.Abs).then_inc(size_ready, 1)


def token_scale_stage(nc, mx, ident, mean_w2, s2_row, dq2):
    with ExitStack() as ctx:
        s = Space(nc, ctx, "ts")
        ones, diag = s.sb("ones", [P, P]), s.sb("diag", [P, TILES, P])
        amax, ax, sx = (s.sb(n, [P, TILES]) for n in ("amax", "ax", "sx"))
        T, R = s.ps("T", [P, 2, 512]), s.ps("R", [P, 2, 512])
        turned, chain, ones_ready, diag_ready, row_made = (s.sem(n) for n in ("turned", "chain", "ones_ready", "diag_ready", "row_made"))
        with nc.Block() as block:

            @block.gpsimd
            def _(pool):
                nc.gpsimd.memset(ones[:], 1.0).then_inc(ones_ready, 1)

            @block.tensor
            def _(pe):
                for t in range(TILES):
                    last = pe.transpose(T[:, t // 4, (t % 4) * P:(t % 4 + 1) * P], mx[:, t * P:(t + 1) * P], ident[:])
                last.then_inc(turned, 1)
                pe.wait_ge(ones_ready, 1)
                for t in range(TILES):
                    last = spread_rows(nc, pe, (diag_ready, t + 1), ones[:], diag[:, t, :], R[:, t // 4, (t % 4) * P:(t % 4 + 1) * P])
                    if t % 4 == 3:
                        last.then_inc(row_made, 1)

            @block.vector
            def _(dve):
                step = [0]

                def link(ins):
                    step[0] += 1
                    ins.then_inc(chain, 1)
                    dve.wait_ge(chain, step[0])

                dve.wait_ge(turned, 1)
                link(nc.vector.tensor_reduce(amax[:], T[:].rearrange("p h (t c) -> p (h t) c", c=P), AX.X, ALU.max))
                link(nc.vector.tensor_scalar(ax[:], amax[:], LEAST, None, ALU.max))
                link(nc.vector.reciprocal(sx[:], ax[:]))
                link(nc.vector.tensor_scalar(sx[:], sx[:], 127.0, None, ALU.mult))
                for t in range(TILES):
                    nc.vector.tensor_scalar(diag[:, t, :], ident[:], sx[:, t:t + 1], None, ALU.mult).then_inc(diag_ready, 1)
                nc.vector.tensor_scalar(dq2[:], ax[:], mean_w2[:, 0:1], 1.0 / 127.0, ALU.mult, ALU.mult)
                for h in range(HALVES):
                    dve.wait_ge(row_made, h + 1)
                    nc.vector.tensor_copy(s2_row[:, h * HALF:(h + 1) * HALF], R[:, h, :])


def ternary_out_stage(nc, x_sb, hs, s2_row, w2q, dq2):
    FCH = hs.shape[1]
    POOL_CHUNKS = [c for c in range(FCH) if c % 5 in (2, 4)]
    DVE_CHUNKS = [c for c in range(FCH) if c not in POOL_CHUNKS]
    with ExitStack() as ctx:
        s = Space(nc, ctx, "to")
        hq = s.sb("hq", [P, 3, TOKENS], BF16)
        O = s.ps("O", [P, TILES, 512])
        scaled_pool, scaled_dve, rounded, clipped, raised, hq_act, hq_dve, used = (s.sem(n) for n in (
            "scaled_pool", "scaled_dve", "rounded", "clipped", "raised", "hq_act", "hq_dve", "used"))
        with nc.Block() as block:

            @block.gpsimd
            def _(pool):
                for c in POOL_CHUNKS:
                    nc.gpsimd.tensor_tensor(hs[:, c, :], hs[:, c, :], s2_row[:], ALU.mult).then_inc(scaled_pool, 1)

            @block.vector
            def _(dve):
                def scale(c):
                    nc.vector.tensor_tensor(hs[:, c, :], hs[:, c, :], s2_row[:], ALU.mult).then_inc(scaled_dve, 1)

                scale(DVE_CHUNKS[0])
                for c in range(FCH):
                    if c in POOL_CHUNKS:
                        i = POOL_CHUNKS.index(c)
                        dve.wait_ge(scaled_pool, i + 1)
                        nc.vector.tensor_scalar(hs[:, c, :], hs[:, c, :], -128.0, ROUND, ALU.max, ALU.add).then_inc(raised, 1)
                        dve.wait_ge(raised, i + 1)
                        if c >= 3:
                            dve.wait_ge(used, TILES * (c - 2))
                        nc.vector.tensor_scalar(hq[:, c % 3, :], hs[:, c, :], ROUND + 127.0, -ROUND, ALU.min, ALU.add).then_inc(hq_dve, 1)
                        continue
                    i = DVE_CHUNKS.index(c)
                    if i + 1 < len(DVE_CHUNKS):
                        scale(DVE_CHUNKS[i + 1])
                    dve.wait_ge(rounded, i + 1)
                    nc.vector.tensor_scalar(hs[:, c, :], hs[:, c, :], ROUND + 127.0, ROUND - 128.0, ALU.min, ALU.max).then_inc(clipped, 1)
                for t in range(TILES):
                    dve.wait_ge(used, FCH * TILES - TILES + t + 1)
                    nc.vector.scalar_tensor_tensor(out=x_sb[:, t, :], in0=O[:, t, :], scalar=dq2[:, t:t + 1], in1=x_sb[:, t, :],
                                                   op0=ALU.mult, op1=ALU.add)

            @block.scalar
            def _(act):
                def rounding(i):
                    act.wait_ge(scaled_dve, i + 1)
                    c = DVE_CHUNKS[i]
                    nc.scalar.activation(hs[:, c, :], hs[:, c, :], ACT.Copy, bias=ROUND).then_inc(rounded, 1)

                rounding(0)
                for i, c in enumerate(DVE_CHUNKS):
                    if i + 1 < len(DVE_CHUNKS):
                        rounding(i + 1)
                    act.wait_ge(clipped, i + 1)
                    if c >= 3:
                        act.wait_ge(used, TILES * (c - 2))
                    nc.scalar.activation(hq[:, c % 3, :], hs[:, c, :], ACT.Copy, bias=-ROUND).then_inc(hq_act, 1)

            @block.tensor
            def _(pe):
                for c in range(FCH):
                    if c in POOL_CHUNKS:
                        pe.wait_ge(hq_dve, POOL_CHUNKS.index(c) + 1)
                    else:
                        pe.wait_ge(hq_act, DVE_CHUNKS.index(c) + 1)
                    for t in range(TILES):
                        pe.matmul(O[:, t, :], hq[:, c % 3, t * P:(t + 1) * P], w2q[:, c, :], start=(c == 0), stop=(c == FCH - 1)).then_inc(used, 1)


def ternary_layer(nc, x_sb, ident, w1T, conv_w, conv_b, w2T):
    FCH = w1T.shape[1] // P
    with ExitStack() as ctx:
        s = Space(nc, ctx, "tern")
        w1q, w2q = s.sb("w1q", [P, KC, w1T.shape[1]], BF16), s.sb("w2q", [P, FCH, D], BF16)
        mean_w2, scale_w2, dq2 = s.sb("mean_w2", [P, 1]), s.sb("scale_w2", [P, 1]), s.sb("dq2", [P, TILES])
        xqT = s.sb("xqT", [P, KC, TOKENS], BF16)
        row, mx = s.sb("row", [P, TOKENS]), s.sb("mx", [P, TOKENS])
        raw2 = s.sb("raw2", [P, FCH * D])
        w1_loaded = [s.sem(f"w1_loaded{c}") for c in range(FCH * D // CH)]
        w2_loaded = [s.sem(f"w2_loaded{c}") for c in range(FCH * D // CH)]
        with ExitStack() as inner:
            i = Space(nc, inner, "ternx")
            raw1, xn = i.sb("raw1", [P, FCH * D]), i.sb("xn", [P, TILES, D])

            def load_weights(sp):
                load_weight(sp, raw1[:], w1T, w1_loaded)
                load_weight(sp, raw2[:], w2T, w2_loaded)

            norm_stage(nc, "n7", x_sb, xn, ident, prefetch=load_weights)
            quantise_stage(nc, xn, ident, raw1, raw2, w1_loaded, w2_loaded, w1q, xqT, row, mean_w2, scale_w2)
        hs = s.sb("hs", [P, FCH, TOKENS])
        hidden_stage(nc, xqT, w1q, row, conv_w, conv_b, hs, mx, raw2, scale_w2, w2q)
        token_scale_stage(nc, mx, ident, mean_w2, row, dq2)
        ternary_out_stage(nc, x_sb, hs, row, w2q, dq2)


def start_stage(nc, x_sb, ident, x):
    with ExitStack() as ctx:
        s = Space(nc, ctx, "start")
        x_loaded, ident_ready = s.sem("x_loaded"), s.sem("ident_ready")
        with nc.Block() as block:

            @block.sync
            def _(sp):
                sp.dma_start(x_sb[:], x.rearrange("(t a) s d -> (a s) t d", a=2)).then_inc(x_loaded, 16)
                sp.wait_ge(x_loaded, 16)

            @block.gpsimd
            def _(pool):
                nc.gpsimd.memset(ident[:], 0.0).then_inc(ident_ready, 1)
                pool.wait_ge(ident_ready, 1)
                nc.gpsimd.affine_select(out=ident[:], in_=ident[:], compare_op=ALU.not_equal, fill=1.0, base=0,
                                        pattern=[[-1, P]], channel_multiplier=1).then_inc(ident_ready, 1)


def end_stage(nc, x_sb, out):
    with ExitStack() as ctx:
        stored = Space(nc, ctx, "end").sem("stored")
        with nc.Block() as block:

            @block.sync
            def _(sp):
                sp.dma_start(out.rearrange("(t a) s d -> (a s) t d", a=2), x_sb[:]).then_inc(stored, 16)
                sp.wait_ge(stored, 16)


def clear_stage(nc):
    free = nc.free_semaphores
    numbers = range(min(free), max(free) + 1)
    assert len(free) == len(numbers)
    with nc.Block() as block:

        @block.gpsimd
        def _(pool):
            pool.sem_clear(numbers)


def perceiver(nc, a, out):
    with ExitStack() as ctx:
        s = Space(nc, ctx, "main")
        x_sb = s.sb("x", [P, TILES, D])
        ident = s.sb("ident", [P, P])

        def of(layer, *names):
            return [a[f"{layer}_{n}"] for n in names]

        start_stage(nc, x_sb, ident, a["x"])
        bidaf_layer(nc, x_sb, ident, a["ctx"], a["ctx_cols"], *of("L0_xattn", "w_sim", "b_sim", "W_qv", "b_qv"))
        causal_layer(nc, x_sb, ident, *of("L0_attn", "Wq", "bq", "Wk", "bk", "Wv", "bv", "Wo", "bo"))
        experts_layer(nc, x_sb, ident, *of("L0_ffn", "router_w", "router_b"), of("L0_ffn", "routed_w1", "routed_w3", "routed_w2"),
                      of("L0_ffn", "shared_w1", "shared_w3", "shared_w2"))
        clear_stage(nc)
        cross_layer(nc, x_sb, ident, a["ctx_cols"], a["mask"], *of("L1_xattn", "Wq", "bq", "Wk", "bk", "Wv", "bv", "Wo", "bo"))
        clear_stage(nc)
        differential_layer(nc, x_sb, ident, *of("L1_attn", "Wq", "Wk", "Wv", "lq1", "lq2", "lk1", "lk2", "Wo", "bo",
                                                "ln1_g", "ln1_b", "ln2_g", "ln2_b", "W1", "b1", "W2", "b2"))
        clear_stage(nc)
        ternary_layer(nc, x_sb, ident, *of("L1_ffn", "w1", "conv_w", "conv_b", "w2"))
        end_stage(nc, x_sb, out)




def kernel(**inputs):
    import numpy as np
    import concourse.bacc as bacc
    from concourse.bass_utils import run_bass_kernel_spmd as run

    arrays = {}
    for name in inputs:
        if name[:3] in ("L0_", "L1_") or name == "x":
            arrays[name] = np.asarray(inputs[name])
    arrays["ctx"] = np.asarray(inputs["ctx_1024"])
    arrays["ctx_cols"] = arrays["ctx"].transpose(0, 2, 1)
    arrays["mask"] = np.asarray(inputs["mask_Bx1xSxS2_bk1"])
    for name in ("L1_attn_Wv", "L1_attn_Wo", "L1_attn_W1", "L1_attn_W2", "L1_ffn_w1", "L1_ffn_w2"):
        arrays[name] = arrays[name].T
    for name in ("L1_attn_Wq", "L1_attn_Wk"):
        arrays[name] = arrays[name].T.reshape(D, 16, 16, 2).transpose(0, 2, 3, 1).reshape(D, D)

    nc = bacc.Bacc("TRN2", target_bir_lowering=False, num_devices=1)
    feed, aps = {}, {}
    for name, array in arrays.items():
        array = np.ascontiguousarray(array)
        feed[f"in_{name}"] = array
        aps[name] = nc.dram_tensor(f"in_{name}", array.shape, mybir.dt.from_np(array.dtype), kind="ExternalInput").ap()
    out = nc.dram_tensor("out_x", (BATCH, SEQ, D), F32, kind="ExternalOutput").ap()
    perceiver(nc, aps, out)
    return run(nc, [feed], core_ids=[0]).results[0]["out_x"]
```
